# Optimizing a Trainium2 kernel written in Bass

```python
import numpy as np
import jax
import jax.numpy as jnp

def _softmax(x, axis=-1):
    return jax.nn.softmax(x, axis=axis)

def _gelu(x):
    return jax.nn.gelu(x, approximate=True)

def _silu(x):
    return jax.nn.silu(x)

def _sigmoid(x):
    return jax.nn.sigmoid(x)

def _layernorm(x, axis=-1, eps=1e-05):
    m = jnp.mean(x, axis=axis, keepdims=True)
    v = jnp.var(x, axis=axis, keepdims=True)
    return (x - m) / jnp.sqrt(v + eps)

def _scatter_add(tgt, idx, src, axis=0):
    return tgt.at[idx].add(src)

def _segment_sum(src, seg, n):
    return jax.ops.segment_sum(src, seg, n)
kernel_name = 'mk_perceiver_d1_seqx_r4_138c11'

def setup_inputs(seed: int=0):
    np.random.seed(seed)
    _w = jnp.asarray

    def _rec_inputs():
        import jax
        import jax.numpy as jnp
        _rk = jax.random.key(seed)
        x = -0.0002737 + 0.9994 * jax.random.normal(jax.random.fold_in(_rk, 1), (32, 64, 256), jnp.float32)
        _lenS = 64 - jax.random.randint(jax.random.fold_in(_rk, 7), (32,), 0, max(1, 64 // 4) + 1, jnp.int32)
        _lenS2 = 1601 - jax.random.randint(jax.random.fold_in(_rk, 8), (32,), 0, max(1, 1601 // 4) + 1, jnp.int32)
        _ctx_1024P = jax.random.normal(jax.random.fold_in(_rk, 11), (32, 16, 256), jnp.float32)
        _ctx_1024c = jax.random.dirichlet(jax.random.fold_in(_rk, 511), 0.3 * jnp.ones((16,), jnp.float32), (32, 1601))
        _ctx_1024t = jnp.einsum('bsk,bkd->bsd', _ctx_1024c, _ctx_1024P)
        _ctx_1024t = _ctx_1024t * jax.lax.rsqrt(jnp.mean(jnp.square(_ctx_1024t)) + 1e-12) * 0.953939
        ctx_1024 = 0.000338537 + 0.999827 * (_ctx_1024t + 0.3 * jax.random.normal(jax.random.fold_in(_rk, 611), (32, 1601, 256), jnp.float32))
        return (x, ctx_1024)
    x, ctx_1024 = _rec_inputs()

    def _L0_xattn_setup():
        import jax, jax.numpy as jnp
        import numpy as np
        B, S, D = (4, 512, 256)
        H = 16
        HD = D // H
        SCALE = float(HD) ** 0.5

        def _split_heads(x):
            b, s, _ = x.shape
            return x.reshape(b, s, H, HD).transpose(0, 2, 1, 3)
        key = jax.random.key(seed)
        ks = jax.random.split(key, 12)
        lim = 1.0 / np.sqrt(D)

        def lin(kw, kb, out_d, in_d):
            W = jax.random.uniform(kw, (out_d, in_d), jnp.float32, -lim, lim)
            b = jax.random.uniform(kb, (out_d,), jnp.float32, -lim, lim)
            return (W, b)
        Wq, bq = lin(ks[0], ks[1], D, D)
        Wk, bk = lin(ks[2], ks[3], D, D)
        Wv, bv = lin(ks[4], ks[5], D, D)
        Wp, bp = lin(ks[6], ks[7], D, D)
        return {'query': jax.random.normal(ks[8], (B, S, D), jnp.float32), 'key': jax.random.normal(ks[9], (B, S, D), jnp.float32), 'value': jax.random.normal(ks[10], (B, S, D), jnp.float32), 'Wq': Wq, 'bq': bq, 'Wk': Wk, 'bk': bk, 'Wv': Wv, 'bv': bv, 'Wp': Wp, 'bp': bp}
    _L0_xattn_all = _L0_xattn_setup()
    _L0_xattn_in = {k: v for k, v in _L0_xattn_all.items() if k in ('Wq', 'bq', 'Wk', 'bk', 'Wv', 'bv', 'Wp', 'bp')}
    del _L0_xattn_all

    def _L0_attn_setup():
        import jax, jax.numpy as jnp
        import numpy as np
        EPS = 1e-05

        def layer_norm(x, g, b):
            mu = jnp.mean(x, axis=-1, keepdims=True)
            var = jnp.mean((x - mu) ** 2, axis=-1, keepdims=True)
            return (x - mu) * jax.lax.rsqrt(var + EPS) * g + b

        def quantum_circuit(v):
            return jnp.cumprod(jnp.cos(v), axis=-1)
        key = jax.random.key(seed)
        ks = jax.random.split(key, 8)
        B, T, C, H = (4, 512, 256, 16)
        dk = C // H
        nq_ffn, ffn_dim = (16, 1024)
        return {'x': jax.random.normal(ks[0], (B, T, C), dtype=jnp.float32) * 0.5, 'attn_circuit_params': jax.random.normal(ks[1], (H, dk), dtype=jnp.float32), 'ffn_circuit_params': jax.random.normal(ks[2], (nq_ffn,), dtype=jnp.float32), 'w1': jax.random.normal(ks[3], (ffn_dim, nq_ffn), dtype=jnp.float32) * 0.1, 'b1': jnp.zeros((ffn_dim,), dtype=jnp.float32), 'w2': jax.random.normal(ks[4], (C, ffn_dim), dtype=jnp.float32) * 0.02, 'b2': jnp.zeros((C,), dtype=jnp.float32), 'gamma1': jnp.ones((C,), dtype=jnp.float32), 'beta1': jnp.zeros((C,), dtype=jnp.float32), 'gamma2': jnp.ones((C,), dtype=jnp.float32), 'beta2': jnp.zeros((C,), dtype=jnp.float32)}
    _L0_attn_all = _L0_attn_setup()
    _L0_attn_in = {k: v for k, v in _L0_attn_all.items() if k in ('attn_circuit_params', 'ffn_circuit_params', 'w1', 'b1', 'w2', 'b2', 'gamma1', 'beta1', 'gamma2', 'beta2')}
    del _L0_attn_all

    def _L0_ffn_setup():
        import jax, jax.numpy as jnp
        import numpy as np
        H, I, E_ROUTED, TOP_K = (256, 704, 7, 2)
        B, S = (4, 512)

        def _expert(h, g, u, d):
            return jnp.einsum('...i,hi->...h', jax.nn.silu(h @ g.T) * (h @ u.T), d)
        key = jax.random.key(seed)
        ks = jax.random.split(key, 10)
        sc = 0.02
        return {'x': jax.random.normal(ks[0], (B, S, H), dtype=jnp.float32), 'sg': jax.random.normal(ks[1], (I, H), dtype=jnp.float32) * sc, 'su': jax.random.normal(ks[2], (I, H), dtype=jnp.float32) * sc, 'sd': jax.random.normal(ks[3], (H, I), dtype=jnp.float32) * sc, 'rg': jax.random.normal(ks[4], (E_ROUTED, I, H), dtype=jnp.float32) * sc, 'ru': jax.random.normal(ks[5], (E_ROUTED, I, H), dtype=jnp.float32) * sc, 'rd': jax.random.normal(ks[6], (E_ROUTED, H, I), dtype=jnp.float32) * sc, 'wr': jax.random.normal(ks[7], (E_ROUTED, H), dtype=jnp.float32) * sc, 'rb': jnp.zeros((E_ROUTED,), dtype=jnp.float32)}
    _L0_ffn_all = _L0_ffn_setup()
    _L0_ffn_in = {k: v for k, v in _L0_ffn_all.items() if k in ('sg', 'su', 'sd', 'rg', 'ru', 'rd', 'wr', 'rb')}
    del _L0_ffn_all
    return {'x': x, 'ctx_1024': ctx_1024, 'L0_xattn_Wq': _L0_xattn_in['Wq'], 'L0_xattn_bq': _L0_xattn_in['bq'], 'L0_xattn_Wk': _L0_xattn_in['Wk'], 'L0_xattn_bk': _L0_xattn_in['bk'], 'L0_xattn_Wv': _L0_xattn_in['Wv'], 'L0_xattn_bv': _L0_xattn_in['bv'], 'L0_xattn_Wp': _L0_xattn_in['Wp'], 'L0_xattn_bp': _L0_xattn_in['bp'], 'L0_attn_attn_circuit_params': _L0_attn_in['attn_circuit_params'], 'L0_attn_ffn_circuit_params': _L0_attn_in['ffn_circuit_params'], 'L0_attn_w1': _L0_attn_in['w1'], 'L0_attn_b1': _L0_attn_in['b1'], 'L0_attn_w2': _L0_attn_in['w2'], 'L0_attn_b2': _L0_attn_in['b2'], 'L0_attn_gamma1': _L0_attn_in['gamma1'], 'L0_attn_beta1': _L0_attn_in['beta1'], 'L0_attn_gamma2': _L0_attn_in['gamma2'], 'L0_attn_beta2': _L0_attn_in['beta2'], 'L0_ffn_sg': _L0_ffn_in['sg'], 'L0_ffn_su': _L0_ffn_in['su'], 'L0_ffn_sd': _L0_ffn_in['sd'], 'L0_ffn_rg': _L0_ffn_in['rg'], 'L0_ffn_ru': _L0_ffn_in['ru'], 'L0_ffn_rd': _L0_ffn_in['rd'], 'L0_ffn_wr': _L0_ffn_in['wr'], 'L0_ffn_rb': _L0_ffn_in['rb']}

def reference(x, ctx_1024, L0_xattn_Wq, L0_xattn_bq, L0_xattn_Wk, L0_xattn_bk, L0_xattn_Wv, L0_xattn_bv, L0_xattn_Wp, L0_xattn_bp, L0_attn_attn_circuit_params, L0_attn_ffn_circuit_params, L0_attn_w1, L0_attn_b1, L0_attn_w2, L0_attn_b2, L0_attn_gamma1, L0_attn_beta1, L0_attn_gamma2, L0_attn_beta2, L0_ffn_sg, L0_ffn_su, L0_ffn_sd, L0_ffn_rg, L0_ffn_ru, L0_ffn_rd, L0_ffn_wr, L0_ffn_rb):
    import jax
    import jax.numpy as jnp

    def _L0_xattn_ref(query, key, value, Wq, bq, Wk, bk, Wv, bv, Wp, bp):
        import jax, jax.numpy as jnp
        import numpy as np
        B, S, D = (4, 512, 256)
        H = 16
        HD = D // H
        SCALE = float(HD) ** 0.5

        def _split_heads(x):
            b, s, _ = x.shape
            return x.reshape(b, s, H, HD).transpose(0, 2, 1, 3)
        q = _split_heads(query @ Wq.T + bq)
        k = _split_heads(key @ Wk.T + bk)
        v = _split_heads(value @ Wv.T + bv)
        score = jnp.einsum('bhqd,bhkd->bhqk', q, k) * SCALE
        attn = jax.nn.softmax(score, axis=-1)
        out = jnp.einsum('bhqk,bhkd->bhqd', attn, v)
        out = out.transpose(0, 2, 1, 3).reshape(query.shape[0], query.shape[1], D)
        return out @ Wp.T + bp

    def _L0_attn_ref(x, attn_circuit_params, ffn_circuit_params, w1, b1, w2, b2, gamma1, beta1, gamma2, beta2):
        import jax, jax.numpy as jnp
        import numpy as np
        EPS = 1e-05

        def layer_norm(x, g, b):
            mu = jnp.mean(x, axis=-1, keepdims=True)
            var = jnp.mean((x - mu) ** 2, axis=-1, keepdims=True)
            return (x - mu) * jax.lax.rsqrt(var + EPS) * g + b

        def quantum_circuit(v):
            return jnp.cumprod(jnp.cos(v), axis=-1)
        B, T, C = x.shape
        H, dk = attn_circuit_params.shape
        nq = ffn_circuit_params.shape[0]
        xh = x.reshape(B, T, H, dk)
        attn_out = quantum_circuit(xh).reshape(B, T, C)
        x1 = layer_norm(x + attn_out, gamma1, beta1)
        q = quantum_circuit(x1[..., :nq])
        h = jnp.einsum('btq,fq->btf', q, w1) + b1
        ffn_out = jnp.einsum('btf,cf->btc', jax.nn.relu(h), w2) + b2
        return layer_norm(x1 + ffn_out, gamma2, beta2)

    def _L0_ffn_ref(x, sg, su, sd, rg, ru, rd, wr, rb):
        import jax, jax.numpy as jnp
        import numpy as np
        H, I, E_ROUTED, TOP_K = (256, 704, 7, 2)
        B, S = (4, 512)

        def _expert(h, g, u, d):
            return jnp.einsum('...i,hi->...h', jax.nn.silu(h @ g.T) * (h @ u.T), d)
        shared_out = _expert(x, sg, su, sd)
        logits = x @ wr.T + rb
        probs = jax.nn.softmax(logits, axis=-1)
        scores, idx = jax.lax.top_k(probs, TOP_K)
        scores = scores / scores.sum(axis=-1, keepdims=True)
        w = jnp.sum(scores[..., None] * jax.nn.one_hot(idx, E_ROUTED, dtype=x.dtype), axis=-2)
        out = shared_out
        for e in range(E_ROUTED):
            out = out + w[..., e:e + 1] * _expert(x, rg[e], ru[e], rd[e])
        return out
    x = x + _L0_xattn_ref(_layernorm(x, axis=-1), ctx_1024, ctx_1024, L0_xattn_Wq, L0_xattn_bq, L0_xattn_Wk, L0_xattn_bk, L0_xattn_Wv, L0_xattn_bv, L0_xattn_Wp, L0_xattn_bp)
    x = x + _L0_attn_ref(_layernorm(x, axis=-1), L0_attn_attn_circuit_params, L0_attn_ffn_circuit_params, L0_attn_w1, L0_attn_b1, L0_attn_w2, L0_attn_b2, L0_attn_gamma1, L0_attn_beta1, L0_attn_gamma2, L0_attn_beta2)
    x = x + _L0_ffn_ref(_layernorm(x, axis=-1), L0_ffn_sg, L0_ffn_su, L0_ffn_sd, L0_ffn_rg, L0_ffn_ru, L0_ffn_rd, L0_ffn_wr, L0_ffn_rb)
    return x

_drawn_inputs = setup_inputs


def setup_inputs(seed=0):
    import zlib

    import numpy as np

    out = dict(_drawn_inputs(seed))
    spreads = {'L0_attn_b1': (0.0, 0.401),
     'L0_attn_b2': (0.0, 0.1),
     'L0_attn_gamma1': (1.0, 0.2),
     'L0_attn_beta1': (0.0, 0.1),
     'L0_attn_gamma2': (1.0, 0.2),
     'L0_attn_beta2': (0.0, 0.1),
     'L0_ffn_rb': (0.0, 0.8)}
    factors = {'L0_xattn_bk': 8.0,
     'L0_xattn_bv': 2.671,
     'L0_attn_w1': 3.83,
     'L0_ffn_sg': 3.878,
     'L0_ffn_su': 3.613,
     'L0_ffn_sd': 3.555,
     'L0_ffn_rg': 5.94,
     'L0_ffn_ru': 5.861,
     'L0_ffn_rd': 5.852,
     'L0_ffn_wr': 7.051}
    for name, (base, spread) in spreads.items():
        noise = np.random.default_rng([zlib.crc32(name.encode()), seed]).standard_normal(out[name].shape)
        drawn = base * np.exp(spread * noise) if base else spread * noise
        out[name] = jnp.asarray(drawn.astype(out[name].dtype))
    for name, factor in factors.items():
        out[name] = (out[name] * factor).astype(out[name].dtype)
    return out
```

```python
import numpy as np
from contextlib import ExitStack

import concourse.bass as bass
from concourse import mybir

F32 = mybir.dt.float32
F32R = mybir.dt.float32r
ALU = mybir.AluOpType
ACT = mybir.ActivationFunctionType
AX = mybir.AxisListType

P = 128
B, SQ, D = 32, 64, 256
SK = 1601
H, HD = 16, 16
NC = D // P
PAIRS = H // 2
QK = 4
KQ = 402
SKP = QK * KQ
KLAST = SK - (QK - 1) * KQ
KT = -(-SK // P)
KTL = SK - (KT - 1) * P
TG = -(-KT // 4)
NT = B * SQ // P
KSTEPS = NC * QK
VSTEPS = -(-KT // 2)
STEPS = KSTEPS + VSTEPS
V_ORDER = [("v", 2 * i) for i in range(VSTEPS)]
K_ORDER = [("k", i // QK, i % QK) for i in range(KSTEPS)]
STEP_ORDER = V_ORDER[0:3] + K_ORDER[0:QK] + V_ORDER[3:] + K_ORDER[QK:]
PAIR_STEPS = [(None, 0), (1, 2), (3, 4), (5, 6), (7, 8), (9, 10), (11, 12), (13, 14)]
HALF = PAIRS // NC
STACK = 3 * 32
COPIES = 16 * 3 * HALF
SCALE = float(HD) ** 0.5
EPS = 1e-5
FF = 1024
FC = FF // P
E, EI = 7, 704
EC = -(-EI // P)
NEXP = E + 1
TOK = B * SQ
GT = 4
NG = NT // GT
TWO_PI_PARTS = (6.28125, 1.93500518798828125e-3, 3.0199159819567e-7)
ROUND = 12582912.0


def rows_keys(t):
    return P if t < KT - 1 else KTL


def project_queries(nc, x, wq, bq, ident, q_scr):
    with ExitStack() as ctx:
        sb = lambda n, s, d=F32: ctx.enter_context(nc.sbuf_tensor(n, s, d))
        sem = lambda n: ctx.enter_context(nc.semaphore(n))
        x_sb = sb("q_x", [P, NT, D])
        wq_sb = sb("q_wq", [P, NC, D])
        bq_sb = sb("q_bq", [P, NC])
        id_sb = sb("q_id", [P, P])
        stats = sb("q_stats", [P, NT, 6])
        mv = sb("q_mv", [P, NT, 2])
        vare = sb("q_vare", [P, NT])
        expo = sb("q_expo", [P, NT])
        rstd = sb("q_rstd", [P, NT])
        xT = sb("q_xT", [P, NC, TOK])
        qT = sb("q_qT", [P, 2, 512])
        q_hi = sb("q_hi", [P, NC, TOK], F32R)
        q_lo = sb("q_lo", [P, NC, TOK], F32R)
        ps_t = ctx.enter_context(nc.psum_tensor("q_pst", [P, 2, 512], F32))
        ps_q = ctx.enter_context(nc.psum_tensor("q_psq", [P, 2, 512], F32))
        w_loaded, x_loaded, stored = sem("q_w_loaded"), sem("q_x_loaded"), sem("q_stored")
        stat_done, aggr_done, var_done, pow_set, pow_done, norm_done = (
            sem("q_stat"), sem("q_aggr"), sem("q_var"), sem("q_pset"), sem("q_pow"), sem("q_norm"))
        t_filled, t_copied, q_filled, q_biased, q_split = (
            sem("q_tf"), sem("q_tc"), sem("q_qf"), sem("q_qb"), sem("q_split"))
        block = ctx.enter_context(nc.Block())

        @block.sync
        def _(sp):
            sp.dma_start(x_sb[:], x.rearrange("t p d -> p t d")).then_inc(x_loaded, 16)
            sp.dma_start(wq_sb[:], wq).then_inc(w_loaded, 16)
            sp.dma_start(bq_sb[:], bq).then_inc(w_loaded, 16)
            sp.dma_start(id_sb[:], ident).then_inc(w_loaded, 16)
            sp.wait_ge(q_split, 2 * NC * NG)
            sp.dma_start(q_scr[0].rearrange("(m p) t -> p m t", p=P), q_hi[:].bitcast(F32)).then_inc(stored, 16)
            sp.dma_start(q_scr[1].rearrange("(m p) t -> p m t", p=P), q_lo[:].bitcast(F32)).then_inc(stored, 16)
            sp.wait_ge(stored, 32)

        @block.gpsimd
        def _(pool):
            nc.gpsimd.memset(expo[:], -0.5).then_inc(pow_set, 1)
            pool.wait_ge(pow_set, 1)
            pool.wait_ge(var_done, 1)
            nc.gpsimd.tensor_tensor(out=rstd[:], in0=vare[:], in1=expo[:], op=ALU.pow).then_inc(pow_done, 1)

        @block.vector
        def _(dve):
            dve.wait_ge(x_loaded, 16)
            for t in range(NT):
                nc.vector.bn_stats(out=stats[:, t, :], in_=x_sb[:, t, :]).then_inc(stat_done, 1)
            for t in range(NT):
                dve.wait_ge(stat_done, t + 1)
                nc.vector.bn_aggr(out=mv[:, t, :], in_=stats[:, t, :]).then_inc(aggr_done, 1)
            dve.wait_ge(aggr_done, NT)
            nc.vector.tensor_scalar(vare[:], mv[:, :, 1], EPS, None, ALU.add).then_inc(var_done, 1)
            dve.wait_ge(pow_done, 1)
            for t in range(NT):
                nc.vector.tensor_scalar(x_sb[:, t, :], x_sb[:, t, :], mv[:, t, 0:1], rstd[:, t:t + 1],
                                        ALU.subtract, ALU.mult).then_inc(norm_done, 1)
            for i in range(NC * NG):
                g, m = i // NC, i % NC
                dve.wait_ge(q_filled, i + 1)
                if i >= 2:
                    dve.wait_ge(q_split, 2 * (i - 1))
                nc.vector.tensor_scalar(qT[:, i % 2, :], ps_q[:, i % 2, :], bq_sb[:, m:m + 1], SCALE,
                                        ALU.add, ALU.mult).then_inc(q_biased, 1)
                dve.wait_ge(q_biased, i + 1)
                hi = q_hi[:, m, g * 512:(g + 1) * 512]
                nc.vector.tensor_copy(hi, qT[:, i % 2, :]).then_inc(q_split, 1)
                dve.wait_ge(q_split, 2 * i + 1)
                nc.vector.tensor_tensor(q_lo[:, m, g * 512:(g + 1) * 512], qT[:, i % 2, :], hi.bitcast(F32),
                                        ALU.subtract).then_inc(q_split, 1)

        @block.scalar
        def _(act):
            for i in range(NC * NG):
                act.wait_ge(t_filled, i + 1)
                g, k = i // NC, i % NC
                nc.scalar.copy(xT[:, k, g * 512:(g + 1) * 512], ps_t[:, i % 2, :]).then_inc(t_copied, 1)

        @block.tensor
        def _(pe):
            pe.wait_ge(w_loaded, 48)
            for g in range(NG):
                for k in range(NC):
                    i = g * NC + k
                    pe.wait_ge(norm_done, GT * (g + 1))
                    if i >= 2:
                        pe.wait_ge(t_copied, i - 1)
                    for j in range(GT):
                        mm = nc.tensor.transpose(ps_t[:, i % 2, j * P:(j + 1) * P],
                                                 x_sb[:, GT * g + j, k * P:(k + 1) * P], id_sb[:])
                    mm.then_inc(t_filled, 1)
            for g in range(NG):
                pe.wait_ge(t_copied, NC * (g + 1))
                for m in range(NC):
                    i = g * NC + m
                    if i >= 2:
                        pe.wait_ge(q_biased, i - 1)
                    for k in range(NC):
                        mm = nc.tensor.matmul(ps_q[:, i % 2, :], wq_sb[:, k, m * P:(m + 1) * P],
                                              xT[:, k, g * 512:(g + 1) * 512], start=(k == 0), stop=(k == NC - 1))
                    mm.then_inc(q_filled, 1)


def cross_attention(nc, ctxT, x, q_scr, wk, bk, wv, bv, wp, rows, ident, sel4, hmask, x1_scr):
    with ExitStack() as ctx:
        sb = lambda n, s, d=F32: ctx.enter_context(nc.sbuf_tensor(n, s, d))
        ps = lambda n, s: ctx.enter_context(nc.psum_tensor(n, s, F32))
        sem = lambda n: ctx.enter_context(nc.semaphore(n))
        raw = sb("a_raw", [P, NC, SKP])
        c_hi, c_lo = sb("a_chi", [P, 2, NC, SKP], F32R), sb("a_clo", [P, 2, NC, SKP], F32R)
        k_hi, k_lo = sb("a_khi", [P, SKP], F32R), sb("a_klo", [P, SKP], F32R)
        k_st = sb("a_kst", [STACK, PAIRS, SKP], F32R)
        v_sb = sb("a_v", [P, 2, KT, D])
        probs = sb("a_probs", [P, 2, SKP])
        pT = sb("a_pT", [P, KT, P])
        w_raw = probs[:, 0, 0:2 * NC * D].rearrange("p (w k d) -> p w k d", w=2, k=NC)
        w_hi, w_lo = sb("a_whi", [P, 2, NC, D], F32R), sb("a_wlo", [P, 2, NC, D], F32R)
        bk_sb, bv_sb = sb("a_bk", [P, NC]), sb("a_bv", [P, 2])
        wp_sb = sb("a_wp", [P, 2, D])
        bp_sb = sb("a_bp", [P, D])
        id_sb, sel_sb, hm_sb = sb("a_id", [P, P]), sb("a_sel", [P, 32]), sb("a_hm", [STACK, 2])
        q_sb = sb("a_q", [STACK, PAIRS, SQ])
        bd = sb("a_bd", [STACK, 2, PAIRS, P], F32R)
        o_part = sb("a_op", [P, 2, PAIRS, P])
        tick = sb("a_tick", [P, 1])
        ticked = sem("a_tk")
        nmax = sb("a_nmax", [P, 2, PAIRS])
        esum = sb("a_esum", [P, 2, PAIRS, 2])
        rsum, rinv = sb("a_rsum", [P, PAIRS]), sb("a_rinv", [P, PAIRS])
        o_head = sb("a_oh", [P, PAIRS, HD])
        oT = sb("a_oT", [P, 2, P])
        x_t, y_t, x1_t = sb("a_x", [P, D]), sb("a_y", [P, D]), sb("a_x1", [P, D])
        ps_s, ps_t, ps_o, ps_k = ps("a_pss", [P, QK, 512]), ps("a_pst", [P, 2, 512]), ps("a_pso", [P, 512]), ps("a_psk", [P, 512])

        const_loaded, ctx_loaded, q_loaded, x_loaded = sem("a_cl"), sem("a_ctxl"), sem("a_ql"), sem("a_xl")
        stacked = [sem("a_st0"), sem("a_st1")]
        w_split, ctx_hi_done, ctx_split, bd_ready = sem("a_ws"), sem("a_ch"), sem("a_cs"), sem("a_bd")
        kv_filled, k_hi_done, kv_copied = sem("a_kvf"), sem("a_khd"), sem("a_kvc")
        s_filled, max_ready, probs_ready = sem("a_sf"), sem("a_mr"), sem("a_pr")
        t_filled, t_copied_act, t_copied_dve = sem("a_tf"), sem("a_tca"), sem("a_tcd")
        o_filled, o_copied = sem("a_of"), sem("a_oc")
        sum_filled, sum_step, head_ready, hT_filled, hT_copied = (
            sem("a_suf"), sem("a_sus"), sem("a_hr"), sem("a_htf"), sem("a_htc"))
        y_filled, y_biased, x1_ready, x1_free = sem("a_yf"), sem("a_yb"), sem("a_x1r"), sem("a_x1f")
        block = ctx.enter_context(nc.Block())

        @block.sync
        def _(sp):
            def load_queries(n):
                for i, part in enumerate((0, 0, 1)):
                    src = q_scr[part, :, bass.ds(n * SQ, SQ)].rearrange("(p r) t -> r p t", r=32)
                    sp.dma_start(q_sb[32 * i:32 * i + 32], src).then_inc(q_loaded, 16)

            def stack_keys(m):
                for j in range(HALF):
                    for i, part in enumerate((k_hi, k_lo, k_hi)):
                        sp.dma_start(k_st[32 * i:32 * i + 32, HALF * m + j, :].bitcast(F32),
                                     part[32 * j:32 * j + 32, :].bitcast(F32)).then_inc(stacked[m], 16)

            sp.dma_start(w_raw[:, 0], wk).then_inc(const_loaded, 16)
            sp.dma_start(w_raw[:, 1], wv).then_inc(const_loaded, 16)
            sp.dma_start(raw[:], ctxT[0]).then_inc(ctx_loaded, 16)
            load_queries(0)
            for dst, src in ((bk_sb[:], bk), (bv_sb[:], bv), (wp_sb[:], wp), (bp_sb[:], rows[:, 0]),
                             (id_sb[:], ident), (sel_sb[:], sel4), (hm_sb[:], hmask)):
                sp.dma_start(dst, src).then_inc(const_loaded, 16)
            sp.wait_ge(ctx_split, 1)
            sp.dma_start(raw[:], ctxT[1]).then_inc(ctx_loaded, 16)
            sp.wait_ge(kv_copied, STEP_ORDER.index(("k", 0, QK - 1)) + 1)
            stack_keys(0)

            def body(it, first, last):
                for b in range(2):
                    n = 2 * it + b
                    sp.wait_ge(kv_copied, STEPS * (n + 1))
                    stack_keys(1)
                    if not (last and b == 1):
                        sp.wait_ge(bd_ready, n + 1)
                        load_queries(n + 1)
                    if not last:
                        sp.wait_ge(ctx_split, n + 2)
                        sp.dma_start(raw[:], ctxT[bass.ds(n + 2, 1)].rearrange("a p k s -> p (a k) s")).then_inc(ctx_loaded, 16)
                    if b == 0 and not first:
                        sp.dma_start(x_t[:], x[bass.ds(it - 1, 1)].rearrange("a p d -> (a p) d")).then_inc(x_loaded, 16)
                    if not (last and b == 1):
                        sp.wait_ge(kv_copied, STEPS * (n + 1) + STEP_ORDER.index(("k", 0, QK - 1)) + 1)
                        stack_keys(0)
                    if b == 0 and not first:
                        sp.wait_ge(x1_ready, it)
                        sp.dma_start(x1_scr[bass.ds(it - 1, 1)].rearrange("a p d -> (a p) d"), x1_t[:]).then_inc(x1_free, 16)

            body(0, True, False)
            with sp.Fori(1, NT - 1) as it:
                body(it, False, False)
            body(NT - 1, False, True)
            sp.wait_ge(x1_ready, NT - 1)
            sp.dma_start(x_t[:], x[NT - 1]).then_inc(x_loaded, 16)
            sp.wait_ge(x1_ready, NT)
            sp.dma_start(x1_scr[NT - 1], x1_t[:]).then_inc(x1_free, 16)
            sp.wait_ge(x1_free, 16 * NT + 1)

        @block.gpsimd
        def _(pool):
            def split_ctx(n, s):
                pool.wait_ge(ctx_loaded, 16 * n + 16)
                nc.gpsimd.tensor_tensor(out=tick[:], in0=tick[:], in1=tick[:], op=ALU.mult).then_inc(ticked, 1)
                nc.gpsimd.tensor_copy(c_hi[:, s], raw[:]).then_inc(ctx_hi_done, 1)
                pool.wait_ge(ctx_hi_done, n + 1)
                nc.gpsimd.tensor_tensor(out=c_lo[:, s], in0=raw[:], in1=c_hi[:, s].bitcast(F32),
                                        op=ALU.subtract).then_inc(ctx_split, 1)

            def spread_queries(n, s):
                pool.wait_ge(q_loaded, 48 * n + 48)
                nc.gpsimd.tensor_tensor(
                    out=bd[:, s].rearrange("r p (h q) -> r p h q", h=2),
                    in0=q_sb[:].unsqueeze(2).to_broadcast([STACK, PAIRS, 2, SQ]),
                    in1=hm_sb[:].unsqueeze(1).unsqueeze(3).to_broadcast([STACK, PAIRS, 2, SQ]),
                    op=ALU.mult).then_inc(bd_ready, 1)

            nc.gpsimd.memset(tick[:], 0.0).then_inc(ticked, 1)
            pool.wait_ge(ticked, 1)
            pool.wait_ge(const_loaded, 16 * 9)
            nc.gpsimd.tensor_copy(w_hi[:], w_raw).then_inc(w_split, 1)
            pool.wait_ge(w_split, 1)
            nc.gpsimd.tensor_tensor(out=w_lo[:], in0=w_raw, in1=w_hi[:].bitcast(F32), op=ALU.subtract).then_inc(w_split, 1)
            split_ctx(0, 0)
            spread_queries(0, 0)
            split_ctx(1, 1)

            def body(it, first, last):
                for b in range(2):
                    n = 2 * it + b
                    if not (last and b == 1):
                        if not (first and b == 0):
                            pool.wait_ge(s_filled, PAIRS * n)
                        spread_queries(n + 1, (b + 1) % 2)
                    if not last:
                        pool.wait_ge(kv_filled, STEPS * (n + 1))
                        split_ctx(n + 2, b)

            body(0, True, False)
            with pool.Fori(1, NT - 1) as it:
                body(it, False, False)
            body(NT - 1, False, True)

        @block.scalar
        def _(act):
            def copy_tiles(g, i):
                act.wait_ge(t_filled, TG * g + i + 1)
                nc.scalar.copy(pT[:, 4 * i:4 * i + 4, :], ps_t[:, i % 2, :].rearrange("p (t q) -> p t q", q=P)).then_inc(t_copied_act, 1)

            def exponentials(g, b, p):
                act.wait_ge(max_ready, g + 1)
                pr = probs[:, p % 2, :].rearrange("p (b k) -> p b k", b=QK)
                bias = nmax[:, b, p:p + 1]
                nc.scalar.activation(pr[:, 0:QK - 1, :], ps_s[:, 0:QK - 1, 0:KQ], ACT.Exp, bias=bias,
                                     accum_out=esum[:, b, p, 0:1])
                nc.scalar.activation(pr[:, QK - 1, 0:KLAST], ps_s[:, QK - 1, 0:KLAST], ACT.Exp, bias=bias,
                                     accum_out=esum[:, b, p, 1:2]).then_inc(probs_ready, 1)

            def copy_out(g, b, p):
                act.wait_ge(o_filled, g + 1)
                nc.scalar.copy(o_part[:, b, p, :], ps_o[:, 0:P]).then_inc(o_copied, 1)

            def body(it, first, last):
                for b in range(2):
                    for p in range(PAIRS):
                        g = PAIRS * (2 * it + b) + p
                        start = first and b == 0 and p == 0
                        if not start:
                            copy_tiles(g - 1, 0)
                            copy_tiles(g - 1, 1)
                        exponentials(g, b, p)
                        if not start:
                            copy_out(g - 1, b if p > 0 else 1 - b, (p - 1) % PAIRS)

            body(0, True, False)
            with act.Fori(1, NT - 1) as it:
                body(it, False, False)
            body(NT - 1, False, True)
            g = PAIRS * B - 1
            copy_tiles(g, 0)
            copy_tiles(g, 1)
            copy_out(g, 1, PAIRS - 1)

        @block.vector
        def _(dve):
            def row_max(g, b, p):
                dve.wait_ge(s_filled, g + 1)
                nc.vector.tensor_reduce(nmax[:, b, p:p + 1], ps_s[:, :, 0:KQ], AX.XY, ALU.max, negate=True).then_inc(max_ready, 1)

            def copy_step(n, slot, s):
                dve.wait_ge(kv_filled, STEPS * n + s + 1)
                kind, *at = STEP_ORDER[s]
                if kind == "k":
                    m, q = at
                    if q == 0 and m == 1:
                        dve.wait_ge(stacked[0], COPIES * (n + 1))
                    if q == 0 and m == 0 and not (isinstance(n, int) and n == 0):
                        dve.wait_ge(stacked[1], COPIES * n)
                    hi, lo = (t[:, q * KQ:(q + 1) * KQ] for t in (k_hi, k_lo))
                    nc.vector.tensor_scalar(hi, ps_k[:, 0:KQ], bk_sb[:, m:m + 1], None, ALU.add).then_inc(k_hi_done, 1)
                    dve.wait_ge(k_hi_done, KSTEPS * n + QK * m + q + 1)
                    nc.vector.scalar_tensor_tensor(out=lo, in0=ps_k[:, 0:KQ], scalar=bk_sb[:, m:m + 1], in1=hi.bitcast(F32),
                                                   op0=ALU.add, op1=ALU.subtract).then_inc(kv_copied, 1)
                else:
                    t = at[0]
                    if t < KT - 1:
                        nc.vector.tensor_copy(v_sb[:, slot, t:t + 2, :], ps_k[:].rearrange("p (t d) -> p t d", t=2)).then_inc(kv_copied, 1)
                    else:
                        nc.vector.tensor_copy(v_sb[0:KTL, slot, t, :], ps_k[0:KTL, 0:D]).then_inc(kv_copied, 1)

            def copy_tiles(g, i):
                dve.wait_ge(t_filled, TG * g + i + 1)
                if i < TG - 1:
                    nc.vector.tensor_copy(pT[:, 4 * i:4 * i + 4, :], ps_t[:, i % 2, :].rearrange("p (t q) -> p t q", q=P)).then_inc(t_copied_dve, 1)
                else:
                    nc.vector.tensor_copy(pT[0:KTL, KT - 1, :], ps_t[0:KTL, i % 2, 0:P]).then_inc(t_copied_dve, 1)

            def normalise(n, b):
                dve.wait_ge(probs_ready, PAIRS * (n + 1))
                nc.vector.tensor_tensor(rsum[:], esum[:, b, :, 0], esum[:, b, :, 1], ALU.add).then_inc(sum_step, 1)
                dve.wait_ge(sum_step, 2 * n + 1)
                nc.vector.reciprocal(rinv[:], rsum[:]).then_inc(sum_step, 1)
                dve.wait_ge(sum_step, 2 * n + 2)
                dve.wait_ge(sum_filled, n + 1)
                for e in range(2):
                    r = slice(SQ * e, SQ * (e + 1))
                    last = nc.vector.tensor_tensor(
                        o_head[r, :, :], ps_k[r, 0:D].rearrange("p (j e d) -> p j e d", e=2, d=HD)[:, :, e, :],
                        rinv[r, :].unsqueeze(2).to_broadcast([SQ, PAIRS, HD]), ALU.mult)
                last.then_inc(head_ready, 1)

            def copy_heads(n, b):
                dve.wait_ge(hT_filled, n + 1)
                for e in range(2):
                    last = nc.vector.tensor_scalar(oT[:, e, SQ * b:SQ * (b + 1)], ps_k[:, SQ * e:SQ * (e + 1)],
                                                   bv_sb[:, e:e + 1], None, ALU.add)
                last.then_inc(hT_copied, 1)

            def residual(t):
                dve.wait_ge(y_filled, t + 1)
                nc.vector.tensor_tensor(y_t[:], ps_k[:, 0:D], bp_sb[:], ALU.add).then_inc(y_biased, 1)
                dve.wait_ge(y_biased, t + 1)
                dve.wait_ge(x_loaded, 16 * (t + 1))
                dve.wait_ge(x1_free, 16 * t + 1)
                nc.vector.tensor_tensor(x1_t[:], y_t[:], x_t[:], ALU.add).then_inc(x1_ready, 1)

            nc.vector.memset(x1_t[:], 0.0).then_inc(x1_free, 1)
            dve.wait_ge(const_loaded, 16 * 9)
            for s in range(STEPS):
                copy_step(0, 0, s)

            def body(it, first, last):
                for b in range(2):
                    n = 2 * it + b
                    ahead = not (last and b == 1)
                    behind = not (first and b == 0)
                    for p in range(PAIRS):
                        g = PAIRS * n + p
                        row_max(g, b, p)
                        steps = PAIR_STEPS[p] if ahead else (None, None)
                        if steps[0] is not None:
                            copy_step(n + 1, 1 - b, steps[0])
                        if behind or p > 0:
                            copy_tiles(g - 1, 2)
                            copy_tiles(g - 1, 3)
                        if steps[1] is not None:
                            copy_step(n + 1, 1 - b, steps[1])
                        if behind and p == 1:
                            normalise(n - 1, 1 - b)
                        if behind and p == 3:
                            copy_heads(n - 1, 1 - b)
                        if behind and p == 5 and b == 0:
                            residual(it - 1)

            body(0, True, False)
            with dve.Fori(1, NT - 1) as it:
                body(it, False, False)
            body(NT - 1, False, True)
            copy_tiles(PAIRS * B - 1, 2)
            copy_tiles(PAIRS * B - 1, 3)
            normalise(B - 1, 1)
            copy_heads(B - 1, 1)
            residual(NT - 1)

        @block.tensor
        def _(pe):
            def three(out, a, b, start, stop):
                nc.tensor.matmul(out, a[0], b[0], start=start, stop=False)
                nc.tensor.matmul(out, a[0], b[1], start=False, stop=False)
                return nc.tensor.matmul(out, a[1], b[0], start=False, stop=stop)

            def step(n, slot, s, after=None):
                if not isinstance(n, int) or STEPS * n + s > 0:
                    pe.wait_ge(kv_copied, STEPS * n + s)
                kind, *at = STEP_ORDER[s]
                if kind == "k":
                    m, q = at
                    for k in range(NC):
                        mm = three(ps_k[:, 0:KQ], [w[:, 0, k, m * P:(m + 1) * P] for w in (w_hi, w_lo)],
                                   [c[:, slot, k, q * KQ:(q + 1) * KQ] for c in (c_hi, c_lo)], k == 0, k == NC - 1)
                else:
                    for t in range(at[0], min(at[0] + 2, KT)):
                        r = rows_keys(t)
                        for k in range(NC):
                            mm = three(ps_k[0:r, (t % 2) * D:(t % 2 + 1) * D],
                                       [c[:, slot, k, t * P:t * P + r] for c in (c_hi, c_lo)],
                                       [w[:, 1, k, :] for w in (w_hi, w_lo)], k == 0, k == NC - 1)
                mm.then_inc(kv_filled, 1)

            def scores(b, p):
                for q in range(QK):
                    mm = nc.tensor.matmul(ps_s[:, q, 0:KQ], bd[:, b, p, :], k_st[:, p, q * KQ:(q + 1) * KQ], start=True, stop=True)
                mm.then_inc(s_filled, 1)

            def turn(p, i):
                for t in range(4 * i, min(4 * i + 4, KT)):
                    r = rows_keys(t)
                    mm = nc.tensor.transpose(ps_t[0:r, i % 2, (t % 4) * P:(t % 4 + 1) * P],
                                             probs[:, p % 2, t * P:t * P + r], id_sb[:])
                mm.then_inc(t_filled, 1)

            def weigh(b, p, i):
                for t in range(4 * i, min(4 * i + 4, KT)):
                    r, c = rows_keys(t), 32 * (t % 4)
                    mm = nc.tensor.matmul(ps_o[c:c + 32, 0:P], v_sb[0:r, b, t, 32 * p:32 * p + 32], pT[0:r, t, :],
                                          start=(t < 4), stop=(t + 4 >= KT))
                return mm

            def sum_parts(n, b):
                pe.wait_ge(o_copied, PAIRS * (n + 1))
                for p in range(PAIRS):
                    mm = nc.tensor.matmul(ps_k[:, 32 * p:32 * p + 32], o_part[:, b, p, :], sel_sb[:], start=True, stop=True)
                mm.then_inc(sum_filled, 1)

            def turn_heads(n):
                pe.wait_ge(head_ready, n + 1)
                nc.tensor.transpose(ps_k[:, 0:P], o_head[:].rearrange("p j d -> p (j d)"), id_sb[:]).then_inc(hT_filled, 1)

            def project_out(t):
                pe.wait_ge(hT_copied, 2 * t + 2)
                for e in range(2):
                    mm = nc.tensor.matmul(ps_k[:, 0:D], oT[:, e, :], wp_sb[:, e, :], start=(e == 0), stop=(e == 1))
                mm.then_inc(y_filled, 1)

            def slot_tail(g, p, b, n, slot, steps):
                if g is not None:
                    if not isinstance(g, int) or g > 0:
                        pe.wait_ge(t_copied_dve, 2 * g)
                    turn(p, 0)
                    turn(p, 1)
                if steps[0] is not None:
                    step(n, slot, steps[0])
                if g is not None:
                    pe.wait_ge(t_copied_act, 2 * g + 1)
                    if not isinstance(g, int) or g > 0:
                        pe.wait_ge(o_copied, g)
                    weigh(b, p, 0)
                    turn(p, 2)
                    pe.wait_ge(t_copied_act, 2 * g + 2)
                    weigh(b, p, 1)
                    turn(p, 3)
                if steps[1] is not None:
                    step(n, slot, steps[1])
                if g is not None:
                    pe.wait_ge(t_copied_dve, 2 * g + 2)
                    weigh(b, p, 2)
                    weigh(b, p, 3).then_inc(o_filled, 1)

            pe.wait_ge(const_loaded, 16 * 9)
            pe.wait_ge(w_split, 2)
            pe.wait_ge(ctx_split, 1)
            for s in range(STEPS):
                step(0, 0, s)

            def body(it, first, last):
                for b in range(2):
                    n = 2 * it + b
                    ahead = not (last and b == 1)
                    behind = not (first and b == 0)
                    pe.wait_ge(bd_ready, n + 1)
                    pe.wait_ge(kv_copied, STEPS * (n + 1))
                    if ahead:
                        pe.wait_ge(ctx_split, n + 2)
                    for p in range(PAIRS):
                        g = PAIRS * n + p
                        if p % HALF == 0:
                            pe.wait_ge(stacked[p // HALF], COPIES * (n + 1))
                        if behind or p > 0:
                            pe.wait_ge(probs_ready, g)
                        scores(b, p)
                        before = g - 1 if behind or p > 0 else None
                        steps = PAIR_STEPS[p] if ahead else (None, None)
                        if behind and p == 2:
                            pe.wait_ge(head_ready, n)
                        if behind and p == 4:
                            pe.wait_ge(hT_copied, n)
                        if behind and p == 6 and b == 0:
                            pe.wait_ge(y_biased, it)
                        slot_tail(before, (p - 1) % PAIRS, b if p > 0 else 1 - b, n + 1, 1 - b, steps)
                        if behind and p in (1, 3) or (behind and p == 5 and b == 0):
                            if ahead:
                                pe.wait_ge(kv_copied, STEPS * (n + 1) + steps[-1] + 1)
                        if behind and p == 1:
                            sum_parts(n - 1, 1 - b)
                        if behind and p == 3:
                            turn_heads(n - 1)
                        if behind and p == 5 and b == 0:
                            project_out(it - 1)

            body(0, True, False)
            with pe.Fori(1, NT - 1) as it:
                body(it, False, False)
            body(NT - 1, False, True)
            pe.wait_ge(probs_ready, PAIRS * B)
            slot_tail(PAIRS * B - 1, PAIRS - 1, 1, None, 0, (None, None))
            sum_parts(B - 1, 1)
            turn_heads(B - 1)
            project_out(NT - 1)


class Chain:

    def __init__(self, eng, sem):
        self.eng, self.sem, self.n = eng, sem, 0

    def __call__(self, ins):
        self.n += 1
        ins.then_inc(self.sem, 1)
        return self.n

    def wait(self, n=None):
        self.eng.wait_ge(self.sem, self.n if n is None else n)


def circuit_ffn(nc, x1_scr, rows, w1, b1, w2, wr, rb, ident, x2_scr, x3_scr, mix_scr):
    with ExitStack() as ctx:
        sb = lambda n, s, d=F32: ctx.enter_context(nc.sbuf_tensor(n, s, d))
        ps = lambda n, s: ctx.enter_context(nc.psum_tensor(n, s, F32))
        sem = lambda n: ctx.enter_context(nc.semaphore(n))
        x1, a, t, c = (sb(f"f_{n}", [P, NT, D]) for n in ("x1", "a", "t", "c"))
        row = sb("f_rows", [P, 6, D])
        stats, mv, vare, expo, rstd = sb("f_st", [P, NT, 6]), sb("f_mv", [P, NT, 2]), sb("f_va", [P, NT]), sb("f_ex", [P, NT]), sb("f_rs", [P, NT])
        half_pi = sb("f_hp", [P, 1])
        qs = sb("f_qs", [P, NT, 16])
        qt = sb("f_qt", [P, NT, 16])
        w1_sb, b1_sb, w2_sb = sb("f_w1", [16, FF]), sb("f_b1", [P, FC]), sb("f_w2", [P, FC, D])
        wr_sb, rb_sb, id_sb = sb("f_wr", [P, NC, E]), sb("f_rb", [P, E]), sb("f_id", [P, P])
        qT, hT = sb("f_qT", [16, 512]), sb("f_hT", [P, FC, 512])
        xT = sb("f_xT", [P, 2, NC, P])
        lg, pr, rank, cmp, tiny = sb("f_lg", [P, NT, E]), sb("f_pr", [P, NT, E]), sb("f_rk", [P, NT, E]), sb("f_cmp", [P, NT, E]), sb("f_ty", [P, NT])
        mix = sb("f_mix", [P, NT, NEXP])
        ps_q, ps_h, ps_f, ps_x, ps_l = ps("f_psq", [16, 512]), ps("f_psh", [P, 2, 512]), ps("f_psf", [P, 2, 512]), ps("f_psx", [P, 2, 512]), ps("f_psl", [P, 512])
        loaded, stored = sem("f_ld"), sem("f_st")
        dv, var_done, pow_done, angle_ready, sin_done, x3_ready = sem("f_dv"), sem("f_vd"), sem("f_pd"), sem("f_ar"), sem("f_sd"), sem("f_x3r")
        qt_filled, qt_copied, h_filled, h_copied, f_filled, f_added = sem("f_qf"), sem("f_qc"), sem("f_hf"), sem("f_hc"), sem("f_ff"), sem("f_fa")
        xt_filled, xt_copied, l_filled, exp_in, exp_done, mix_ready = sem("f_xf"), sem("f_xc"), sem("f_lf"), sem("f_ei"), sem("f_ed"), sem("f_mr")
        q_ready, x2_ready = sem("f_qr"), sem("f_x2r")
        block = ctx.enter_context(nc.Block())
        G1, B1, FB, G2, B2 = 1, 2, 3, 4, 5

        @block.sync
        def _(sp):
            for dst, src in ((x1[:], x1_scr.rearrange("t p d -> p t d")), (row[:], rows), (w1_sb[:], w1), (b1_sb[:], b1),
                             (w2_sb[:], w2), (wr_sb[:], wr), (rb_sb[:], rb), (id_sb[:], ident)):
                sp.dma_start(dst, src).then_inc(loaded, 16)
            sp.wait_ge(x2_ready, 1)
            sp.dma_start(x2_scr.rearrange("t p d -> p t d"), x1[:]).then_inc(stored, 16)
            sp.wait_ge(x3_ready, 1)
            sp.dma_start(x3_scr.rearrange("t p d -> p t d"), a[:]).then_inc(stored, 16)
            sp.wait_ge(mix_ready, 1)
            sp.dma_start(mix_scr, mix[:]).then_inc(stored, 16)
            sp.wait_ge(stored, 48)

        @block.gpsimd
        def _(pool):
            nc.gpsimd.memset(expo[:], -0.5).then_inc(pow_done, 1)
            pool.wait_ge(pow_done, 1)
            for i in range(4):
                pool.wait_ge(var_done, i + 1)
                nc.gpsimd.tensor_tensor(out=rstd[:], in0=vare[:], in1=expo[:], op=ALU.pow).then_inc(pow_done, 1)

        @block.vector
        def _(dve):
            ch = Chain(dve, dv)
            norms = [0]

            def v(ins):
                ch(ins)
                ch.wait()

            def bc(r, n=NT):
                return row[:, r, :].unsqueeze(1).to_broadcast([P, n, D])

            def layer_norm(dst, src):
                for i in range(NT):
                    ch(nc.vector.bn_stats(out=stats[:, i, :], in_=src[:, i, :]))
                ch.wait()
                for i in range(NT):
                    ch(nc.vector.bn_aggr(out=mv[:, i, :], in_=stats[:, i, :]))
                ch.wait()
                nc.vector.tensor_scalar(vare[:], mv[:, :, 1], EPS, None, ALU.add).then_inc(var_done, 1)
                norms[0] += 1
                dve.wait_ge(pow_done, norms[0] + 1)
                for i in range(NT):
                    ch(nc.vector.tensor_scalar(dst[:, i, :], src[:, i, :], mv[:, i, 0:1], rstd[:, i:i + 1], ALU.subtract, ALU.mult))
                ch.wait()

            def angle(dst, src, tmp):
                v(nc.vector.tensor_scalar(tmp, src, 1.0 / (2.0 * np.pi), ROUND, ALU.mult, ALU.add))
                v(nc.vector.tensor_scalar(tmp, tmp, ROUND, None, ALU.subtract))
                v(nc.vector.scalar_tensor_tensor(out=dst, in0=tmp, scalar=-TWO_PI_PARTS[0], in1=src, op0=ALU.mult, op1=ALU.add))
                v(nc.vector.scalar_tensor_tensor(out=dst, in0=tmp, scalar=-TWO_PI_PARTS[1], in1=dst, op0=ALU.mult, op1=ALU.add))
                v(nc.vector.scalar_tensor_tensor(out=dst, in0=tmp, scalar=-TWO_PI_PARTS[2], in1=dst, op0=ALU.mult, op1=ALU.add))
                nc.vector.scalar_tensor_tensor(out=dst, in0=dst, scalar=-1.0, in1=dst, op0=ALU.mult, op1=ALU.max).then_inc(angle_ready, 1)

            def cumprod(z):
                for j in range(1, 16):
                    v(nc.vector.tensor_tensor(z[:, :, j], z[:, :, j], z[:, :, j - 1], ALU.mult))

            v(nc.vector.memset(half_pi[:], float(np.pi / 2)))
            dve.wait_ge(loaded, 16 * 8)
            flat = lambda z: z[:].rearrange("p t d -> p (t d)")
            layer_norm(a, x1)
            angle(flat(c), flat(a), flat(t))
            dve.wait_ge(sin_done, 1)
            cumprod(c[:].rearrange("p t (h d) -> p (t h) d", d=16))
            v(nc.vector.tensor_tensor(flat(t), flat(a), flat(c), ALU.add))
            layer_norm(a, t)
            v(nc.vector.tensor_tensor(a[:], a[:], bc(G1), ALU.mult))
            v(nc.vector.tensor_tensor(a[:], a[:], bc(B1), ALU.add))
            v(nc.vector.tensor_copy(qt[:], a[:, :, 0:16]))
            fq = lambda z: z[:].rearrange("p t d -> p (t d)")
            qtmp = c[:, 0, :]
            angle(fq(qs), fq(qt), qtmp)
            dve.wait_ge(sin_done, 2)
            cumprod(qs[:])
            nc.vector.tensor_copy(qt[:], qs[:]).then_inc(q_ready, 1)
            v(nc.vector.tensor_tensor(t[:], a[:], bc(FB), ALU.add))
            for g in range(NG):
                dve.wait_ge(qt_filled, g + 1)
                nc.vector.tensor_copy(qT[:], ps_q[:]).then_inc(qt_copied, 1)
                for j in range(GT):
                    i = g * GT + j
                    dve.wait_ge(f_filled, i + 1)
                    nc.vector.tensor_tensor(c[:, i, :], ps_f[:, i % 2, 0:D], t[:, i, :], ALU.add).then_inc(f_added, 1)
            dve.wait_ge(f_added, NT)
            layer_norm(a, c)
            v(nc.vector.tensor_tensor(a[:], a[:], bc(G2), ALU.mult))
            v(nc.vector.tensor_tensor(a[:], a[:], bc(B2), ALU.add))
            v(nc.vector.tensor_tensor(x1[:], x1[:], a[:], ALU.add))
            nc.vector.memset(tiny[:], 0.0).then_inc(x2_ready, 1)
            layer_norm(a, x1)
            v(nc.vector.memset(tiny[:], 0.0))
            nc.vector.memset(tiny[:], 0.0).then_inc(x3_ready, 1)
            for i in range(NT):
                dve.wait_ge(xt_filled, i + 1)
                if i >= 2:
                    dve.wait_ge(l_filled, i - 1)
                nc.vector.tensor_copy(xT[:, i % 2], ps_x[:, i % 2, 0:NC * P].rearrange("p (k t) -> p k t", k=NC)).then_inc(xt_copied, 1)
            dve.wait_ge(l_filled, NT)
            bt = lambda z, n=E: z.unsqueeze(2).to_broadcast([P, NT, n])
            v(nc.vector.tensor_tensor(lg[:], ps_l[:, 0:NT * E].rearrange("p (t e) -> p t e", e=E), rb_sb[:].unsqueeze(1).to_broadcast([P, NT, E]), ALU.add))
            v(nc.vector.tensor_reduce(tiny[:], lg[:], AX.X, ALU.max))
            nc.vector.tensor_tensor(lg[:], lg[:], bt(tiny[:]), ALU.subtract).then_inc(exp_in, 1)
            dve.wait_ge(exp_done, 1)
            v(nc.vector.tensor_reduce(tiny[:], pr[:], AX.X, ALU.add))
            v(nc.vector.reciprocal(tiny[:], tiny[:]))
            v(nc.vector.tensor_tensor(pr[:], pr[:], bt(tiny[:]), ALU.mult))
            for e in range(E):
                if e < E - 1:
                    ch(nc.vector.tensor_tensor(cmp[:, :, e + 1:], pr[:, :, e + 1:], bt(pr[:, :, e], E - 1 - e), ALU.is_gt))
                if e > 0:
                    ch(nc.vector.tensor_tensor(cmp[:, :, 0:e], pr[:, :, 0:e], bt(pr[:, :, e], e), ALU.is_ge))
                v(nc.vector.memset(cmp[:, :, e:e + 1], 0.0))
                v(nc.vector.tensor_reduce(rank[:, :, e], cmp[:], AX.X, ALU.add))
            v(nc.vector.tensor_scalar(rank[:], rank[:], 1.5, None, ALU.is_lt))
            v(nc.vector.tensor_tensor(pr[:], pr[:], rank[:], ALU.mult))
            v(nc.vector.tensor_reduce(tiny[:], pr[:], AX.X, ALU.add))
            v(nc.vector.reciprocal(tiny[:], tiny[:]))
            v(nc.vector.memset(mix[:, :, 0:1], 1.0))
            v(nc.vector.tensor_tensor(mix[:, :, 1:], pr[:], bt(tiny[:]), ALU.mult))
            nc.vector.memset(tiny[:], 0.0).then_inc(mix_ready, 1)

        @block.scalar
        def _(act):
            flat = lambda z: z[:].rearrange("p t d -> p (t d)")
            act.wait_ge(angle_ready, 1)
            nc.scalar.activation(flat(c), flat(c), ACT.Sin, bias=half_pi[:, 0:1], scale=-1.0).then_inc(sin_done, 1)
            act.wait_ge(angle_ready, 2)
            nc.scalar.activation(flat(qs), flat(qs), ACT.Sin, bias=half_pi[:, 0:1], scale=-1.0).then_inc(sin_done, 1)
            for g in range(NG):
                if g > 0:
                    act.wait_ge(f_filled, GT * g)
                for j in range(FC):
                    i = g * FC + j
                    act.wait_ge(h_filled, i + 1)
                    nc.scalar.activation(hT[:, j, :], ps_h[:, i % 2, :], ACT.Relu, bias=b1_sb[:, j:j + 1]).then_inc(h_copied, 1)
            act.wait_ge(exp_in, 1)
            nc.scalar.activation(pr[:], lg[:], ACT.Exp).then_inc(exp_done, 1)

        @block.tensor
        def _(pe):
            pe.wait_ge(loaded, 16 * 8)
            pe.wait_ge(q_ready, 1)
            for g in range(NG):
                if g > 0:
                    pe.wait_ge(qt_copied, g)
                for j in range(GT):
                    mm = nc.tensor.transpose(ps_q[:, j * P:(j + 1) * P], qt[:, g * GT + j, :], id_sb[:])
                mm.then_inc(qt_filled, 1)
                pe.wait_ge(qt_copied, g + 1)
                for j in range(FC):
                    i = g * FC + j
                    if i >= 2:
                        pe.wait_ge(h_copied, i - 1)
                    nc.tensor.matmul(ps_h[:, i % 2, :], w1_sb[:, j * P:(j + 1) * P], qT[:], start=True, stop=True).then_inc(h_filled, 1)
                pe.wait_ge(h_copied, FC * (g + 1))
                for j in range(GT):
                    i = g * GT + j
                    if i >= 2:
                        pe.wait_ge(f_added, i - 1)
                    for m in range(FC):
                        mm = nc.tensor.matmul(ps_f[:, i % 2, 0:D], hT[:, m, j * P:(j + 1) * P], w2_sb[:, m, :], start=(m == 0), stop=(m == FC - 1))
                    mm.then_inc(f_filled, 1)
            pe.wait_ge(x3_ready, 1)
            for i in range(NT):
                if i >= 2:
                    pe.wait_ge(xt_copied, i - 1)
                for k in range(NC):
                    mm = nc.tensor.transpose(ps_x[:, i % 2, k * P:(k + 1) * P], a[:, i, k * P:(k + 1) * P], id_sb[:])
                mm.then_inc(xt_filled, 1)
                pe.wait_ge(xt_copied, i + 1)
                for k in range(NC):
                    mm = nc.tensor.matmul(ps_l[:, i * E:(i + 1) * E], xT[:, i % 2, k, :], wr_sb[:, k, :], start=(k == 0), stop=(k == NC - 1))
                mm.then_inc(l_filled, 1)


def experts(nc, x2_scr, x3_scr, mix_scr, wg, wu, wd, ident, out):
    with ExitStack() as ctx:
        sb = lambda n, s, d=F32: ctx.enter_context(nc.sbuf_tensor(n, s, d))
        ps = lambda n, s: ctx.enter_context(nc.psum_tensor(n, s, F32))
        sem = lambda n: ctx.enter_context(nc.semaphore(n))
        IP = EC * P
        tick = sb("e_tick", [P, 1])
        ticked = sem("e_tk")
        acc, xr, mix, id_sb = sb("e_acc", [P, NT, D]), sb("e_x", [P, D]), sb("e_mix", [P, NT, NEXP]), sb("e_id", [P, P])
        x_hi, x_lo = sb("e_xhi", [P, NC, TOK], F32R), sb("e_xlo", [P, NC, TOK], F32R)
        g_raw, u_raw, d_raw = sb("e_gr", [P, NC, IP]), sb("e_ur", [P, NC, IP]), sb("e_dr", [P, EC, D])
        g_hi, g_lo, u_hi, u_lo = (sb(f"e_{n}", [P, NC, IP], F32R) for n in ("gh", "gl", "uh", "ul"))
        d_hi, d_lo = (sb(f"e_{n}", [P, EC, D], F32R) for n in ("dh", "dl"))
        act_g, h = sb("e_sg", [P, 2, 512]), sb("e_h", [P, 2, 512])
        h_hi, h_lo = sb("e_hh", [P, EC, 512], F32R), sb("e_hl", [P, EC, 512], F32R)
        ps_g, ps_u, ps_y, ps_x = ps("e_psg", [P, 2, 512]), ps("e_psu", [P, 2, 512]), ps("e_psy", [P, 2, 512]), ps("e_psx", [P, 2, 512])
        loaded, x_loaded, w_loaded, stored = sem("e_ld"), sem("e_xl"), sem("e_wl"), sem("e_st")
        xt_filled, x_split, w_hi_done, w_split = sem("e_xf"), sem("e_xs"), sem("e_wh"), sem("e_ws")
        g_filled, g_done, h_done, h_hi_done, h_split = sem("e_gf"), sem("e_gd"), sem("e_hd"), sem("e_hhd"), sem("e_hs")
        y_filled, y_added = sem("e_yf"), sem("e_ya")
        block = ctx.enter_context(nc.Block())
        PER = NG * EC
        WG = 3

        @block.sync
        def _(sp):
            sp.dma_start(id_sb[:], ident).then_inc(loaded, 16)
            sp.dma_start(mix[:], mix_scr).then_inc(loaded, 16)
            sp.dma_start(acc[:], x2_scr.rearrange("t p d -> p t d")).then_inc(loaded, 16)
            for t in range(NT):
                if t > 0:
                    sp.wait_ge(xt_filled, t)
                sp.dma_start(xr[:], x3_scr[t]).then_inc(x_loaded, 16)

            def load(e):
                for dst, src in ((g_raw, wg), (u_raw, wu), (d_raw, wd)):
                    sp.dma_start(dst[:], src[bass.ds(e, 1)].rearrange("a p k i -> p (a k) i")).then_inc(w_loaded, 16)

            load(0)
            with sp.Fori(1, NEXP) as e:
                sp.wait_ge(w_split, WG * e)
                load(e)
            sp.wait_ge(y_added, NEXP * NT)
            sp.dma_start(out.rearrange("t p d -> p t d"), acc[:]).then_inc(stored, 16)
            sp.wait_ge(stored, 16)

        @block.gpsimd
        def _(pool):
            def split(e):
                pool.wait_ge(w_loaded, 16 * WG * (e + 1))
                if not isinstance(e, int) or e > 0:
                    pool.wait_ge(y_filled, NT * e)
                nc.gpsimd.tensor_tensor(out=tick[:], in0=tick[:], in1=tick[:], op=ALU.mult).then_inc(ticked, 1)
                for raw_w, hi in ((g_raw, g_hi), (u_raw, u_hi), (d_raw, d_hi)):
                    nc.gpsimd.tensor_copy(hi[:], raw_w[:]).then_inc(w_hi_done, 1)
                for i, (raw_w, hi, lo) in enumerate(((g_raw, g_hi, g_lo), (u_raw, u_hi, u_lo), (d_raw, d_hi, d_lo))):
                    pool.wait_ge(w_hi_done, WG * e + i + 1)
                    nc.gpsimd.tensor_tensor(out=lo[:], in0=raw_w[:], in1=hi[:].bitcast(F32), op=ALU.subtract).then_inc(w_split, 1)

            nc.gpsimd.memset(tick[:], 0.0).then_inc(ticked, 1)
            pool.wait_ge(ticked, 1)
            split(0)
            with pool.Fori(1, NEXP) as e:
                split(e)

        @block.vector
        def _(dve):
            dve.wait_ge(loaded, 48)
            for t in range(NT):
                dve.wait_ge(xt_filled, t + 1)
                src = ps_x[:, t % 2, 0:NC * P].rearrange("p (k t) -> p k t", k=NC)
                hi = x_hi[:, :, t * P:(t + 1) * P]
                nc.vector.tensor_copy(hi, src).then_inc(x_split, 1)
                dve.wait_ge(x_split, 2 * t + 1)
                nc.vector.tensor_tensor(x_lo[:, :, t * P:(t + 1) * P], src, hi.bitcast(F32), ALU.subtract).then_inc(x_split, 1)

            def body(e, first):
                for g in range(NG):
                    for c in range(EC):
                        i = PER * e + EC * g + c
                        dve.wait_ge(g_done, i + 1)
                        if c == 0 and not (first and g == 0):
                            dve.wait_ge(y_filled, NT * e + GT * g)
                        nc.vector.tensor_tensor(h[:, c % 2, :], ps_u[:, c % 2, :], act_g[:, c % 2, :], ALU.mult).then_inc(h_done, 1)
                        dve.wait_ge(h_done, i + 1)
                        nc.vector.tensor_copy(h_hi[:, c, :], h[:, c % 2, :]).then_inc(h_hi_done, 1)
                        dve.wait_ge(h_hi_done, i + 1)
                        nc.vector.tensor_tensor(h_lo[:, c, :], h[:, c % 2, :], h_hi[:, c, :].bitcast(F32), ALU.subtract).then_inc(h_split, 1)
                    for j in range(GT):
                        t = GT * g + j
                        dve.wait_ge(y_filled, NT * e + t + 1)
                        nc.vector.scalar_tensor_tensor(out=acc[:, t, :], in0=ps_y[:, t % 2, 0:D], scalar=mix_e(e, t),
                                                       in1=acc[:, t, :], op0=ALU.mult, op1=ALU.add).then_inc(y_added, 1)

            def mix_e(e, t):
                return mix[:, t, bass.ds(e, 1)]

            body(0, True)
            with dve.Fori(1, NEXP) as e:
                body(e, False)

        @block.scalar
        def _(act):
            def body(e):
                for g in range(NG):
                    for c in range(EC):
                        i = PER * e + EC * g + c
                        act.wait_ge(g_filled, i + 1)
                        if not (isinstance(i, int) and i < 2):
                            act.wait_ge(h_done, i - 1)
                        nc.scalar.activation(act_g[:, c % 2, :], ps_g[:, c % 2, :], ACT.Silu).then_inc(g_done, 1)

            body(0)
            with act.Fori(1, NEXP) as e:
                body(e)

        @block.tensor
        def _(pe):
            def three(out, a, b, start, stop):
                nc.tensor.matmul(out, a[0], b[0], start=start, stop=False)
                nc.tensor.matmul(out, a[0], b[1], start=False, stop=False)
                return nc.tensor.matmul(out, a[1], b[0], start=False, stop=stop)

            pe.wait_ge(loaded, 48)
            for t in range(NT):
                pe.wait_ge(x_loaded, 16 * (t + 1))
                if t >= 2:
                    pe.wait_ge(x_split, 2 * (t - 1))
                for k in range(NC):
                    mm = nc.tensor.transpose(ps_x[:, t % 2, k * P:(k + 1) * P], xr[:, k * P:(k + 1) * P], id_sb[:])
                mm.then_inc(xt_filled, 1)
            pe.wait_ge(x_split, 2 * NT)

            def body(e, first):
                pe.wait_ge(w_split, WG * (e + 1))
                for g in range(NG):
                    cols = slice(g * 512, (g + 1) * 512)
                    for c in range(EC):
                        i = PER * e + EC * g + c
                        if not (isinstance(i, int) and i < 2):
                            pe.wait_ge(h_done, i - 1)
                        for bank, w in ((ps_g, (g_hi, g_lo)), (ps_u, (u_hi, u_lo))):
                            for k in range(NC):
                                mm = three(bank[:, c % 2, :], [z[:, k, c * P:(c + 1) * P] for z in w],
                                           [z[:, k, cols] for z in (x_hi, x_lo)], k == 0, k == NC - 1)
                        mm.then_inc(g_filled, 1)
                    pe.wait_ge(h_split, PER * e + EC * (g + 1))
                    for j in range(GT):
                        t = GT * g + j
                        if not (first and t < 2):
                            pe.wait_ge(y_added, NT * e + t - 1)
                        for c in range(EC):
                            mm = three(ps_y[:, t % 2, 0:D], [z[:, c, j * P:(j + 1) * P] for z in (h_hi, h_lo)],
                                       [z[:, c, :] for z in (d_hi, d_lo)], c == 0, c == EC - 1)
                        mm.then_inc(y_filled, 1)

            body(0, True)
            with pe.Fori(1, NEXP) as e:
                body(e, False)


def build(nc, ins, out):
    def scratch(name, shape):
        return nc.dram_tensor(name, shape, F32, kind="Internal").ap()

    q_scr = scratch("q_scr", [2, D, TOK])
    x1_scr, x2_scr, x3_scr = (scratch(n, [NT, P, D]) for n in ("x1_scr", "x2_scr", "x3_scr"))
    mix_scr = scratch("mix_scr", [P, NT, NEXP])
    project_queries(nc, ins["x"], ins["wq"], ins["bq"], ins["ident"], q_scr)
    cross_attention(nc, ins["ctxT"], ins["x"], q_scr, ins["wk"], ins["bk"], ins["wv"], ins["bv"], ins["wp"],
                    ins["rows"], ins["ident"], ins["sel4"], ins["hmask"], x1_scr)
    circuit_ffn(nc, x1_scr, ins["rows"], ins["w1"], ins["b1"], ins["w2"], ins["wr"], ins["rb"], ins["ident"],
                x2_scr, x3_scr, mix_scr)
    experts(nc, x2_scr, x3_scr, mix_scr, ins["wg"], ins["wu"], ins["wd"], ins["ident"], out)


def kernel(**inputs):
    import concourse.bacc as bacc
    from concourse.bass_utils import run_bass_kernel_spmd as run

    a = {k: np.asarray(v) for k, v in inputs.items()}
    chunked = lambda m: np.ascontiguousarray(m.reshape(m.shape[0] // P, P, -1).transpose(1, 0, 2))
    wide = lambda r: np.broadcast_to(r, (P,) + r.shape)
    ctx = a["ctx_1024"]
    ctx = np.concatenate([ctx, np.repeat(ctx[:, -1:], SKP - SK, axis=1)], axis=1)
    heads = lambda v: v.reshape(PAIRS, 2, HD, *v.shape[1:]).swapaxes(0, 1).reshape(2, P, *v.shape[1:])
    pad = EC * P - EI

    def up(shared, routed):
        w = np.concatenate([shared[None], routed]).transpose(0, 2, 1)
        w = np.pad(w, ((0, 0), (0, 0), (0, pad)))
        return w.reshape(NEXP, NC, P, EC * P).transpose(0, 2, 1, 3)

    wd = np.concatenate([a["L0_ffn_sd"][None], a["L0_ffn_rd"]]).transpose(0, 2, 1)
    wd = np.pad(wd, ((0, 0), (0, pad), (0, 0))).reshape(NEXP, EC, P, D).transpose(0, 2, 1, 3)
    data = {
        "x": a["x"].reshape(NT, P, D),
        "ctxT": ctx.transpose(0, 2, 1).reshape(B, NC, P, SKP).transpose(0, 2, 1, 3),
        "wq": chunked(a["L0_xattn_Wq"].T), "bq": a["L0_xattn_bq"].reshape(NC, P).T,
        "wk": chunked(a["L0_xattn_Wk"].T), "bk": a["L0_xattn_bk"].reshape(NC, P).T,
        "wv": chunked(a["L0_xattn_Wv"].T), "bv": heads(a["L0_xattn_bv"]).T,
        "wp": heads(np.ascontiguousarray(a["L0_xattn_Wp"].T)).transpose(1, 0, 2),
        "rows": wide(np.stack([a["L0_xattn_bp"], a["L0_attn_gamma1"], a["L0_attn_beta1"], a["L0_attn_b2"],
                               a["L0_attn_gamma2"], a["L0_attn_beta2"]])),
        "w1": a["L0_attn_w1"].T, "b1": a["L0_attn_b1"].reshape(FC, P).T, "w2": chunked(a["L0_attn_w2"].T),
        "wr": chunked(a["L0_ffn_wr"].T), "rb": wide(a["L0_ffn_rb"]),
        "wg": up(a["L0_ffn_sg"], a["L0_ffn_rg"]), "wu": up(a["L0_ffn_su"], a["L0_ffn_ru"]), "wd": wd,
        "ident": np.eye(P, dtype=np.float32),
        "sel4": np.tile(np.eye(32, dtype=np.float32), (4, 1)),
        "hmask": np.tile(np.repeat(np.eye(2, dtype=np.float32), HD, axis=0), (3, 1)),
    }
    nc = bacc.Bacc("TRN2", target_bir_lowering=False, num_devices=1)
    ins = {}
    for name in data:
        data[name] = np.ascontiguousarray(data[name])
        ins[name] = nc.dram_tensor("in_" + name, data[name].shape, mybir.dt.from_np(data[name].dtype), kind="ExternalInput").ap()
    out = nc.dram_tensor("out", (NT, P, D), F32, kind="ExternalOutput").ap()
    build(nc, ins, out)
    r = run(nc, [{"in_" + k: v for k, v in data.items()}], core_ids=[0])
    return r.results[0]["out"].reshape(B, SQ, D)
```

```python
import numpy as np
from contextlib import ExitStack

import concourse.bass as bass
from concourse import mybir

F32 = mybir.dt.float32
F32R = mybir.dt.float32r
ALU = mybir.AluOpType
ACT = mybir.ActivationFunctionType
AX = mybir.AxisListType

P = 128
B, SQ, D = 32, 64, 256
SK = 1601
H, HD = 16, 16
NC = D // P
PAIRS = H // 2
QK = 4
KQ = 402
SKP = QK * KQ
KLAST = SK - (QK - 1) * KQ
KT = -(-SK // P)
KTL = SK - (KT - 1) * P
TG = -(-KT // 4)
NT = B * SQ // P
KSTEPS = NC * QK
VSTEPS = -(-KT // 2)
STEPS = KSTEPS + VSTEPS
K_ORDER = [("k", i // QK, i % QK) for i in range(KSTEPS)]
STEP_ORDER = [K_ORDER[i // 2] if i % 2 == 0 else ("v", i - 1) for i in range(STEPS)]
PAIR_STEPS = [(None if p == 0 else 2 * p - 1, 2 * p) for p in range(PAIRS)]
HALF = PAIRS // NC
STACK = 3 * 32
PIECES = 2
COPIES = 16 * 3 * HALF
SCALE = float(HD) ** 0.5
EPS = 1e-5
FF = 1024
FC = FF // P
E, EI = 7, 704
EC = -(-EI // P)
NEXP = E + 1
TOK = B * SQ
GT = 4
NG = NT // GT
BR = 256
BJ = BR // P
TOPK = 2
NBLK = (TOPK * TOK + E * (BR - 1)) // BR
TWO_PI_PARTS = (6.28125, 1.93500518798828125e-3, 3.0199159819567e-7)
ROUND = 12582912.0


def rows_keys(t):
    return P if t < KT - 1 else KTL


def project_queries(nc, x, wq, bq, ident, q_scr, xs_scr):
    with ExitStack() as ctx:
        sb = lambda n, s, d=F32: ctx.enter_context(nc.sbuf_tensor(n, s, d))
        sem = lambda n: ctx.enter_context(nc.semaphore(n))
        x_sb = sb("q_x", [P, NT, D])
        wq_sb = sb("q_wq", [P, NC, D])
        bq_sb = sb("q_bq", [P, NC])
        id_sb = sb("q_id", [P, P])
        stats = sb("q_stats", [P, NT, 6])
        mv = sb("q_mv", [P, NT, 2])
        vare = sb("q_vare", [P, NT])
        expo = sb("q_expo", [P, NT])
        rstd = sb("q_rstd", [P, NT])
        xT = sb("q_xT", [P, NC, TOK])
        zero, zeroed, cleared = sb("q_zero", [P, NBLK * BJ, D]), sem("q_zeroed"), sem("q_cleared")
        qT = sb("q_qT", [P, 2, 512])
        q_hi = sb("q_hi", [P, NC, TOK], F32R)
        q_lo = sb("q_lo", [P, NC, TOK], F32R)
        ps_t = ctx.enter_context(nc.psum_tensor("q_pst", [P, 2, 512], F32))
        ps_q = ctx.enter_context(nc.psum_tensor("q_psq", [P, 2, 512], F32))
        w_loaded, x_loaded, stored = sem("q_w_loaded"), sem("q_x_loaded"), sem("q_stored")
        stat_done, aggr_done, var_done, pow_set, pow_done, norm_done = (
            sem("q_stat"), sem("q_aggr"), sem("q_var"), sem("q_pset"), sem("q_pow"), sem("q_norm"))
        t_filled, t_copied, q_filled, q_biased, q_split = (
            sem("q_tf"), sem("q_tc"), sem("q_qf"), sem("q_qb"), sem("q_split"))
        block = ctx.enter_context(nc.Block())

        @block.sync
        def _(sp):
            sp.dma_start(x_sb[:], x.rearrange("t p d -> p t d")).then_inc(x_loaded, 16)
            sp.dma_start(wq_sb[:], wq).then_inc(w_loaded, 16)
            sp.dma_start(bq_sb[:], bq).then_inc(w_loaded, 16)
            sp.dma_start(id_sb[:], ident).then_inc(w_loaded, 16)
            sp.wait_ge(zeroed, 1)
            sp.dma_start(xs_scr.rearrange("(j p) d -> p j d", p=P), zero[:]).then_inc(cleared, 16)
            sp.wait_ge(q_split, 2 * NC * NG)
            sp.dma_start(q_scr[0].rearrange("(m p) t -> p m t", p=P), q_hi[:].bitcast(F32)).then_inc(stored, 16)
            sp.dma_start(q_scr[1].rearrange("(m p) t -> p m t", p=P), q_lo[:].bitcast(F32)).then_inc(stored, 16)
            sp.wait_ge(stored, 32)
            sp.wait_ge(cleared, 16)

        @block.gpsimd
        def _(pool):
            nc.gpsimd.memset(zero[:], 0.0).then_inc(zeroed, 1)
            nc.gpsimd.memset(expo[:], -0.5).then_inc(pow_set, 1)
            pool.wait_ge(pow_set, 1)
            pool.wait_ge(var_done, 1)
            nc.gpsimd.tensor_tensor(out=rstd[:], in0=vare[:], in1=expo[:], op=ALU.pow).then_inc(pow_done, 1)

        @block.vector
        def _(dve):
            dve.wait_ge(x_loaded, 16)
            for t in range(NT):
                nc.vector.bn_stats(out=stats[:, t, :], in_=x_sb[:, t, :]).then_inc(stat_done, 1)
            for t in range(NT):
                dve.wait_ge(stat_done, t + 1)
                nc.vector.bn_aggr(out=mv[:, t, :], in_=stats[:, t, :]).then_inc(aggr_done, 1)
            dve.wait_ge(aggr_done, NT)
            nc.vector.tensor_scalar(vare[:], mv[:, :, 1], EPS, None, ALU.add).then_inc(var_done, 1)
            dve.wait_ge(pow_done, 1)
            for t in range(NT):
                nc.vector.tensor_scalar(x_sb[:, t, :], x_sb[:, t, :], mv[:, t, 0:1], rstd[:, t:t + 1],
                                        ALU.subtract, ALU.mult).then_inc(norm_done, 1)
            for i in range(NC * NG):
                g, m = i // NC, i % NC
                dve.wait_ge(q_filled, i + 1)
                if i >= 2:
                    dve.wait_ge(q_split, 2 * (i - 1))
                nc.vector.tensor_scalar(qT[:, i % 2, :], ps_q[:, i % 2, :], bq_sb[:, m:m + 1], SCALE,
                                        ALU.add, ALU.mult).then_inc(q_biased, 1)
                dve.wait_ge(q_biased, i + 1)
                hi = q_hi[:, m, g * 512:(g + 1) * 512]
                nc.vector.tensor_copy(hi, qT[:, i % 2, :]).then_inc(q_split, 1)
                dve.wait_ge(q_split, 2 * i + 1)
                nc.vector.tensor_tensor(q_lo[:, m, g * 512:(g + 1) * 512], qT[:, i % 2, :], hi.bitcast(F32),
                                        ALU.subtract).then_inc(q_split, 1)

        @block.scalar
        def _(act):
            for i in range(NC * NG):
                act.wait_ge(t_filled, i + 1)
                g, k = i // NC, i % NC
                nc.scalar.copy(xT[:, k, g * 512:(g + 1) * 512], ps_t[:, i % 2, :]).then_inc(t_copied, 1)

        @block.tensor
        def _(pe):
            pe.wait_ge(w_loaded, 48)
            for g in range(NG):
                for k in range(NC):
                    i = g * NC + k
                    pe.wait_ge(norm_done, GT * (g + 1))
                    if i >= 2:
                        pe.wait_ge(t_copied, i - 1)
                    for j in range(GT):
                        mm = nc.tensor.transpose(ps_t[:, i % 2, j * P:(j + 1) * P],
                                                 x_sb[:, GT * g + j, k * P:(k + 1) * P], id_sb[:])
                    mm.then_inc(t_filled, 1)
            for g in range(NG):
                pe.wait_ge(t_copied, NC * (g + 1))
                for m in range(NC):
                    i = g * NC + m
                    if i >= 2:
                        pe.wait_ge(q_biased, i - 1)
                    for k in range(NC):
                        mm = nc.tensor.matmul(ps_q[:, i % 2, :], wq_sb[:, k, m * P:(m + 1) * P],
                                              xT[:, k, g * 512:(g + 1) * 512], start=(k == 0), stop=(k == NC - 1))
                    mm.then_inc(q_filled, 1)


def cross_attention(nc, ctxT, x, q_scr, wk, bk, wv, bv, wp, rows, ident, sel4, hmask, x1_scr):
    with ExitStack() as ctx:
        sb = lambda n, s, d=F32: ctx.enter_context(nc.sbuf_tensor(n, s, d))
        ps = lambda n, s: ctx.enter_context(nc.psum_tensor(n, s, F32))
        sem = lambda n: ctx.enter_context(nc.semaphore(n))
        raw = sb("a_raw", [P, NC, SKP])
        c_hi, c_lo = sb("a_chi", [P, 2, NC, SKP], F32R), sb("a_clo", [P, 2, NC, SKP], F32R)
        k_hi, k_lo = sb("a_khi", [P, SKP], F32R), sb("a_klo", [P, SKP], F32R)
        k_st = sb("a_kst", [STACK, PAIRS, SKP], F32R)
        v_sb = sb("a_v", [P, 2, KT, D])
        probs = sb("a_probs", [P, 2, SKP])
        pT = sb("a_pT", [P, KT, P])
        w_raw = probs[:, 0, 0:2 * NC * D].rearrange("p (w k d) -> p w k d", w=2, k=NC)
        w_hi, w_lo = sb("a_whi", [P, 2, NC, D], F32R), sb("a_wlo", [P, 2, NC, D], F32R)
        bk_sb, bv_sb = sb("a_bk", [P, NC]), sb("a_bv", [P, 2])
        wp_sb = sb("a_wp", [P, 2, D])
        bp_sb = sb("a_bp", [P, D])
        id_sb, sel_sb, hm_sb = sb("a_id", [P, P]), sb("a_sel", [P, 32]), sb("a_hm", [STACK, 2])
        q_sb = sb("a_q", [STACK, PAIRS, SQ])
        bd = sb("a_bd", [STACK, 2, PAIRS, P], F32R)
        o_part = sb("a_op", [P, 2, PAIRS, P])
        tick = sb("a_tick", [P, 1])
        ticked = sem("a_tk")
        nmax = sb("a_nmax", [P, 2, PAIRS])
        esum = sb("a_esum", [P, 2, PAIRS, 2])
        rsum, rinv = sb("a_rsum", [P, PAIRS]), sb("a_rinv", [P, PAIRS])
        o_head = sb("a_oh", [P, PAIRS, HD])
        oT = sb("a_oT", [P, 2, P])
        x_t, y_t, x1_t = sb("a_x", [P, D]), sb("a_y", [P, D]), sb("a_x1", [P, D])
        ps_s, ps_t, ps_o, ps_k = ps("a_pss", [P, QK, 512]), ps("a_pst", [P, 2, 512]), ps("a_pso", [P, 512]), ps("a_psk", [P, 512])

        const_loaded, ctx_loaded, q_loaded, x_loaded = sem("a_cl"), sem("a_ctxl"), sem("a_ql"), sem("a_xl")
        stacked = [[sem(f"a_st{m}{z}") for z in range(PIECES)] for m in range(NC)]
        w_split, ctx_hi_done, ctx_split, bd_ready = sem("a_ws"), sem("a_ch"), sem("a_cs"), sem("a_bd")
        kv_filled, k_hi_done, kv_copied = sem("a_kvf"), sem("a_khd"), sem("a_kvc")
        s_filled, max_ready, probs_ready = sem("a_sf"), sem("a_mr"), sem("a_pr")
        t_filled, t_copied_act, t_copied_dve = sem("a_tf"), sem("a_tca"), sem("a_tcd")
        o_filled, o_copied = sem("a_of"), sem("a_oc")
        sum_filled, sum_step, head_ready, hT_filled, hT_copied = (
            sem("a_suf"), sem("a_sus"), sem("a_hr"), sem("a_htf"), sem("a_htc"))
        y_filled, y_biased, x1_ready, x1_free = sem("a_yf"), sem("a_yb"), sem("a_x1r"), sem("a_x1f")
        block = ctx.enter_context(nc.Block())

        @block.sync
        def _(sp):
            def load_queries(n):
                for i, part in enumerate((0, 0, 1)):
                    src = q_scr[part, :, bass.ds(n * SQ, SQ)].rearrange("(p r) t -> r p t", r=32)
                    sp.dma_start(q_sb[32 * i:32 * i + 32], src).then_inc(q_loaded, 16)

            def stack_keys(n, m):
                for z in range(PIECES):
                    if z == 0 and not (isinstance(n, int) and n == 0):
                        sp.wait_ge(s_filled, PAIRS * n - (PAIRS - HALF) if m == 0 else PAIRS * n)
                    else:
                        sp.wait_ge(kv_copied, STEPS * n + STEP_ORDER.index(("k", m, QK // PIECES * (z + 1) - 1)) + 1)
                    cols = slice(z * SKP // PIECES, (z + 1) * SKP // PIECES)
                    for j in range(HALF):
                        for i, part in enumerate((k_hi, k_lo, k_hi)):
                            sp.dma_start(k_st[32 * i:32 * i + 32, HALF * m + j, cols].bitcast(F32),
                                         part[32 * j:32 * j + 32, cols].bitcast(F32)).then_inc(stacked[m][z], 16)

            sp.dma_start(w_raw[:, 0], wk).then_inc(const_loaded, 16)
            sp.dma_start(w_raw[:, 1], wv).then_inc(const_loaded, 16)
            sp.dma_start(raw[:], ctxT[0]).then_inc(ctx_loaded, 16)
            load_queries(0)
            for dst, src in ((bk_sb[:], bk), (bv_sb[:], bv), (wp_sb[:], wp), (bp_sb[:], rows[:, 0]),
                             (id_sb[:], ident), (sel_sb[:], sel4), (hm_sb[:], hmask)):
                sp.dma_start(dst, src).then_inc(const_loaded, 16)
            sp.wait_ge(ctx_split, 1)
            sp.dma_start(raw[:], ctxT[1]).then_inc(ctx_loaded, 16)
            stack_keys(0, 0)

            def body(it, first, last):
                for b in range(2):
                    n = 2 * it + b
                    stack_keys(n, 1)
                    if not (last and b == 1):
                        sp.wait_ge(bd_ready, n + 1)
                        load_queries(n + 1)
                    if not last:
                        sp.wait_ge(ctx_split, n + 2)
                        sp.dma_start(raw[:], ctxT[bass.ds(n + 2, 1)].rearrange("a p k s -> p (a k) s")).then_inc(ctx_loaded, 16)
                    if b == 0 and not first:
                        sp.dma_start(x_t[:], x[bass.ds(it - 1, 1)].rearrange("a p d -> (a p) d")).then_inc(x_loaded, 16)
                    if not (last and b == 1):
                        stack_keys(n + 1, 0)
                    if b == 0 and not first:
                        sp.wait_ge(x1_ready, it)
                        sp.dma_start(x1_scr[bass.ds(it - 1, 1)].rearrange("a p d -> (a p) d"), x1_t[:]).then_inc(x1_free, 16)

            body(0, True, False)
            with sp.Fori(1, NT - 1) as it:
                body(it, False, False)
            body(NT - 1, False, True)
            sp.wait_ge(x1_ready, NT - 1)
            sp.dma_start(x_t[:], x[NT - 1]).then_inc(x_loaded, 16)
            sp.wait_ge(x1_ready, NT)
            sp.dma_start(x1_scr[NT - 1], x1_t[:]).then_inc(x1_free, 16)
            sp.wait_ge(x1_free, 16 * NT + 1)

        @block.gpsimd
        def _(pool):
            def split_ctx(n, s):
                pool.wait_ge(ctx_loaded, 16 * n + 16)
                nc.gpsimd.tensor_tensor(out=tick[:], in0=tick[:], in1=tick[:], op=ALU.mult).then_inc(ticked, 1)
                nc.gpsimd.tensor_copy(c_hi[:, s], raw[:]).then_inc(ctx_hi_done, 1)
                pool.wait_ge(ctx_hi_done, n + 1)
                nc.gpsimd.tensor_tensor(out=c_lo[:, s], in0=raw[:], in1=c_hi[:, s].bitcast(F32),
                                        op=ALU.subtract).then_inc(ctx_split, 1)

            def spread_queries(n, s):
                pool.wait_ge(q_loaded, 48 * n + 48)
                nc.gpsimd.tensor_tensor(
                    out=bd[:, s].rearrange("r p (h q) -> r p h q", h=2),
                    in0=q_sb[:].unsqueeze(2).to_broadcast([STACK, PAIRS, 2, SQ]),
                    in1=hm_sb[:].unsqueeze(1).unsqueeze(3).to_broadcast([STACK, PAIRS, 2, SQ]),
                    op=ALU.mult).then_inc(bd_ready, 1)

            nc.gpsimd.memset(tick[:], 0.0).then_inc(ticked, 1)
            pool.wait_ge(ticked, 1)
            pool.wait_ge(const_loaded, 16 * 9)
            nc.gpsimd.tensor_copy(w_hi[:], w_raw).then_inc(w_split, 1)
            pool.wait_ge(w_split, 1)
            nc.gpsimd.tensor_tensor(out=w_lo[:], in0=w_raw, in1=w_hi[:].bitcast(F32), op=ALU.subtract).then_inc(w_split, 1)
            split_ctx(0, 0)
            spread_queries(0, 0)
            split_ctx(1, 1)

            def body(it, first, last):
                for b in range(2):
                    n = 2 * it + b
                    if not (last and b == 1):
                        if not (first and b == 0):
                            pool.wait_ge(s_filled, PAIRS * n)
                        spread_queries(n + 1, (b + 1) % 2)
                    if not last:
                        pool.wait_ge(kv_filled, STEPS * (n + 1))
                        split_ctx(n + 2, b)

            body(0, True, False)
            with pool.Fori(1, NT - 1) as it:
                body(it, False, False)
            body(NT - 1, False, True)

        @block.scalar
        def _(act):
            def copy_tiles(g, i):
                act.wait_ge(t_filled, TG * g + i + 1)
                nc.scalar.copy(pT[:, 4 * i:4 * i + 4, :], ps_t[:, i % 2, :].rearrange("p (t q) -> p t q", q=P)).then_inc(t_copied_act, 1)

            def exponentials(g, b, p):
                act.wait_ge(max_ready, g + 1)
                pr = probs[:, p % 2, :].rearrange("p (b k) -> p b k", b=QK)
                bias = nmax[:, b, p:p + 1]
                nc.scalar.activation(pr[:, 0:QK - 1, :], ps_s[:, 0:QK - 1, 0:KQ], ACT.Exp, bias=bias,
                                     accum_out=esum[:, b, p, 0:1])
                nc.scalar.activation(pr[:, QK - 1, 0:KLAST], ps_s[:, QK - 1, 0:KLAST], ACT.Exp, bias=bias,
                                     accum_out=esum[:, b, p, 1:2]).then_inc(probs_ready, 1)

            def copy_out(g, b, p):
                act.wait_ge(o_filled, g + 1)
                nc.scalar.copy(o_part[:, b, p, :], ps_o[:, 0:P]).then_inc(o_copied, 1)

            def body(it, first, last):
                for b in range(2):
                    for p in range(PAIRS):
                        g = PAIRS * (2 * it + b) + p
                        start = first and b == 0 and p == 0
                        if not start:
                            copy_tiles(g - 1, 0)
                            copy_tiles(g - 1, 1)
                        exponentials(g, b, p)
                        if not start:
                            copy_out(g - 1, b if p > 0 else 1 - b, (p - 1) % PAIRS)

            body(0, True, False)
            with act.Fori(1, NT - 1) as it:
                body(it, False, False)
            body(NT - 1, False, True)
            g = PAIRS * B - 1
            copy_tiles(g, 0)
            copy_tiles(g, 1)
            copy_out(g, 1, PAIRS - 1)

        @block.vector
        def _(dve):
            def row_max(g, b, p):
                dve.wait_ge(s_filled, g + 1)
                nc.vector.tensor_reduce(nmax[:, b, p:p + 1], ps_s[:, :, 0:KQ], AX.XY, ALU.max, negate=True).then_inc(max_ready, 1)

            def copy_step(n, slot, s):
                dve.wait_ge(kv_filled, STEPS * n + s + 1)
                kind, *at = STEP_ORDER[s]
                if kind == "k":
                    m, q = at
                    if q % (QK // PIECES) == 0:
                        z = q // (QK // PIECES)
                        if m == 1:
                            dve.wait_ge(stacked[0][z], COPIES * (n + 1))
                        elif not (isinstance(n, int) and n == 0):
                            dve.wait_ge(stacked[1][z], COPIES * n)
                    hi, lo = (t[:, q * KQ:(q + 1) * KQ] for t in (k_hi, k_lo))
                    nc.vector.tensor_scalar(hi, ps_k[:, 0:KQ], bk_sb[:, m:m + 1], None, ALU.add).then_inc(k_hi_done, 1)
                    dve.wait_ge(k_hi_done, KSTEPS * n + QK * m + q + 1)
                    nc.vector.scalar_tensor_tensor(out=lo, in0=ps_k[:, 0:KQ], scalar=bk_sb[:, m:m + 1], in1=hi.bitcast(F32),
                                                   op0=ALU.add, op1=ALU.subtract).then_inc(kv_copied, 1)
                else:
                    t = at[0]
                    if t < KT - 1:
                        nc.vector.tensor_copy(v_sb[:, slot, t:t + 2, :], ps_k[:].rearrange("p (t d) -> p t d", t=2)).then_inc(kv_copied, 1)
                    else:
                        nc.vector.tensor_copy(v_sb[0:KTL, slot, t, :], ps_k[0:KTL, 0:D]).then_inc(kv_copied, 1)

            def copy_tiles(g, i):
                dve.wait_ge(t_filled, TG * g + i + 1)
                if i < TG - 1:
                    nc.vector.tensor_copy(pT[:, 4 * i:4 * i + 4, :], ps_t[:, i % 2, :].rearrange("p (t q) -> p t q", q=P)).then_inc(t_copied_dve, 1)
                else:
                    nc.vector.tensor_copy(pT[0:KTL, KT - 1, :], ps_t[0:KTL, i % 2, 0:P]).then_inc(t_copied_dve, 1)

            def normalise(n, b):
                dve.wait_ge(probs_ready, PAIRS * (n + 1))
                nc.vector.tensor_tensor(rsum[:], esum[:, b, :, 0], esum[:, b, :, 1], ALU.add).then_inc(sum_step, 1)
                dve.wait_ge(sum_step, 2 * n + 1)
                nc.vector.reciprocal(rinv[:], rsum[:]).then_inc(sum_step, 1)
                dve.wait_ge(sum_step, 2 * n + 2)
                dve.wait_ge(sum_filled, n + 1)
                for e in range(2):
                    r = slice(SQ * e, SQ * (e + 1))
                    last = nc.vector.tensor_tensor(
                        o_head[r, :, :], ps_k[r, 0:D].rearrange("p (j e d) -> p j e d", e=2, d=HD)[:, :, e, :],
                        rinv[r, :].unsqueeze(2).to_broadcast([SQ, PAIRS, HD]), ALU.mult)
                last.then_inc(head_ready, 1)

            def copy_heads(n, b):
                dve.wait_ge(hT_filled, n + 1)
                for e in range(2):
                    last = nc.vector.tensor_scalar(oT[:, e, SQ * b:SQ * (b + 1)], ps_k[:, SQ * e:SQ * (e + 1)],
                                                   bv_sb[:, e:e + 1], None, ALU.add)
                last.then_inc(hT_copied, 1)

            def residual(t):
                dve.wait_ge(y_filled, t + 1)
                nc.vector.tensor_tensor(y_t[:], ps_k[:, 0:D], bp_sb[:], ALU.add).then_inc(y_biased, 1)
                dve.wait_ge(y_biased, t + 1)
                dve.wait_ge(x_loaded, 16 * (t + 1))
                dve.wait_ge(x1_free, 16 * t + 1)
                nc.vector.tensor_tensor(x1_t[:], y_t[:], x_t[:], ALU.add).then_inc(x1_ready, 1)

            nc.vector.memset(x1_t[:], 0.0).then_inc(x1_free, 1)
            dve.wait_ge(const_loaded, 16 * 9)
            for s in range(STEPS):
                copy_step(0, 0, s)

            def body(it, first, last):
                for b in range(2):
                    n = 2 * it + b
                    ahead = not (last and b == 1)
                    behind = not (first and b == 0)
                    for p in range(PAIRS):
                        g = PAIRS * n + p
                        row_max(g, b, p)
                        steps = PAIR_STEPS[p] if ahead else (None, None)
                        closing = behind and (p in (1, 3) or (p == 5 and b == 0))
                        if closing and p == 1:
                            normalise(n - 1, 1 - b)
                        elif closing and p == 3:
                            copy_heads(n - 1, 1 - b)
                        elif closing:
                            residual(it - 1)
                        if steps[0] is not None and not closing:
                            copy_step(n + 1, 1 - b, steps[0])
                        if behind or p > 0:
                            copy_tiles(g - 1, 2)
                            copy_tiles(g - 1, 3)
                        if steps[0] is not None and closing:
                            copy_step(n + 1, 1 - b, steps[0])
                        if steps[1] is not None:
                            copy_step(n + 1, 1 - b, steps[1])

            body(0, True, False)
            with dve.Fori(1, NT - 1) as it:
                body(it, False, False)
            body(NT - 1, False, True)
            copy_tiles(PAIRS * B - 1, 2)
            copy_tiles(PAIRS * B - 1, 3)
            normalise(B - 1, 1)
            copy_heads(B - 1, 1)
            residual(NT - 1)

        @block.tensor
        def _(pe):
            def three(out, a, b, start, stop):
                nc.tensor.matmul(out, a[0], b[0], start=start, stop=False)
                nc.tensor.matmul(out, a[0], b[1], start=False, stop=False)
                return nc.tensor.matmul(out, a[1], b[0], start=False, stop=stop)

            def step(n, slot, s, after=None):
                if not isinstance(n, int) or STEPS * n + s > 0:
                    pe.wait_ge(kv_copied, STEPS * n + s)
                kind, *at = STEP_ORDER[s]
                if kind == "k":
                    m, q = at
                    for k in range(NC):
                        mm = three(ps_k[:, 0:KQ], [w[:, 0, k, m * P:(m + 1) * P] for w in (w_hi, w_lo)],
                                   [c[:, slot, k, q * KQ:(q + 1) * KQ] for c in (c_hi, c_lo)], k == 0, k == NC - 1)
                else:
                    for t in range(at[0], min(at[0] + 2, KT)):
                        r = rows_keys(t)
                        for k in range(NC):
                            mm = three(ps_k[0:r, (t % 2) * D:(t % 2 + 1) * D],
                                       [c[:, slot, k, t * P:t * P + r] for c in (c_hi, c_lo)],
                                       [w[:, 1, k, :] for w in (w_hi, w_lo)], k == 0, k == NC - 1)
                mm.then_inc(kv_filled, 1)

            def scores(b, p):
                for q in range(QK):
                    mm = nc.tensor.matmul(ps_s[:, q, 0:KQ], bd[:, b, p, :], k_st[:, p, q * KQ:(q + 1) * KQ], start=True, stop=True)
                mm.then_inc(s_filled, 1)

            def turn(p, i):
                for t in range(4 * i, min(4 * i + 4, KT)):
                    r = rows_keys(t)
                    mm = nc.tensor.transpose(ps_t[0:r, i % 2, (t % 4) * P:(t % 4 + 1) * P],
                                             probs[:, p % 2, t * P:t * P + r], id_sb[:])
                mm.then_inc(t_filled, 1)

            def weigh(b, p, i):
                for t in range(4 * i, min(4 * i + 4, KT)):
                    r, c = rows_keys(t), 32 * (t % 4)
                    mm = nc.tensor.matmul(ps_o[c:c + 32, 0:P], v_sb[0:r, b, t, 32 * p:32 * p + 32], pT[0:r, t, :],
                                          start=(t < 4), stop=(t + 4 >= KT))
                return mm

            def sum_parts(n, b):
                pe.wait_ge(o_copied, PAIRS * (n + 1))
                for p in range(PAIRS):
                    mm = nc.tensor.matmul(ps_k[:, 32 * p:32 * p + 32], o_part[:, b, p, :], sel_sb[:], start=True, stop=True)
                mm.then_inc(sum_filled, 1)

            def turn_heads(n):
                pe.wait_ge(head_ready, n + 1)
                nc.tensor.transpose(ps_k[:, 0:P], o_head[:].rearrange("p j d -> p (j d)"), id_sb[:]).then_inc(hT_filled, 1)

            def project_out(t):
                pe.wait_ge(hT_copied, 2 * t + 2)
                for e in range(2):
                    mm = nc.tensor.matmul(ps_k[:, 0:D], oT[:, e, :], wp_sb[:, e, :], start=(e == 0), stop=(e == 1))
                mm.then_inc(y_filled, 1)

            def slot_tail(g, p, b, n, slot, steps, closing=None, closed=None):
                if g is not None:
                    if not isinstance(g, int) or g > 0:
                        pe.wait_ge(t_copied_dve, 2 * g)
                    turn(p, 0)
                    turn(p, 1)
                if closing is not None:
                    if steps[0] is not None:
                        pe.wait_ge(kv_copied, STEPS * n + steps[0])
                    closing()
                elif steps[0] is not None:
                    step(n, slot, steps[0])
                if g is not None:
                    pe.wait_ge(t_copied_act, 2 * g + 1)
                    if not isinstance(g, int) or g > 0:
                        pe.wait_ge(o_copied, g)
                    weigh(b, p, 0)
                    turn(p, 2)
                    pe.wait_ge(t_copied_act, 2 * g + 2)
                    weigh(b, p, 1)
                    turn(p, 3)
                if closing is not None:
                    if steps[0] is not None:
                        pe.wait_ge(*closed)
                        step(n, slot, steps[0])
                elif steps[1] is not None:
                    step(n, slot, steps[1])
                if g is not None:
                    pe.wait_ge(t_copied_dve, 2 * g + 2)
                    weigh(b, p, 2)
                    weigh(b, p, 3).then_inc(o_filled, 1)
                if closing is not None and steps[1] is not None:
                    step(n, slot, steps[1])

            pe.wait_ge(const_loaded, 16 * 9)
            pe.wait_ge(w_split, 2)
            pe.wait_ge(ctx_split, 1)
            for s in range(STEPS):
                step(0, 0, s)

            def body(it, first, last):
                for b in range(2):
                    n = 2 * it + b
                    ahead = not (last and b == 1)
                    behind = not (first and b == 0)
                    pe.wait_ge(bd_ready, n + 1)
                    if ahead:
                        pe.wait_ge(ctx_split, n + 2)
                    else:
                        pe.wait_ge(kv_copied, STEPS * (n + 1))
                    for p in range(PAIRS):
                        g = PAIRS * n + p
                        if p % HALF == 0:
                            for piece in stacked[p // HALF]:
                                pe.wait_ge(piece, COPIES * (n + 1))
                        if behind or p > 0:
                            pe.wait_ge(probs_ready, g)
                        scores(b, p)
                        before = g - 1 if behind or p > 0 else None
                        steps = PAIR_STEPS[p] if ahead else (None, None)
                        closing = closed = None
                        if behind and p == 1:
                            closing, closed = (lambda: sum_parts(n - 1, 1 - b)), (head_ready, n)
                        elif behind and p == 3:
                            closing, closed = (lambda: turn_heads(n - 1)), (hT_copied, n)
                        elif behind and p == 5 and b == 0:
                            closing, closed = (lambda: project_out(it - 1)), (y_biased, it)
                        slot_tail(before, (p - 1) % PAIRS, b if p > 0 else 1 - b, n + 1, 1 - b, steps, closing, closed)

            body(0, True, False)
            with pe.Fori(1, NT - 1) as it:
                body(it, False, False)
            body(NT - 1, False, True)
            pe.wait_ge(probs_ready, PAIRS * B)
            slot_tail(PAIRS * B - 1, PAIRS - 1, 1, None, 0, (None, None))
            sum_parts(B - 1, 1)
            turn_heads(B - 1)
            project_out(NT - 1)


class Chain:

    def __init__(self, eng, sem):
        self.eng, self.sem, self.n = eng, sem, 0

    def __call__(self, ins):
        self.n += 1
        ins.then_inc(self.sem, 1)
        return self.n

    def wait(self, n=None):
        self.eng.wait_ge(self.sem, self.n if n is None else n)


def circuit_ffn(nc, x1_scr, rows, w1, b1, w2, wr, rb, ident, x2_scr, x3_scr, top_scr, wgt_scr):
    with ExitStack() as ctx:
        sb = lambda n, s, d=F32: ctx.enter_context(nc.sbuf_tensor(n, s, d))
        ps = lambda n, s: ctx.enter_context(nc.psum_tensor(n, s, F32))
        sem = lambda n: ctx.enter_context(nc.semaphore(n))
        x1, a, t, c = (sb(f"f_{n}", [P, NT, D]) for n in ("x1", "a", "t", "c"))
        row = sb("f_rows", [P, 6, D])
        stats, mv, vare, expo, rstd = sb("f_st", [P, NT, 6]), sb("f_mv", [P, NT, 2]), sb("f_va", [P, NT]), sb("f_ex", [P, NT]), sb("f_rs", [P, NT])
        half_pi = sb("f_hp", [P, 1])
        qs = sb("f_qs", [P, NT, 16])
        qt = sb("f_qt", [P, NT, 16])
        w1_sb, b1_sb, w2_sb = sb("f_w1", [16, FF]), sb("f_b1", [P, FC]), sb("f_w2", [P, FC, D])
        wr_sb, rb_sb, id_sb = sb("f_wr", [P, NC, E]), sb("f_rb", [P, E]), sb("f_id", [P, P])
        qT, hT = sb("f_qT", [16, 512]), sb("f_hT", [P, FC, 512])
        xT = sb("f_xT", [P, 2, NC, P])
        lg, pr, rank, cmp, tiny = sb("f_lg", [P, NT, E]), sb("f_pr", [P, NT, E]), sb("f_rk", [P, NT, E]), sb("f_cmp", [P, NT, E]), sb("f_ty", [P, NT])
        top, wgt = sb("f_top", [P, TOPK, NT, E]), sb("f_wgt", [P, TOPK, NT])
        ps_q, ps_h, ps_f, ps_x, ps_l = ps("f_psq", [16, 512]), ps("f_psh", [P, 2, 512]), ps("f_psf", [P, 2, 512]), ps("f_psx", [P, 2, 512]), ps("f_psl", [P, 512])
        loaded, stored = sem("f_ld"), sem("f_st")
        dv, var_done, pow_done, angle_ready, sin_done, x3_ready = sem("f_dv"), sem("f_vd"), sem("f_pd"), sem("f_ar"), sem("f_sd"), sem("f_x3r")
        qt_filled, qt_copied, h_filled, h_copied, f_filled, f_added = sem("f_qf"), sem("f_qc"), sem("f_hf"), sem("f_hc"), sem("f_ff"), sem("f_fa")
        xt_filled, xt_copied, l_filled, exp_in, exp_done, mix_ready = sem("f_xf"), sem("f_xc"), sem("f_lf"), sem("f_ei"), sem("f_ed"), sem("f_mr")
        q_ready, x2_ready = sem("f_qr"), sem("f_x2r")
        block = ctx.enter_context(nc.Block())
        G1, B1, FB, G2, B2 = 1, 2, 3, 4, 5

        @block.sync
        def _(sp):
            for dst, src in ((x1[:], x1_scr.rearrange("t p d -> p t d")), (row[:], rows), (w1_sb[:], w1), (b1_sb[:], b1),
                             (w2_sb[:], w2), (wr_sb[:], wr), (rb_sb[:], rb), (id_sb[:], ident)):
                sp.dma_start(dst, src).then_inc(loaded, 16)
            sp.wait_ge(x2_ready, 1)
            sp.dma_start(x2_scr.rearrange("t p d -> p t d"), x1[:]).then_inc(stored, 16)
            sp.wait_ge(x3_ready, 1)
            sp.dma_start(x3_scr.rearrange("t p d -> p t d"), a[:]).then_inc(stored, 16)
            sp.wait_ge(mix_ready, 1)
            sp.dma_start(top_scr, top[:]).then_inc(stored, 16)
            sp.dma_start(wgt_scr, wgt[:]).then_inc(stored, 16)
            sp.wait_ge(stored, 64)

        @block.gpsimd
        def _(pool):
            nc.gpsimd.memset(expo[:], -0.5).then_inc(pow_done, 1)
            pool.wait_ge(pow_done, 1)
            for i in range(4):
                pool.wait_ge(var_done, i + 1)
                nc.gpsimd.tensor_tensor(out=rstd[:], in0=vare[:], in1=expo[:], op=ALU.pow).then_inc(pow_done, 1)

        @block.vector
        def _(dve):
            ch = Chain(dve, dv)
            norms = [0]

            def v(ins):
                ch(ins)
                ch.wait()

            def bc(r, n=NT):
                return row[:, r, :].unsqueeze(1).to_broadcast([P, n, D])

            def layer_norm(dst, src):
                for i in range(NT):
                    ch(nc.vector.bn_stats(out=stats[:, i, :], in_=src[:, i, :]))
                ch.wait()
                for i in range(NT):
                    ch(nc.vector.bn_aggr(out=mv[:, i, :], in_=stats[:, i, :]))
                ch.wait()
                nc.vector.tensor_scalar(vare[:], mv[:, :, 1], EPS, None, ALU.add).then_inc(var_done, 1)
                norms[0] += 1
                dve.wait_ge(pow_done, norms[0] + 1)
                for i in range(NT):
                    ch(nc.vector.tensor_scalar(dst[:, i, :], src[:, i, :], mv[:, i, 0:1], rstd[:, i:i + 1], ALU.subtract, ALU.mult))
                ch.wait()

            def angle(dst, src, tmp):
                v(nc.vector.tensor_scalar(tmp, src, 1.0 / (2.0 * np.pi), ROUND, ALU.mult, ALU.add))
                v(nc.vector.tensor_scalar(tmp, tmp, ROUND, None, ALU.subtract))
                v(nc.vector.scalar_tensor_tensor(out=dst, in0=tmp, scalar=-TWO_PI_PARTS[0], in1=src, op0=ALU.mult, op1=ALU.add))
                v(nc.vector.scalar_tensor_tensor(out=dst, in0=tmp, scalar=-TWO_PI_PARTS[1], in1=dst, op0=ALU.mult, op1=ALU.add))
                v(nc.vector.scalar_tensor_tensor(out=dst, in0=tmp, scalar=-TWO_PI_PARTS[2], in1=dst, op0=ALU.mult, op1=ALU.add))
                nc.vector.scalar_tensor_tensor(out=dst, in0=dst, scalar=-1.0, in1=dst, op0=ALU.mult, op1=ALU.max).then_inc(angle_ready, 1)

            def cumprod(z):
                for j in range(1, 16):
                    v(nc.vector.tensor_tensor(z[:, :, j], z[:, :, j], z[:, :, j - 1], ALU.mult))

            v(nc.vector.memset(half_pi[:], float(np.pi / 2)))
            dve.wait_ge(loaded, 16 * 8)
            flat = lambda z: z[:].rearrange("p t d -> p (t d)")
            layer_norm(a, x1)
            angle(flat(c), flat(a), flat(t))
            dve.wait_ge(sin_done, 1)
            cumprod(c[:].rearrange("p t (h d) -> p (t h) d", d=16))
            v(nc.vector.tensor_tensor(flat(t), flat(a), flat(c), ALU.add))
            layer_norm(a, t)
            v(nc.vector.tensor_tensor(a[:], a[:], bc(G1), ALU.mult))
            v(nc.vector.tensor_tensor(a[:], a[:], bc(B1), ALU.add))
            v(nc.vector.tensor_copy(qt[:], a[:, :, 0:16]))
            fq = lambda z: z[:].rearrange("p t d -> p (t d)")
            qtmp = c[:, 0, :]
            angle(fq(qs), fq(qt), qtmp)
            dve.wait_ge(sin_done, 2)
            cumprod(qs[:])
            nc.vector.tensor_copy(qt[:], qs[:]).then_inc(q_ready, 1)
            v(nc.vector.tensor_tensor(t[:], a[:], bc(FB), ALU.add))
            for g in range(NG):
                dve.wait_ge(qt_filled, g + 1)
                nc.vector.tensor_copy(qT[:], ps_q[:]).then_inc(qt_copied, 1)
                for j in range(GT):
                    i = g * GT + j
                    dve.wait_ge(f_filled, i + 1)
                    nc.vector.tensor_tensor(c[:, i, :], ps_f[:, i % 2, 0:D], t[:, i, :], ALU.add).then_inc(f_added, 1)
            dve.wait_ge(f_added, NT)
            layer_norm(a, c)
            v(nc.vector.tensor_tensor(a[:], a[:], bc(G2), ALU.mult))
            v(nc.vector.tensor_tensor(a[:], a[:], bc(B2), ALU.add))
            v(nc.vector.tensor_tensor(x1[:], x1[:], a[:], ALU.add))
            nc.vector.memset(tiny[:], 0.0).then_inc(x2_ready, 1)
            layer_norm(a, x1)
            v(nc.vector.memset(tiny[:], 0.0))
            nc.vector.memset(tiny[:], 0.0).then_inc(x3_ready, 1)
            for i in range(NT):
                dve.wait_ge(xt_filled, i + 1)
                if i >= 2:
                    dve.wait_ge(l_filled, i - 1)
                nc.vector.tensor_copy(xT[:, i % 2], ps_x[:, i % 2, 0:NC * P].rearrange("p (k t) -> p k t", k=NC)).then_inc(xt_copied, 1)
            dve.wait_ge(l_filled, NT)
            bt = lambda z, n=E: z.unsqueeze(2).to_broadcast([P, NT, n])
            v(nc.vector.tensor_tensor(lg[:], ps_l[:, 0:NT * E].rearrange("p (t e) -> p t e", e=E), rb_sb[:].unsqueeze(1).to_broadcast([P, NT, E]), ALU.add))
            v(nc.vector.tensor_reduce(tiny[:], lg[:], AX.X, ALU.max))
            nc.vector.tensor_tensor(lg[:], lg[:], bt(tiny[:]), ALU.subtract).then_inc(exp_in, 1)
            dve.wait_ge(exp_done, 1)
            v(nc.vector.tensor_reduce(tiny[:], pr[:], AX.X, ALU.add))
            v(nc.vector.reciprocal(tiny[:], tiny[:]))
            v(nc.vector.tensor_tensor(pr[:], pr[:], bt(tiny[:]), ALU.mult))
            for e in range(E):
                if e < E - 1:
                    ch(nc.vector.tensor_tensor(cmp[:, :, e + 1:], pr[:, :, e + 1:], bt(pr[:, :, e], E - 1 - e), ALU.is_gt))
                if e > 0:
                    ch(nc.vector.tensor_tensor(cmp[:, :, 0:e], pr[:, :, 0:e], bt(pr[:, :, e], e), ALU.is_ge))
                v(nc.vector.memset(cmp[:, :, e:e + 1], 0.0))
                v(nc.vector.tensor_reduce(rank[:, :, e], cmp[:], AX.X, ALU.add))
            v(nc.vector.tensor_scalar(top[:, 0], rank[:], 0.5, None, ALU.is_lt))
            v(nc.vector.tensor_scalar(rank[:], rank[:], 1.5, None, ALU.is_lt))
            v(nc.vector.tensor_tensor(top[:, 1], rank[:], top[:, 0], ALU.subtract))
            for k in range(TOPK):
                v(nc.vector.tensor_tensor(cmp[:], pr[:], top[:, k], ALU.mult))
                v(nc.vector.tensor_reduce(wgt[:, k], cmp[:], AX.X, ALU.add))
            v(nc.vector.tensor_tensor(tiny[:], wgt[:, 0], wgt[:, 1], ALU.add))
            v(nc.vector.reciprocal(tiny[:], tiny[:]))
            v(nc.vector.tensor_tensor(wgt[:], wgt[:], tiny[:].unsqueeze(1).to_broadcast([P, TOPK, NT]), ALU.mult))
            nc.vector.memset(tiny[:], 0.0).then_inc(mix_ready, 1)

        @block.scalar
        def _(act):
            flat = lambda z: z[:].rearrange("p t d -> p (t d)")
            act.wait_ge(angle_ready, 1)
            nc.scalar.activation(flat(c), flat(c), ACT.Sin, bias=half_pi[:, 0:1], scale=-1.0).then_inc(sin_done, 1)
            act.wait_ge(angle_ready, 2)
            nc.scalar.activation(flat(qs), flat(qs), ACT.Sin, bias=half_pi[:, 0:1], scale=-1.0).then_inc(sin_done, 1)
            for g in range(NG):
                if g > 0:
                    act.wait_ge(f_filled, GT * g)
                for j in range(FC):
                    i = g * FC + j
                    act.wait_ge(h_filled, i + 1)
                    nc.scalar.activation(hT[:, j, :], ps_h[:, i % 2, :], ACT.Relu, bias=b1_sb[:, j:j + 1]).then_inc(h_copied, 1)
            act.wait_ge(exp_in, 1)
            nc.scalar.activation(pr[:], lg[:], ACT.Exp).then_inc(exp_done, 1)

        @block.tensor
        def _(pe):
            pe.wait_ge(loaded, 16 * 8)
            pe.wait_ge(q_ready, 1)
            for g in range(NG):
                if g > 0:
                    pe.wait_ge(qt_copied, g)
                for j in range(GT):
                    mm = nc.tensor.transpose(ps_q[:, j * P:(j + 1) * P], qt[:, g * GT + j, :], id_sb[:])
                mm.then_inc(qt_filled, 1)
                pe.wait_ge(qt_copied, g + 1)
                for j in range(FC):
                    i = g * FC + j
                    if i >= 2:
                        pe.wait_ge(h_copied, i - 1)
                    nc.tensor.matmul(ps_h[:, i % 2, :], w1_sb[:, j * P:(j + 1) * P], qT[:], start=True, stop=True).then_inc(h_filled, 1)
                pe.wait_ge(h_copied, FC * (g + 1))
                for j in range(GT):
                    i = g * GT + j
                    if i >= 2:
                        pe.wait_ge(f_added, i - 1)
                    for m in range(FC):
                        mm = nc.tensor.matmul(ps_f[:, i % 2, 0:D], hT[:, m, j * P:(j + 1) * P], w2_sb[:, m, :], start=(m == 0), stop=(m == FC - 1))
                    mm.then_inc(f_filled, 1)
            pe.wait_ge(x3_ready, 1)
            for i in range(NT):
                if i >= 2:
                    pe.wait_ge(xt_copied, i - 1)
                for k in range(NC):
                    mm = nc.tensor.transpose(ps_x[:, i % 2, k * P:(k + 1) * P], a[:, i, k * P:(k + 1) * P], id_sb[:])
                mm.then_inc(xt_filled, 1)
                pe.wait_ge(xt_copied, i + 1)
                for k in range(NC):
                    mm = nc.tensor.matmul(ps_l[:, i * E:(i + 1) * E], xT[:, i % 2, k, :], wr_sb[:, k, :], start=(k == 0), stop=(k == NC - 1))
                mm.then_inc(l_filled, 1)


def experts(nc, x2_scr, x3_scr, top_scr, wgt_scr, xs_scr, ys_scr, wg, wu, wd, ident, tri, blocks, out):
    with ExitStack() as ctx:
        sb = lambda n, s, d=F32: ctx.enter_context(nc.sbuf_tensor(n, s, d))
        ps = lambda n, s: ctx.enter_context(nc.psum_tensor(n, s, F32))
        sem = lambda n: ctx.enter_context(nc.semaphore(n))
        IP = EC * P
        I32 = mybir.dt.int32
        x3, acc, id_sb = sb("e_x3", [P, NT, D]), sb("e_acc", [P, NT, D]), sb("e_id", [P, P])
        x_hi, x_lo = sb("e_xhi", [P, NC, TOK], F32R), sb("e_xlo", [P, NC, TOK], F32R)
        g_w, u_w, d_w = sb("e_gw", [P, 2, NC, IP]), sb("e_uw", [P, 2, NC, IP]), sb("e_dw", [P, 2, EC, D])
        g_hi, g_lo, u_hi, u_lo = (sb(f"e_{n}", [P, NC, IP], F32R) for n in ("gh", "gl", "uh", "ul"))
        d_hi, d_lo = (sb(f"e_{n}", [P, EC, D], F32R) for n in ("dh", "dl"))
        silu, h = sb("e_sg", [P, 2, 512]), sb("e_h", [P, 2, 512])
        h_hi, h_lo = sb("e_hh", [P, EC, 512], F32R), sb("e_hl", [P, EC, 512], F32R)
        hb = sb("e_hb", [P, 2, EC, BR])
        xb, xbT, yb = sb("e_xb", [P, 2, BJ, D]), sb("e_xbT", [P, 2, NC, BR]), sb("e_yb", [P, 2, BJ, D])
        YG = 4
        yg = sb("e_yg", [P, YG, TOPK, D])
        tri_sb, one_sb, blk_sb = sb("e_tri", [P, P]), sb("e_one", [P, P]), sb("e_blk", [P, NBLK])
        top, wgt = sb("e_top", [P, TOPK, NT, E]), sb("e_wgt", [P, TOPK, NT])
        taken, count, place, mine = (sb(f"e_{n}", [P, NT, E]) for n in ("tk", "ct", "pl", "mi"))
        total, nblk, first_blk, last_blk = (sb(f"e_{n}", [P, E]) for n in ("tot", "nb", "fb", "lb"))
        past, idf, ids = sb("e_past", [P, NBLK, E]), sb("e_idf", [P, NBLK]), sb("e_ids", [P, NBLK], I32)
        posf, pos = sb("e_posf", [P, TOPK, NT]), sb("e_pos", [P, TOPK, NT], I32)
        ps_gu, ps_y, ps_x = ps("e_psg", [P, 4, 512]), ps("e_psy", [P, 2, 512]), ps("e_psx", [P, 2, 512])
        loaded, x_loaded, w_loaded, acc_loaded = sem("e_ld"), sem("e_xl"), sem("e_wl"), sem("e_al")
        dv, taken_ready, ranks_filled, plan_ready, scattered = sem("e_dv"), sem("e_tr"), sem("e_rf"), sem("e_pr"), sem("e_sc")
        xt_filled, x_split, w_hi_done, w_split = sem("e_xf"), sem("e_xs"), sem("e_wh"), sem("e_ws")
        gu_filled, silu_done, h_done, h_hi_done, h_split = sem("e_gf"), sem("e_gd"), sem("e_hd"), sem("e_hhd"), sem("e_hs")
        y_filled, y_added = sem("e_yf"), sem("e_ya")
        bw_loaded, bx_loaded, by_stored = ([sem(f"e_{n}{s}") for s in range(2)] for n in ("bw", "bx", "bst"))
        bx_filled, bx_copied, bgu_filled, bsilu_done, bh_done = sem("e_bxf"), sem("e_bxc"), sem("e_bgf"), sem("e_bsd"), sem("e_bhd")
        by_filled, by_copied = sem("e_byf"), sem("e_byc")
        gathered, combined, half_combined, stored = [sem(f"e_ga{s}") for s in range(YG)], sem("e_co"), sem("e_hc"), sem("e_st")
        block = ctx.enter_context(nc.Block())

        @block.sync
        def _(sp):
            sp.dma_start(top[:], top_scr).then_inc(loaded, 16)
            for dst, src in ((wgt, wgt_scr), (tri_sb, tri), (blk_sb, blocks), (id_sb, ident)):
                sp.dma_start(dst[:], src).then_inc(loaded, 16)
            sp.dma_start(x3[:], x3_scr.rearrange("t p d -> p t d")).then_inc(x_loaded, 16)
            for dst, src in ((g_w, wg), (u_w, wu), (d_w, wd)):
                sp.dma_start(dst[:, 0], src[0]).then_inc(w_loaded, 16)
            sp.dma_start(acc[:], x2_scr.rearrange("t p d -> p t d")).then_inc(acc_loaded, 16)

            def load_weights(b, s):
                e = sp.value_load(ids[0:1, b:b + 1] if isinstance(b, int) else ids[0:1, bass.ds(b, 1)], min_val=0, max_val=E)
                for dst, src in ((g_w, wg), (u_w, wu), (d_w, wd)):
                    sp.dma_start(dst[:, s], src[bass.ds(e, 1)].rearrange("a p k i -> p (a k) i")).then_inc(bw_loaded[s], 16)

            def load_rows(b, s):
                sp.dma_start(xb[:, s], xs_scr[bass.ds(b * BR, BR), :].rearrange("(j p) d -> p j d", p=P)).then_inc(bx_loaded[s], 16)

            def store_rows(b, s):
                sp.wait_ge(by_copied, b + 1)
                sp.dma_start(ys_scr[bass.ds(b * BR, BR), :].rearrange("(j p) d -> p j d", p=P), yb[:, s]).then_inc(by_stored[s], 16)

            sp.wait_ge(plan_ready, 1)
            sp.wait_ge(w_split, 3)
            for b in range(2):
                load_weights(b, b)
            sp.wait_ge(scattered, 16 * TOPK * NT)
            for b in range(3):
                if b == 2:
                    sp.wait_ge(bx_filled, 1)
                load_rows(b, b % 2)

            def body(it, last):
                for s in range(2):
                    b = 2 * it + s
                    sp.wait_ge(by_filled, b - 1)
                    load_weights(b, s)
                    if not (last and s == 1):
                        sp.wait_ge(bx_filled, b)
                        load_rows(b + 1, 1 - s)
                    store_rows(b - 2, s)

            with sp.Fori(1, NBLK // 2 - 1) as it:
                body(it, False)
            body(NBLK // 2 - 1, True)
            for b in range(NBLK - 2, NBLK):
                store_rows(b, b % 2)
            for q in range(NG):
                sp.wait_ge(combined, GT * (q + 1))
                sp.dma_start(out[GT * q:GT * (q + 1)].rearrange("t p d -> p t d"), acc[:, GT * q:GT * (q + 1), :]).then_inc(stored, 16)
            sp.wait_ge(stored, 16 * NG)

        @block.gpsimd
        def _(pool):
            pool.wait_ge(w_loaded, 48)
            nc.gpsimd.tensor_copy(g_hi[:], g_w[:, 0]).then_inc(w_hi_done, 1)
            pool.wait_ge(plan_ready, 1)
            pool.wait_ge(x_loaded, 16)
            for t in range(NT):
                for k in range(TOPK):
                    nc.gpsimd.indirect_dma_start(xs_scr, bass.IndirectOffsetOnAxis(pos[:, k, t:t + 1], 0), x3[:, t, :], None).then_inc(scattered, 16)
            for s in range(2):
                pool.wait_ge(by_stored[s], 16 * (NBLK // 2))
            for t in range(NT):
                if t >= YG:
                    pool.wait_ge(combined, t - YG + 1)
                for k in range(TOPK):
                    nc.gpsimd.indirect_dma_start(yg[:, t % YG, k, :], None, ys_scr, bass.IndirectOffsetOnAxis(pos[:, k, t:t + 1], 0)).then_inc(gathered[t % YG], 16)

        @block.vector
        def _(dve):
            ch = Chain(dve, dv)

            def v(ins):
                ch(ins)
                ch.wait()

            v(nc.vector.memset(one_sb[:], 1.0))
            dve.wait_ge(loaded, 16 * 5)
            nc.vector.tensor_tensor(taken[:], top[:, 0], top[:, 1], ALU.add).then_inc(taken_ready, 1)
            dve.wait_ge(ranks_filled, 1)
            r = NT * E
            v(nc.vector.tensor_copy(count[:].rearrange("p t e -> p (t e)"), ps_y[:, 1, 0:r]))
            v(nc.vector.tensor_reduce(total[:], count[:].rearrange("p t e -> p e t"), AX.X, ALU.add))
            v(nc.vector.tensor_scalar(nblk[:], total[:], 1.0 / BR, (BR - 1.0) / BR - 0.5 + 0.5 / BR, ALU.mult, ALU.add))
            v(nc.vector.tensor_scalar(nblk[:], nblk[:], ROUND, None, ALU.add))
            v(nc.vector.tensor_scalar(nblk[:], nblk[:], ROUND, None, ALU.subtract))
            v(nc.vector.memset(first_blk[:, 0:1], 0.0))
            for e in range(1, E):
                v(nc.vector.tensor_tensor(first_blk[:, e:e + 1], first_blk[:, e - 1:e], nblk[:, e - 1:e], ALU.add))
            v(nc.vector.tensor_tensor(last_blk[:], first_blk[:], nblk[:], ALU.add))
            v(nc.vector.tensor_tensor(past[:], last_blk[:].unsqueeze(1).to_broadcast([P, NBLK, E]),
                                      blk_sb[:].unsqueeze(2).to_broadcast([P, NBLK, E]), ALU.is_le))
            v(nc.vector.tensor_reduce(idf[:], past[:], AX.X, ALU.add))
            v(nc.vector.tensor_scalar(idf[:], idf[:], E - 1.0, 1.0, ALU.min, ALU.add))
            v(nc.vector.tensor_copy(ids[:], idf[:]))
            v(nc.vector.tensor_scalar(place[:, 0, :], first_blk[:], float(BR), None, ALU.mult))
            for t in range(1, NT):
                v(nc.vector.tensor_tensor(place[:, t, :], place[:, t - 1, :], count[:, t - 1, :], ALU.add))
            v(nc.vector.tensor_tensor(place[:].rearrange("p t e -> p (t e)"), place[:].rearrange("p t e -> p (t e)"), ps_y[:, 0, 0:r], ALU.add))
            for k in range(TOPK):
                v(nc.vector.tensor_tensor(mine[:], place[:], top[:, k], ALU.mult))
                v(nc.vector.tensor_reduce(posf[:, k], mine[:], AX.X, ALU.add))
            nc.vector.tensor_copy(pos[:], posf[:]).then_inc(plan_ready, 1)

            for t in range(NT):
                dve.wait_ge(xt_filled, t + 1)
                src = ps_x[:, t % 2, 0:NC * P].rearrange("p (k t) -> p k t", k=NC)
                hi = x_hi[:, :, t * P:(t + 1) * P]
                nc.vector.tensor_copy(hi, src).then_inc(x_split, 1)
                dve.wait_ge(x_split, 2 * t + 1)
                nc.vector.tensor_tensor(x_lo[:, :, t * P:(t + 1) * P], src, hi.bitcast(F32), ALU.subtract).then_inc(x_split, 1)
            for i, (raw_w, hi, lo) in enumerate(((g_w, g_hi, g_lo), (u_w, u_hi, u_lo), (d_w, d_hi, d_lo))):
                dve.wait_ge(w_hi_done, 3)
                nc.vector.tensor_tensor(lo[:], raw_w[:, 0], hi[:].bitcast(F32), ALU.subtract).then_inc(w_split, 1)

            dve.wait_ge(acc_loaded, 16)
            for g in range(NG):
                for c in range(EC):
                    i = EC * g + c
                    dve.wait_ge(silu_done, i + 1)
                    if c == 0 and g > 0:
                        dve.wait_ge(y_filled, GT * g)
                    nc.vector.tensor_tensor(h[:, c % 2, :], ps_gu[:, 2 * (c % 2) + 1, :], silu[:, c % 2, :], ALU.mult).then_inc(h_done, 1)
                    dve.wait_ge(h_done, i + 1)
                    nc.vector.tensor_copy(h_hi[:, c, :], h[:, c % 2, :]).then_inc(h_hi_done, 1)
                    dve.wait_ge(h_hi_done, i + 1)
                    nc.vector.tensor_tensor(h_lo[:, c, :], h[:, c % 2, :], h_hi[:, c, :].bitcast(F32), ALU.subtract).then_inc(h_split, 1)
                for j in range(GT):
                    t = GT * g + j
                    dve.wait_ge(y_filled, t + 1)
                    nc.vector.tensor_tensor(acc[:, t, :], ps_y[:, t % 2, 0:D], acc[:, t, :], ALU.add).then_inc(y_added, 1)

            def gate(b, s, c):
                i = EC * b + c
                dve.wait_ge(bsilu_done, i + 1)
                if c == 0 and not (isinstance(b, int) and b < 2):
                    dve.wait_ge(by_filled, b - 1)
                nc.vector.tensor_tensor(hb[:, s, c, :], ps_gu[:, (EC * s + c) % 4, BR:2 * BR], silu[:, c % 2, 0:BR], ALU.mult).then_inc(bh_done, 1)

            def body(it, last):
                for s in range(2):
                    b = 2 * it + s
                    for c in range(1, EC):
                        gate(b, s, c)
                    if not (last and s == 1):
                        gate(b + 1, 1 - s, 0)

            gate(0, 0, 0)
            body(0, False)
            with dve.Fori(1, NBLK // 2 - 1) as it:
                body(it, False)
            body(NBLK // 2 - 1, True)
            for t in range(NT):
                dve.wait_ge(gathered[t % YG], 16 * TOPK * (t // YG + 1))
                for k in range(TOPK):
                    ins = nc.vector.scalar_tensor_tensor(out=acc[:, t, :], in0=yg[:, t % YG, k, :], scalar=wgt[:, k, t:t + 1],
                                                         in1=acc[:, t, :], op0=ALU.mult, op1=ALU.add)
                    if k == 0:
                        ins.then_inc(half_combined, 1)
                        dve.wait_ge(half_combined, t + 1)
                ins.then_inc(combined, 1)

        @block.scalar
        def _(act):
            act.wait_ge(w_loaded, 48)
            for raw_w, hi in ((u_w, u_hi), (d_w, d_hi)):
                nc.scalar.copy(hi[:], raw_w[:, 0]).then_inc(w_hi_done, 1)
            for g in range(NG):
                for c in range(EC):
                    i = EC * g + c
                    act.wait_ge(gu_filled, i + 1)
                    if i >= 2:
                        act.wait_ge(h_done, i - 1)
                    nc.scalar.activation(silu[:, c % 2, :], ps_gu[:, 2 * (c % 2), :], ACT.Silu).then_inc(silu_done, 1)

            def gate(b, s, c):
                i = EC * b + c
                act.wait_ge(bgu_filled, i + 1)
                if not (isinstance(i, int) and i < 2):
                    act.wait_ge(bh_done, i - 1)
                elif i == 0:
                    act.wait_ge(h_done, NG * EC)
                nc.scalar.activation(silu[:, c % 2, 0:BR], ps_gu[:, (EC * s + c) % 4, 0:BR], ACT.Silu).then_inc(bsilu_done, 1)

            def copy_rows(b, s):
                act.wait_ge(bx_filled, b + 1)
                nc.scalar.copy(xbT[:, s].rearrange("p k r -> p (k r)"), ps_x[:, s, :]).then_inc(bx_copied, 1)

            def body(it, first, last):
                for s in range(2):
                    b = 2 * it + s
                    gate(b, s, 1)
                    gate(b, s, 2)
                    if not (last and s == 1):
                        copy_rows(b + 1, 1 - s)
                    for c in range(3, EC):
                        gate(b, s, c)
                    if not (last and s == 1):
                        gate(b + 1, 1 - s, 0)
                    act.wait_ge(by_filled, b + 1)
                    if not first:
                        act.wait_ge(by_stored[s], 16 * it)
                    nc.scalar.copy(yb[:, s].rearrange("p j d -> p (j d)"), ps_y[:, s, :]).then_inc(by_copied, 1)

            copy_rows(0, 0)
            gate(0, 0, 0)
            body(0, True, False)
            with act.Fori(1, NBLK // 2 - 1) as it:
                body(it, False, False)
            body(NBLK // 2 - 1, False, True)

        @block.tensor
        def _(pe):
            def three(out, a, b, start, stop):
                nc.tensor.matmul(out, a[0], b[0], start=start, stop=False)
                nc.tensor.matmul(out, a[0], b[1], start=False, stop=False)
                return nc.tensor.matmul(out, a[1], b[0], start=False, stop=stop)

            pe.wait_ge(loaded, 16 * 5)
            pe.wait_ge(taken_ready, 1)
            flat = taken[:].rearrange("p t e -> p (t e)")
            nc.tensor.matmul(ps_y[:, 0, 0:NT * E], tri_sb[:], flat, start=True, stop=True)
            nc.tensor.matmul(ps_y[:, 1, 0:NT * E], one_sb[:], flat, start=True, stop=True).then_inc(ranks_filled, 1)
            pe.wait_ge(x_loaded, 16)
            for t in range(NT):
                if t >= 2:
                    pe.wait_ge(x_split, 2 * (t - 1))
                for k in range(NC):
                    mm = nc.tensor.transpose(ps_x[:, t % 2, k * P:(k + 1) * P], x3[:, t, k * P:(k + 1) * P], id_sb[:])
                mm.then_inc(xt_filled, 1)
            pe.wait_ge(x_split, 2 * NT)
            pe.wait_ge(plan_ready, 1)
            pe.wait_ge(w_split, 3)
            for g in range(NG):
                cols = slice(g * 512, (g + 1) * 512)
                for c in range(EC):
                    i = EC * g + c
                    if i >= 2:
                        pe.wait_ge(h_done, i - 1)
                    for half, w in enumerate(((g_hi, g_lo), (u_hi, u_lo))):
                        for k in range(NC):
                            mm = three(ps_gu[:, 2 * (c % 2) + half, :], [z[:, k, c * P:(c + 1) * P] for z in w],
                                       [z[:, k, cols] for z in (x_hi, x_lo)], k == 0, k == NC - 1)
                    mm.then_inc(gu_filled, 1)
                pe.wait_ge(h_split, EC * (g + 1))
                for j in range(GT):
                    t = GT * g + j
                    if t >= 2:
                        pe.wait_ge(y_added, t - 1)
                    for c in range(EC):
                        mm = three(ps_y[:, t % 2, 0:D], [z[:, c, j * P:(j + 1) * P] for z in (h_hi, h_lo)],
                                   [z[:, c, :] for z in (d_hi, d_lo)], c == 0, c == EC - 1)
                    mm.then_inc(y_filled, 1)

            def turn_rows(b, s):
                pe.wait_ge(bx_loaded[s], 16 * (b // 2 + 1) if isinstance(b, int) else 8 * b + (16 if s == 0 else 8))
                if not (isinstance(b, int) and b < 2):
                    pe.wait_ge(bx_copied, b - 1)
                for k in range(NC):
                    for j in range(BJ):
                        mm = nc.tensor.transpose(ps_x[:, s, k * BR + j * P:k * BR + (j + 1) * P], xb[:, s, j, k * P:(k + 1) * P], id_sb[:])
                mm.then_inc(bx_filled, 1)

            def gate_up(b, s, c):
                i = EC * b + c
                if not (isinstance(i, int) and i < 4):
                    pe.wait_ge(bh_done, i - 3)
                bank = ps_gu[:, (EC * s + c) % 4, :]
                for half, w in enumerate((g_w, u_w)):
                    for k in range(NC):
                        mm = nc.tensor.matmul(bank[:, half * BR:(half + 1) * BR], w[:, s, k, c * P:(c + 1) * P], xbT[:, s, k, :],
                                              start=(k == 0), stop=(k == NC - 1))
                mm.then_inc(bgu_filled, 1)

            def start_block(b, s):
                pe.wait_ge(bw_loaded[s], 48 * (b // 2 + 1) if isinstance(b, int) else 24 * b + (48 if s == 0 else 24))
                pe.wait_ge(bx_copied, b + 1)
                gate_up(b, s, 0)

            def body(it, first, last):
                for s in range(2):
                    b = 2 * it + s
                    gate_up(b, s, 1)
                    gate_up(b, s, 2)
                    if not (last and s == 1):
                        turn_rows(b + 1, 1 - s)
                    for c in range(3, EC):
                        gate_up(b, s, c)
                    if not (last and s == 1):
                        start_block(b + 1, 1 - s)
                    pe.wait_ge(bh_done, EC * b + EC)
                    if not first:
                        pe.wait_ge(by_copied, b - 1)
                    for j in range(BJ):
                        for c in range(EC):
                            mm = nc.tensor.matmul(ps_y[:, s, j * D:(j + 1) * D], hb[:, s, c, j * P:(j + 1) * P], d_w[:, s, c, :],
                                                  start=(c == 0), stop=(c == EC - 1))
                    mm.then_inc(by_filled, 1)

            pe.wait_ge(h_done, NG * EC)
            pe.wait_ge(y_added, NT)
            turn_rows(0, 0)
            start_block(0, 0)
            body(0, True, False)
            with pe.Fori(1, NBLK // 2 - 1) as it:
                body(it, False, False)
            body(NBLK // 2 - 1, False, True)


def build(nc, ins, out):
    def scratch(name, shape):
        return nc.dram_tensor(name, shape, F32, kind="Internal").ap()

    q_scr = scratch("q_scr", [2, D, TOK])
    x1_scr, x2_scr, x3_scr = (scratch(n, [NT, P, D]) for n in ("x1_scr", "x2_scr", "x3_scr"))
    top_scr, wgt_scr = scratch("top_scr", [P, TOPK, NT, E]), scratch("wgt_scr", [P, TOPK, NT])
    xs_scr, ys_scr = scratch("xs_scr", [NBLK * BR, D]), scratch("ys_scr", [NBLK * BR, D])
    project_queries(nc, ins["x"], ins["wq"], ins["bq"], ins["ident"], q_scr, xs_scr)
    cross_attention(nc, ins["ctxT"], ins["x"], q_scr, ins["wk"], ins["bk"], ins["wv"], ins["bv"], ins["wp"],
                    ins["rows"], ins["ident"], ins["sel4"], ins["hmask"], x1_scr)
    circuit_ffn(nc, x1_scr, ins["rows"], ins["w1"], ins["b1"], ins["w2"], ins["wr"], ins["rb"], ins["ident"],
                x2_scr, x3_scr, top_scr, wgt_scr)
    experts(nc, x2_scr, x3_scr, top_scr, wgt_scr, xs_scr, ys_scr, ins["wg"], ins["wu"], ins["wd"], ins["ident"],
            ins["tri"], ins["blocks"], out)


def kernel(**inputs):
    import concourse.bacc as bacc
    from concourse.bass_utils import run_bass_kernel_spmd as run

    a = {k: np.asarray(v) for k, v in inputs.items()}
    chunked = lambda m: np.ascontiguousarray(m.reshape(m.shape[0] // P, P, -1).transpose(1, 0, 2))
    wide = lambda r: np.broadcast_to(r, (P,) + r.shape)
    ctx = a["ctx_1024"]
    ctx = np.concatenate([ctx, np.repeat(ctx[:, -1:], SKP - SK, axis=1)], axis=1)
    heads = lambda v: v.reshape(PAIRS, 2, HD, *v.shape[1:]).swapaxes(0, 1).reshape(2, P, *v.shape[1:])
    pad = EC * P - EI

    def up(shared, routed):
        w = np.concatenate([shared[None], routed]).transpose(0, 2, 1)
        w = np.pad(w, ((0, 0), (0, 0), (0, pad)))
        return w.reshape(NEXP, NC, P, EC * P).transpose(0, 2, 1, 3)

    wd = np.concatenate([a["L0_ffn_sd"][None], a["L0_ffn_rd"]]).transpose(0, 2, 1)
    wd = np.pad(wd, ((0, 0), (0, pad), (0, 0))).reshape(NEXP, EC, P, D).transpose(0, 2, 1, 3)
    data = {
        "x": a["x"].reshape(NT, P, D),
        "ctxT": ctx.transpose(0, 2, 1).reshape(B, NC, P, SKP).transpose(0, 2, 1, 3),
        "wq": chunked(a["L0_xattn_Wq"].T), "bq": a["L0_xattn_bq"].reshape(NC, P).T,
        "wk": chunked(a["L0_xattn_Wk"].T), "bk": a["L0_xattn_bk"].reshape(NC, P).T,
        "wv": chunked(a["L0_xattn_Wv"].T), "bv": heads(a["L0_xattn_bv"]).T,
        "wp": heads(np.ascontiguousarray(a["L0_xattn_Wp"].T)).transpose(1, 0, 2),
        "rows": wide(np.stack([a["L0_xattn_bp"], a["L0_attn_gamma1"], a["L0_attn_beta1"], a["L0_attn_b2"],
                               a["L0_attn_gamma2"], a["L0_attn_beta2"]])),
        "w1": a["L0_attn_w1"].T, "b1": a["L0_attn_b1"].reshape(FC, P).T, "w2": chunked(a["L0_attn_w2"].T),
        "wr": chunked(a["L0_ffn_wr"].T), "rb": wide(a["L0_ffn_rb"]),
        "wg": up(a["L0_ffn_sg"], a["L0_ffn_rg"]), "wu": up(a["L0_ffn_su"], a["L0_ffn_ru"]), "wd": wd,
        "tri": np.triu(np.ones((P, P), np.float32), 1),
        "blocks": wide(np.arange(NBLK, dtype=np.float32)),
        "ident": np.eye(P, dtype=np.float32),
        "sel4": np.tile(np.eye(32, dtype=np.float32), (4, 1)),
        "hmask": np.tile(np.repeat(np.eye(2, dtype=np.float32), HD, axis=0), (3, 1)),
    }
    nc = bacc.Bacc("TRN2", target_bir_lowering=False, num_devices=1)
    ins = {}
    for name in data:
        data[name] = np.ascontiguousarray(data[name])
        ins[name] = nc.dram_tensor("in_" + name, data[name].shape, mybir.dt.from_np(data[name].dtype), kind="ExternalInput").ap()
    out = nc.dram_tensor("out", (NT, P, D), F32, kind="ExternalOutput").ap()
    build(nc, ins, out)
    r = run(nc, [{"in_" + k: v for k, v in data.items()}], core_ids=[0])
    return r.results[0]["out"].reshape(B, SQ, D)
```

```python
import numpy as np
from contextlib import ExitStack

import concourse.bass as bass
from concourse import mybir

F32 = mybir.dt.float32
F32R = mybir.dt.float32r
ALU = mybir.AluOpType
ACT = mybir.ActivationFunctionType
AX = mybir.AxisListType

P = 128
B, SQ, D = 32, 64, 256
SK = 1601
H, HD = 16, 16
NC = D // P
PAIRS = H // 2
QK = 4
KQ = 402
SKP = QK * KQ
KLAST = SK - (QK - 1) * KQ
KT = -(-SK // P)
KTL = SK - (KT - 1) * P
TG = -(-KT // 4)
NT = B * SQ // P
KSTEPS = NC * QK
VSTEPS = -(-KT // 2)
STEPS = KSTEPS + VSTEPS
K_ORDER = [("k", i // QK, i % QK) for i in range(KSTEPS)]
STEP_ORDER = [K_ORDER[i // 2] if i % 2 == 0 else ("v", i - 1) for i in range(STEPS)]
PAIR_STEPS = [(None if p == 0 else 2 * p - 1, 2 * p) for p in range(PAIRS)]
CLOSING = (2, 4, 6)
HALF = PAIRS // NC
STACK = 3 * 32
PIECES = 2
COPIES = 16 * 3 * HALF
SCALE = float(HD) ** 0.5
EPS = 1e-5
FF = 1024
FC = FF // P
E, EI = 7, 704
EC = -(-EI // P)
NEXP = E + 1
TOK = B * SQ
GT = 4
NG = NT // GT
BR = 256
BJ = BR // P
TOPK = 2
NBLK = (TOPK * TOK + E * (BR - 1)) // BR
HEAD = TOK // BR // 2
NALL = NBLK + 2 * HEAD
ZROWS = NBLK * BR // NT
ZP = ZROWS // 4
COMBINED_IN = {NALL - 3: range(0, 4), NALL - 2: range(4, 9), NALL - 1: range(9, NT)}
TWO_PI_PARTS = (6.28125, 2.0 * np.pi - 6.28125)
ROUND = 12582912.0


def rows_keys(t):
    return P if t < KT - 1 else KTL


def project_queries(nc, x, wq, bq, ident, q_scr):
    with ExitStack() as ctx:
        sb = lambda n, s, d=F32: ctx.enter_context(nc.sbuf_tensor(n, s, d))
        sem = lambda n: ctx.enter_context(nc.semaphore(n))
        x_sb = sb("q_x", [P, NT, D])
        wq_sb = sb("q_wq", [P, NC, D])
        bq_sb, bq_scaled = sb("q_bq", [P, NC]), sb("q_bqs", [P, NC])
        id_sb = sb("q_id", [P, P])
        stats = sb("q_stats", [P, NT, 6])
        mv = sb("q_mv", [P, NT, 2])
        vare, expo, rstd = sb("q_vare", [P, NT]), sb("q_expo", [P, NT]), sb("q_rstd", [P, NT])
        xT = sb("q_xT", [P, NC, TOK])
        qT = sb("q_qT", [P, 4, 512])
        q_hi = sb("q_hi", [P, NC, TOK], F32R)
        q_lo = sb("q_lo", [P, NC, TOK], F32R)
        ps_t = ctx.enter_context(nc.psum_tensor("q_pst", [P, 4, 512], F32))
        ps_q = ctx.enter_context(nc.psum_tensor("q_psq", [P, 4, 512], F32))
        x_loaded = [sem(f"q_xl{g}") for g in range(NG)]
        w_loaded, stored, bias_ready = sem("q_w_loaded"), sem("q_stored"), sem("q_br")
        stat_done, aggr_done, var_done, pow_set, pow_done, norm_done = (
            sem("q_stat"), sem("q_aggr"), sem("q_var"), sem("q_pset"), sem("q_pow"), sem("q_norm"))
        t_filled, t_copied, q_filled, q_biased, q_hi_done, q_split = (
            sem("q_tf"), sem("q_tc"), sem("q_qf"), sem("q_qb"), sem("q_qh"), sem("q_qs"))
        block = ctx.enter_context(nc.Block())
        cols = lambda g: slice(g * 512, (g + 1) * 512)

        @block.sync
        def _(sp):
            for g in range(NG):
                sp.dma_start(x_sb[:, GT * g:GT * (g + 1), :], x[GT * g:GT * (g + 1)].rearrange("t p d -> p t d")).then_inc(x_loaded[g], 16)
                if g == 0:
                    for dst, src in ((id_sb, ident), (wq_sb, wq), (bq_sb, bq)):
                        sp.dma_start(dst[:], src).then_inc(w_loaded, 16)
            for g in range(NG):
                sp.wait_ge(q_split, NC * (g + 1))
                for i, part in enumerate((q_hi, q_lo)):
                    sp.dma_start(q_scr[i].rearrange("(m p) t -> p m t", p=P)[:, :, cols(g)], part[:, :, cols(g)].bitcast(F32)).then_inc(stored, 16)
            sp.wait_ge(stored, 32 * NG)

        @block.gpsimd
        def _(pool):
            nc.gpsimd.memset(expo[:], -0.5).then_inc(pow_set, 1)
            pool.wait_ge(pow_set, 1)
            for g in range(NG):
                tiles = slice(GT * g, GT * (g + 1))
                pool.wait_ge(var_done, g + 1)
                nc.gpsimd.tensor_tensor(out=rstd[:, tiles], in0=vare[:, tiles], in1=expo[:, tiles], op=ALU.pow).then_inc(pow_done, 1)

        @block.vector
        def _(dve):
            def sums(g):
                dve.wait_ge(x_loaded[g], 16)
                for t in range(GT * g, GT * (g + 1)):
                    nc.vector.bn_stats(out=stats[:, t, :], in_=x_sb[:, t, :]).then_inc(stat_done, 1)
                for t in range(GT * g, GT * (g + 1)):
                    dve.wait_ge(stat_done, t + 1)
                    nc.vector.bn_aggr(out=mv[:, t, :], in_=stats[:, t, :]).then_inc(aggr_done, 1)
                dve.wait_ge(aggr_done, GT * (g + 1))
                tiles = slice(GT * g, GT * (g + 1))
                nc.vector.tensor_scalar(vare[:, tiles], mv[:, tiles, 1], EPS, None, ALU.add).then_inc(var_done, 1)

            def normalise(g):
                dve.wait_ge(pow_done, g + 1)
                for t in range(GT * g, GT * (g + 1)):
                    nc.vector.tensor_scalar(x_sb[:, t, :], x_sb[:, t, :], mv[:, t, 0:1], rstd[:, t:t + 1],
                                            ALU.subtract, ALU.mult).then_inc(norm_done, 1)

            def lower(g):
                for m in range(NC):
                    i = NC * g + m
                    dve.wait_ge(q_hi_done, i + 1)
                    nc.vector.tensor_tensor(q_lo[:, m, cols(g)], qT[:, i % 4, :], q_hi[:, m, cols(g)].bitcast(F32), ALU.subtract).then_inc(q_split, 1)

            sums(0)
            dve.wait_ge(w_loaded, 48)
            nc.vector.tensor_scalar(bq_scaled[:], bq_sb[:], SCALE, None, ALU.mult).then_inc(bias_ready, 1)
            for g in range(NG):
                if g < NG - 1:
                    sums(g + 1)
                normalise(g)
                if g > 0:
                    lower(g - 1)
            lower(NG - 1)

        @block.scalar
        def _(act):
            act.wait_ge(bias_ready, 1)

            def copy_rows(g):
                for k in range(NC):
                    i = NC * g + k
                    act.wait_ge(t_filled, i + 1)
                    nc.scalar.copy(xT[:, k, cols(g)], ps_t[:, i % 4, :]).then_inc(t_copied, 1)

            copy_rows(0)
            for g in range(NG):
                if g < NG - 1:
                    copy_rows(g + 1)
                for m in range(NC):
                    i = NC * g + m
                    act.wait_ge(q_filled, i + 1)
                    if i >= 4:
                        act.wait_ge(q_split, i - 3)
                    nc.scalar.activation(qT[:, i % 4, :], ps_q[:, i % 4, :], ACT.Identity, bias=bq_scaled[:, m:m + 1], scale=SCALE).then_inc(q_biased, 1)
                    act.wait_ge(q_biased, i + 1)
                    nc.scalar.copy(q_hi[:, m, cols(g)], qT[:, i % 4, :]).then_inc(q_hi_done, 1)

        @block.tensor
        def _(pe):
            pe.wait_ge(w_loaded, 48)

            def turn(g):
                pe.wait_ge(norm_done, GT * (g + 1))
                for k in range(NC):
                    i = g * NC + k
                    if i >= 4:
                        pe.wait_ge(t_copied, i - 3)
                    for j in range(GT):
                        mm = nc.tensor.transpose(ps_t[:, i % 4, j * P:(j + 1) * P],
                                                 x_sb[:, GT * g + j, k * P:(k + 1) * P], id_sb[:])
                    mm.then_inc(t_filled, 1)

            turn(0)
            for g in range(NG):
                if g < NG - 1:
                    turn(g + 1)
                pe.wait_ge(t_copied, NC * (g + 1))
                for m in range(NC):
                    i = g * NC + m
                    if i >= 4:
                        pe.wait_ge(q_biased, i - 3)
                    for k in range(NC):
                        mm = nc.tensor.matmul(ps_q[:, i % 4, :], wq_sb[:, k, m * P:(m + 1) * P],
                                              xT[:, k, cols(g)], start=(k == 0), stop=(k == NC - 1))
                    mm.then_inc(q_filled, 1)


def cross_attention(nc, ctxT, x, q_scr, wk, bk, wv, bv, wp, rows, ident, sel4, hmask, x1_scr, rows_scr):
    with ExitStack() as ctx:
        sb = lambda n, s, d=F32: ctx.enter_context(nc.sbuf_tensor(n, s, d))
        ps = lambda n, s: ctx.enter_context(nc.psum_tensor(n, s, F32))
        sem = lambda n: ctx.enter_context(nc.semaphore(n))
        raw = sb("a_raw", [P, NC, SKP])
        c_hi, c_lo = sb("a_chi", [P, 2, NC, SKP], F32R), sb("a_clo", [P, 2, NC, SKP], F32R)
        k_hi, k_lo = sb("a_khi", [P, SKP], F32R), sb("a_klo", [P, SKP], F32R)
        k_st = sb("a_kst", [STACK, PAIRS, SKP], F32R)
        v_sb = sb("a_v", [P, 2, KT, D])
        probs = sb("a_probs", [P, 2, SKP])
        pT = sb("a_pT", [P, KT, P])
        w_raw = probs[:, 0, 0:2 * NC * D].rearrange("p (w k d) -> p w k d", w=2, k=NC)
        w_hi, w_lo = sb("a_whi", [P, 2, NC, D], F32R), sb("a_wlo", [P, 2, NC, D], F32R)
        bk_sb, bv_sb = sb("a_bk", [P, NC]), sb("a_bv", [P, 2])
        wp_sb = sb("a_wp", [P, 2, D])
        bp_sb = sb("a_bp", [P, D])
        id_sb, sel_sb, hm_sb = sb("a_id", [P, P]), sb("a_sel", [P, 32]), sb("a_hm", [STACK, 2])
        q_sb = sb("a_q", [STACK, PAIRS, SQ])
        bd = sb("a_bd", [STACK, 2, PAIRS, P], F32R)
        o_part = sb("a_op", [P, 2, PAIRS, P])
        tick = sb("a_tick", [P, 1])
        zero, zeroed, cleared = sb("a_zero", [ZP, D]), sem("a_zeroed"), sem("a_cleared")
        ticked = sem("a_tk")
        nmax = sb("a_nmax", [P, 2, PAIRS])
        esum = sb("a_esum", [P, 2, PAIRS, 2])
        rsum, rinv = sb("a_rsum", [P, PAIRS]), sb("a_rinv", [P, PAIRS])
        o_head = sb("a_oh", [P, PAIRS, HD])
        oT = sb("a_oT", [P, 2, P])
        x_t, y_t, x1_t = sb("a_x", [P, D]), sb("a_y", [P, D]), sb("a_x1", [P, D])
        ps_s, ps_t, ps_o, ps_k = ps("a_pss", [P, QK, 512]), ps("a_pst", [P, 2, 512]), ps("a_pso", [P, 512]), ps("a_psk", [P, 512])

        w_loaded, ctx0_hi_done, w_hi_done = sem("a_wl"), sem("a_c0"), sem("a_wh")
        const_loaded, ctx_loaded, q_loaded, x_loaded = sem("a_cl"), sem("a_ctxl"), sem("a_ql"), sem("a_xl")
        stacked = [[sem(f"a_st{m}{z}") for z in range(PIECES)] for m in range(NC)]
        w_split, ctx_hi_done, ctx_split, bd_ready = sem("a_ws"), sem("a_ch"), sem("a_cs"), sem("a_bd")
        kv_filled, k_hi_done, kv_copied = sem("a_kvf"), sem("a_khd"), sem("a_kvc")
        s_filled, max_ready, probs_ready = sem("a_sf"), sem("a_mr"), sem("a_pr")
        t_filled, t_copied_act, t_copied_dve = sem("a_tf"), sem("a_tca"), sem("a_tcd")
        o_filled, o_copied = sem("a_of"), sem("a_oc")
        sum_filled, sum_step, head_ready, hT_filled, hT_copied = (
            sem("a_suf"), sem("a_sus"), sem("a_hr"), sem("a_htf"), sem("a_htc"))
        y_filled, y_biased, x1_ready, x1_free = sem("a_yf"), sem("a_yb"), sem("a_x1r"), sem("a_x1f")
        block = ctx.enter_context(nc.Block())
        first_banks = [ps_k[:]] + [ps_s[:, i, :] for i in range(QK)]

        @block.sync
        def _(sp):
            def load_queries(n):
                for i, part in enumerate((0, 0, 1)):
                    src = q_scr[part, :, bass.ds(n * SQ, SQ)].rearrange("(p r) t -> r p t", r=32)
                    sp.dma_start(q_sb[32 * i:32 * i + 32], src).then_inc(q_loaded, 16)

            def stack_keys(n, m):
                for z in range(PIECES):
                    if z == 0 and not (isinstance(n, int) and n == 0):
                        sp.wait_ge(s_filled, PAIRS * n - (PAIRS - HALF) if m == 0 else PAIRS * n)
                    else:
                        sp.wait_ge(kv_copied, STEPS * n + STEP_ORDER.index(("k", m, QK // PIECES * (z + 1) - 1)) + 1)
                    cols = slice(z * SKP // PIECES, (z + 1) * SKP // PIECES)
                    for j in range(HALF):
                        for i, part in enumerate((k_hi, k_lo, k_hi)):
                            sp.dma_start(k_st[32 * i:32 * i + 32, HALF * m + j, cols].bitcast(F32),
                                         part[32 * j:32 * j + 32, cols].bitcast(F32)).then_inc(stacked[m][z], 16)

            sp.dma_start(w_raw[:, 0], wk).then_inc(w_loaded, 16)
            sp.dma_start(w_raw[:, 1], wv).then_inc(w_loaded, 16)
            sp.dma_start(raw[:], ctxT[0]).then_inc(ctx_loaded, 16)
            load_queries(0)
            for dst, src in ((bk_sb[:], bk), (bv_sb[:], bv), (wp_sb[:], wp), (bp_sb[:], rows[:, 0]),
                             (id_sb[:], ident), (sel_sb[:], sel4), (hm_sb[:], hmask)):
                sp.dma_start(dst, src).then_inc(const_loaded, 16)
            sp.wait_ge(ctx_split, 1)
            sp.dma_start(raw[:], ctxT[1]).then_inc(ctx_loaded, 16)
            sp.wait_ge(zeroed, 1)
            stack_keys(0, 0)

            def body(it, first, last):
                for b in range(2):
                    n = 2 * it + b
                    stack_keys(n, 1)
                    if not (last and b == 1):
                        sp.wait_ge(bd_ready, n + 1)
                        load_queries(n + 1)
                    if not last:
                        sp.wait_ge(ctx_split, n + 2)
                        sp.dma_start(raw[:], ctxT[bass.ds(n + 2, 1)].rearrange("a p k s -> p (a k) s")).then_inc(ctx_loaded, 16)
                    if b == 1:
                        sp.dma_start(rows_scr[bass.ds(it * ZROWS + HEAD * BR, ZROWS), :].rearrange("(j p) d -> p j d", p=ZP),
                                     zero[:].unsqueeze(1).to_broadcast([ZP, ZROWS // ZP, D])).then_inc(cleared, 16)
                    if b == 0 and not first:
                        sp.dma_start(x_t[:], x[bass.ds(it - 1, 1)].rearrange("a p d -> (a p) d")).then_inc(x_loaded, 16)
                    if not (last and b == 1):
                        stack_keys(n + 1, 0)
                    if b == 0 and not first:
                        sp.wait_ge(x1_ready, it)
                        sp.dma_start(x1_scr[bass.ds(it - 1, 1)].rearrange("a p d -> (a p) d"), x1_t[:]).then_inc(x1_free, 16)

            body(0, True, False)
            with sp.Fori(1, NT - 1) as it:
                body(it, False, False)
            body(NT - 1, False, True)
            sp.wait_ge(x1_ready, NT - 1)
            sp.dma_start(x_t[:], x[NT - 1]).then_inc(x_loaded, 16)
            sp.wait_ge(x1_ready, NT)
            sp.dma_start(x1_scr[NT - 1], x1_t[:]).then_inc(x1_free, 16)
            sp.wait_ge(x1_free, 16 * NT + 1)
            sp.wait_ge(cleared, 16 * NT)

        @block.gpsimd
        def _(pool):
            def split_ctx(n, s):
                pool.wait_ge(ctx_loaded, 16 * n + 16)
                nc.gpsimd.tensor_tensor(out=tick[:], in0=tick[:], in1=tick[:], op=ALU.mult).then_inc(ticked, 1)
                nc.gpsimd.tensor_copy(c_hi[:, s], raw[:]).then_inc(ctx_hi_done, 1)
                pool.wait_ge(ctx_hi_done, n)
                nc.gpsimd.tensor_tensor(out=c_lo[:, s], in0=raw[:], in1=c_hi[:, s].bitcast(F32),
                                        op=ALU.subtract).then_inc(ctx_split, 1)

            def spread_queries(n, s):
                pool.wait_ge(q_loaded, 48 * n + 48)
                nc.gpsimd.tensor_tensor(
                    out=bd[:, s].rearrange("r p (h q) -> r p h q", h=2),
                    in0=q_sb[:].unsqueeze(2).to_broadcast([STACK, PAIRS, 2, SQ]),
                    in1=hm_sb[:].unsqueeze(1).unsqueeze(3).to_broadcast([STACK, PAIRS, 2, SQ]),
                    op=ALU.mult).then_inc(bd_ready, 1)

            nc.gpsimd.memset(zero[:], 0.0).then_inc(zeroed, 1)
            nc.gpsimd.memset(tick[:], 0.0).then_inc(ticked, 1)
            pool.wait_ge(ticked, 1)
            pool.wait_ge(const_loaded, 16 * 7)
            spread_queries(0, 0)
            split_ctx(1, 1)

            def body(it, first, last):
                for b in range(2):
                    n = 2 * it + b
                    if not (last and b == 1):
                        if not (first and b == 0):
                            pool.wait_ge(s_filled, PAIRS * n)
                        spread_queries(n + 1, (b + 1) % 2)
                    if not last:
                        pool.wait_ge(kv_filled, STEPS * (n + 1))
                        split_ctx(n + 2, b)

            body(0, True, False)
            with pool.Fori(1, NT - 1) as it:
                body(it, False, False)
            body(NT - 1, False, True)

        @block.scalar
        def _(act):
            def copy_tiles(g, i):
                act.wait_ge(t_filled, TG * g + i + 1)
                nc.scalar.copy(pT[:, 4 * i:4 * i + 4, :], ps_t[:, i % 2, :].rearrange("p (t q) -> p t q", q=P)).then_inc(t_copied_act, 1)

            def exponentials(g, b, p):
                act.wait_ge(max_ready, g + 1)
                pr = probs[:, p % 2, :].rearrange("p (b k) -> p b k", b=QK)
                bias = nmax[:, b, p:p + 1]
                nc.scalar.activation(pr[:, 0:QK - 1, :], ps_s[:, 0:QK - 1, 0:KQ], ACT.Exp, bias=bias,
                                     accum_out=esum[:, b, p, 0:1])
                nc.scalar.activation(pr[:, QK - 1, 0:KLAST], ps_s[:, QK - 1, 0:KLAST], ACT.Exp, bias=bias,
                                     accum_out=esum[:, b, p, 1:2]).then_inc(probs_ready, 1)

            def copy_out(g, b, p):
                act.wait_ge(o_filled, g + 1)
                nc.scalar.copy(o_part[:, b, p, :], ps_o[:, 0:P]).then_inc(o_copied, 1)

            def copy_heads(n, b):
                act.wait_ge(hT_filled, n + 1)
                for e in range(2):
                    last = nc.scalar.activation(oT[:, e, SQ * b:SQ * (b + 1)], ps_k[:, SQ * e:SQ * (e + 1)], ACT.Identity,
                                                bias=bv_sb[:, e:e + 1])
                last.then_inc(hT_copied, 1)

            act.wait_ge(w_loaded, 32)
            nc.scalar.copy(w_hi[:], w_raw).then_inc(w_hi_done, 1)
            act.wait_ge(ctx_loaded, 16)
            for k in range(NC):
                nc.scalar.copy(c_hi[:, 0, k, :], raw[:, k, :]).then_inc(ctx0_hi_done, 1)

            def body(it, first, last):
                for b in range(2):
                    for p in range(PAIRS):
                        g = PAIRS * (2 * it + b) + p
                        start = first and b == 0 and p == 0
                        if not start:
                            copy_tiles(g - 1, 0)
                            copy_tiles(g - 1, 1)
                        if p == CLOSING[1] and not (first and b == 0):
                            if first:
                                act.wait_ge(const_loaded, 16 * 7)
                            copy_heads(2 * it + b - 1, 1 - b)
                        exponentials(g, b, p)
                        if not start:
                            copy_out(g - 1, b if p > 0 else 1 - b, (p - 1) % PAIRS)

            body(0, True, False)
            with act.Fori(1, NT - 1) as it:
                body(it, False, False)
            body(NT - 1, False, True)
            g = PAIRS * B - 1
            copy_tiles(g, 0)
            copy_tiles(g, 1)
            copy_out(g, 1, PAIRS - 1)
            copy_heads(B - 1, 1)

        @block.vector
        def _(dve):
            def row_max(g, b, p):
                dve.wait_ge(s_filled, g + 1)
                nc.vector.tensor_reduce(nmax[:, b, p:p + 1], ps_s[:, :, 0:KQ], AX.XY, ALU.max, negate=True).then_inc(max_ready, 1)

            def copy_step(n, slot, s, ps_k=ps_k):
                dve.wait_ge(kv_filled, STEPS * n + s + 1)
                kind, *at = STEP_ORDER[s]
                if kind == "k":
                    m, q = at
                    if q % (QK // PIECES) == 0:
                        z = q // (QK // PIECES)
                        if m == 1:
                            dve.wait_ge(stacked[0][z], COPIES * (n + 1))
                        elif not (isinstance(n, int) and n == 0):
                            dve.wait_ge(stacked[1][z], COPIES * n)
                    hi, lo = (t[:, q * KQ:(q + 1) * KQ] for t in (k_hi, k_lo))
                    nc.vector.tensor_scalar(hi, ps_k[:, 0:KQ], bk_sb[:, m:m + 1], None, ALU.add).then_inc(k_hi_done, 1)
                    dve.wait_ge(k_hi_done, KSTEPS * n + QK * m + q + 1)
                    nc.vector.scalar_tensor_tensor(out=lo, in0=ps_k[:, 0:KQ], scalar=bk_sb[:, m:m + 1], in1=hi.bitcast(F32),
                                                   op0=ALU.add, op1=ALU.subtract).then_inc(kv_copied, 1)
                else:
                    t = at[0]
                    if t < KT - 1:
                        nc.vector.tensor_copy(v_sb[:, slot, t:t + 2, :], ps_k[:, :].rearrange("p (t d) -> p t d", t=2)).then_inc(kv_copied, 1)
                    else:
                        nc.vector.tensor_copy(v_sb[0:KTL, slot, t, :], ps_k[0:KTL, 0:D]).then_inc(kv_copied, 1)

            def copy_tiles(g, i):
                dve.wait_ge(t_filled, TG * g + i + 1)
                if i < TG - 1:
                    nc.vector.tensor_copy(pT[:, 4 * i:4 * i + 4, :], ps_t[:, i % 2, :].rearrange("p (t q) -> p t q", q=P)).then_inc(t_copied_dve, 1)
                else:
                    nc.vector.tensor_copy(pT[0:KTL, KT - 1, :], ps_t[0:KTL, i % 2, 0:P]).then_inc(t_copied_dve, 1)

            def normalise(n, b):
                dve.wait_ge(probs_ready, PAIRS * (n + 1))
                nc.vector.tensor_tensor(rsum[:], esum[:, b, :, 0], esum[:, b, :, 1], ALU.add).then_inc(sum_step, 1)
                dve.wait_ge(sum_step, 2 * n + 1)
                nc.vector.reciprocal(rinv[:], rsum[:]).then_inc(sum_step, 1)
                dve.wait_ge(sum_step, 2 * n + 2)
                dve.wait_ge(sum_filled, n + 1)
                for e in range(2):
                    r = slice(SQ * e, SQ * (e + 1))
                    last = nc.vector.tensor_tensor(
                        o_head[r, :, :], ps_k[r, 0:D].rearrange("p (j e d) -> p j e d", e=2, d=HD)[:, :, e, :],
                        rinv[r, :].unsqueeze(2).to_broadcast([SQ, PAIRS, HD]), ALU.mult)
                last.then_inc(head_ready, 1)

            def residual(t):
                dve.wait_ge(y_filled, t + 1)
                nc.vector.tensor_tensor(y_t[:], ps_k[:, 0:D], bp_sb[:], ALU.add).then_inc(y_biased, 1)
                dve.wait_ge(y_biased, t + 1)
                dve.wait_ge(x_loaded, 16 * (t + 1))
                dve.wait_ge(x1_free, 16 * t + 1)
                nc.vector.tensor_tensor(x1_t[:], y_t[:], x_t[:], ALU.add).then_inc(x1_ready, 1)

            nc.vector.memset(x1_t[:], 0.0).then_inc(x1_free, 1)
            dve.wait_ge(w_hi_done, 1)
            nc.vector.tensor_tensor(w_lo[:], w_raw, w_hi[:].bitcast(F32), ALU.subtract).then_inc(w_split, 1)
            for k in range(NC):
                dve.wait_ge(ctx0_hi_done, k + 1)
                last = nc.vector.tensor_tensor(c_lo[:, 0, k, :], raw[:, k, :], c_hi[:, 0, k, :].bitcast(F32), ALU.subtract)
            last.then_inc(ctx_split, 1)
            dve.wait_ge(const_loaded, 16 * 7)
            for s in range(STEPS):
                copy_step(0, 0, s, first_banks[s % (QK + 1)])

            def body(it, first, last):
                for b in range(2):
                    n = 2 * it + b
                    ahead = not (last and b == 1)
                    behind = not (first and b == 0)
                    for p in range(PAIRS):
                        g = PAIRS * n + p
                        row_max(g, b, p)
                        steps = PAIR_STEPS[p] if ahead else (None, None)
                        closing = behind and (p in CLOSING[:2] or (p == CLOSING[2] and b == 0))
                        if closing and p == CLOSING[0]:
                            normalise(n - 1, 1 - b)
                        elif closing and p == CLOSING[2]:
                            residual(it - 1)
                        if steps[0] is not None and not closing:
                            copy_step(n + 1, 1 - b, steps[0])
                        if behind or p > 0:
                            copy_tiles(g - 1, 2)
                            copy_tiles(g - 1, 3)
                        if steps[0] is not None and closing:
                            copy_step(n + 1, 1 - b, steps[0])
                        if steps[1] is not None:
                            copy_step(n + 1, 1 - b, steps[1])

            body(0, True, False)
            with dve.Fori(1, NT - 1) as it:
                body(it, False, False)
            body(NT - 1, False, True)
            copy_tiles(PAIRS * B - 1, 2)
            copy_tiles(PAIRS * B - 1, 3)
            normalise(B - 1, 1)
            residual(NT - 1)

        @block.tensor
        def _(pe):
            def three(out, a, b, start, stop):
                nc.tensor.matmul(out, a[0], b[0], start=start, stop=False)
                nc.tensor.matmul(out, a[0], b[1], start=False, stop=False)
                return nc.tensor.matmul(out, a[1], b[0], start=False, stop=stop)

            def step(n, slot, s, ps_k=ps_k, ahead=0):
                if not isinstance(n, int) or STEPS * n + s > ahead:
                    pe.wait_ge(kv_copied, STEPS * n + s - ahead)
                kind, *at = STEP_ORDER[s]
                if kind == "k":
                    m, q = at
                    for k in range(NC):
                        mm = three(ps_k[:, 0:KQ], [w[:, 0, k, m * P:(m + 1) * P] for w in (w_hi, w_lo)],
                                   [c[:, slot, k, q * KQ:(q + 1) * KQ] for c in (c_hi, c_lo)], k == 0, k == NC - 1)
                else:
                    for t in range(at[0], min(at[0] + 2, KT)):
                        r = rows_keys(t)
                        for k in range(NC):
                            mm = three(ps_k[0:r, (t % 2) * D:(t % 2 + 1) * D],
                                       [c[:, slot, k, t * P:t * P + r] for c in (c_hi, c_lo)],
                                       [w[:, 1, k, :] for w in (w_hi, w_lo)], k == 0, k == NC - 1)
                mm.then_inc(kv_filled, 1)

            def scores(b, p):
                for q in range(QK):
                    mm = nc.tensor.matmul(ps_s[:, q, 0:KQ], bd[:, b, p, :], k_st[:, p, q * KQ:(q + 1) * KQ], start=True, stop=True)
                mm.then_inc(s_filled, 1)

            def turn(p, i):
                for t in range(4 * i, min(4 * i + 4, KT)):
                    r = rows_keys(t)
                    mm = nc.tensor.transpose(ps_t[0:r, i % 2, (t % 4) * P:(t % 4 + 1) * P],
                                             probs[:, p % 2, t * P:t * P + r], id_sb[:])
                mm.then_inc(t_filled, 1)

            def weigh(b, p, i):
                for t in range(4 * i, min(4 * i + 4, KT)):
                    r, c = rows_keys(t), 32 * (t % 4)
                    mm = nc.tensor.matmul(ps_o[c:c + 32, 0:P], v_sb[0:r, b, t, 32 * p:32 * p + 32], pT[0:r, t, :],
                                          start=(t < 4), stop=(t + 4 >= KT))
                return mm

            def sum_parts(n, b):
                pe.wait_ge(o_copied, PAIRS * (n + 1))
                for p in range(PAIRS):
                    mm = nc.tensor.matmul(ps_k[:, 32 * p:32 * p + 32], o_part[:, b, p, :], sel_sb[:], start=True, stop=True)
                mm.then_inc(sum_filled, 1)

            def turn_heads(n):
                pe.wait_ge(head_ready, n + 1)
                nc.tensor.transpose(ps_k[:, 0:P], o_head[:].rearrange("p j d -> p (j d)"), id_sb[:]).then_inc(hT_filled, 1)

            def project_out(t):
                pe.wait_ge(hT_copied, 2 * t + 2)
                for e in range(2):
                    mm = nc.tensor.matmul(ps_k[:, 0:D], oT[:, e, :], wp_sb[:, e, :], start=(e == 0), stop=(e == 1))
                mm.then_inc(y_filled, 1)

            def slot_tail(g, p, b, n, slot, steps, closing=None, closed=None):
                if g is not None:
                    if not isinstance(g, int) or g > 0:
                        pe.wait_ge(t_copied_dve, 2 * g)
                    turn(p, 0)
                    turn(p, 1)
                if closing is not None:
                    if steps[0] is not None:
                        pe.wait_ge(kv_copied, STEPS * n + steps[0])
                    closing()
                elif steps[0] is not None:
                    step(n, slot, steps[0])
                if g is not None:
                    pe.wait_ge(t_copied_act, 2 * g + 1)
                    if not isinstance(g, int) or g > 0:
                        pe.wait_ge(o_copied, g)
                    weigh(b, p, 0)
                    turn(p, 2)
                    pe.wait_ge(t_copied_act, 2 * g + 2)
                    weigh(b, p, 1)
                    turn(p, 3)
                if closing is not None:
                    if steps[0] is not None:
                        pe.wait_ge(*closed)
                        step(n, slot, steps[0])
                elif steps[1] is not None:
                    step(n, slot, steps[1])
                if g is not None:
                    pe.wait_ge(t_copied_dve, 2 * g + 2)
                    weigh(b, p, 2)
                    weigh(b, p, 3).then_inc(o_filled, 1)
                if closing is not None and steps[1] is not None:
                    step(n, slot, steps[1])

            pe.wait_ge(const_loaded, 16 * 7)
            pe.wait_ge(w_split, 1)
            pe.wait_ge(ctx_split, 1)
            for s in range(STEPS):
                step(0, 0, s, first_banks[s % (QK + 1)], QK)
            pe.wait_ge(kv_copied, STEPS)

            def body(it, first, last):
                for b in range(2):
                    n = 2 * it + b
                    ahead = not (last and b == 1)
                    behind = not (first and b == 0)
                    pe.wait_ge(bd_ready, n + 1)
                    if ahead:
                        pe.wait_ge(ctx_split, n + 2)
                    else:
                        pe.wait_ge(kv_copied, STEPS * (n + 1))
                    for p in range(PAIRS):
                        g = PAIRS * n + p
                        if p % HALF == 0:
                            for piece in stacked[p // HALF]:
                                pe.wait_ge(piece, COPIES * (n + 1))
                        if behind or p > 0:
                            pe.wait_ge(probs_ready, g)
                        scores(b, p)
                        before = g - 1 if behind or p > 0 else None
                        steps = PAIR_STEPS[p] if ahead else (None, None)
                        closing = closed = None
                        if behind and p == CLOSING[0]:
                            closing, closed = (lambda: sum_parts(n - 1, 1 - b)), (head_ready, n)
                        elif behind and p == CLOSING[1]:
                            closing, closed = (lambda: turn_heads(n - 1)), (hT_copied, n)
                        elif behind and p == CLOSING[2] and b == 0:
                            closing, closed = (lambda: project_out(it - 1)), (y_biased, it)
                        slot_tail(before, (p - 1) % PAIRS, b if p > 0 else 1 - b, n + 1, 1 - b, steps, closing, closed)

            body(0, True, False)
            with pe.Fori(1, NT - 1) as it:
                body(it, False, False)
            body(NT - 1, False, True)
            pe.wait_ge(probs_ready, PAIRS * B)
            slot_tail(PAIRS * B - 1, PAIRS - 1, 1, None, 0, (None, None))
            sum_parts(B - 1, 1)
            turn_heads(B - 1)
            project_out(NT - 1)


class Chain:

    def __init__(self, eng, sem):
        self.eng, self.sem, self.n = eng, sem, 0

    def __call__(self, ins):
        self.n += 1
        ins.then_inc(self.sem, 1)
        return self.n

    def wait(self, n=None):
        self.eng.wait_ge(self.sem, self.n if n is None else n)


def circuit_ffn(nc, x1_scr, rows, w1, b1, w2, wr, rb, ident, x2_scr, rows_scr, top_scr, wgt_scr):
    with ExitStack() as ctx:
        sb = lambda n, s, d=F32: ctx.enter_context(nc.sbuf_tensor(n, s, d))
        ps = lambda n, s: ctx.enter_context(nc.psum_tensor(n, s, F32))
        sem = lambda n: ctx.enter_context(nc.semaphore(n))
        x1, a, t, c = (sb(f"f_{n}", [P, NT, D]) for n in ("x1", "a", "t", "c"))
        row = sb("f_rows", [P, 6, D])
        stats, mv, vare, expo, rstd = sb("f_st", [P, NT, 6]), sb("f_mv", [P, NT, 2]), sb("f_va", [P, NT]), sb("f_ex", [P, NT]), sb("f_rs", [P, NT])
        half_pi, less_round = sb("f_hp", [P, 1]), sb("f_lr", [P, 1])
        qx, qs, qt, qn = (sb(f"f_{n}", [P, NT, HD]) for n in ("qx", "qs", "qt", "qn"))
        w1_sb, b1_sb, w2_sb = sb("f_w1", [P, FF]), sb("f_b1", [P, FC]), sb("f_w2", [P, FC, D])
        wr_sb, rb_sb, id_sb = sb("f_wr", [P, NC, E]), sb("f_rb", [P, E]), sb("f_id", [P, P])
        qT, hT = sb("f_qT", [P, 512]), sb("f_hT", [P, FC, 512])
        xT = sb("f_xT", [P, GT, NC, P])
        lg, pr, rank, cmp, tiny = sb("f_lg", [P, NT, E]), sb("f_pr", [P, NT, E]), sb("f_rk", [P, NT, E]), sb("f_cmp", [P, NT, E]), sb("f_ty", [P, NT])
        top, wgt = sb("f_top", [P, TOPK, NT, E]), sb("f_wgt", [P, TOPK, NT])
        ps_q, ps_h, ps_f, ps_x, ps_l = ps("f_psq", [HD, 512]), ps("f_psh", [P, 2, 512]), ps("f_psf", [P, 2, 512]), ps("f_psx", [P, 2, 512]), ps("f_psl", [P, 512])
        loaded, expo_set, consts_set, stored, dv = sem("f_ld"), sem("f_es"), sem("f_cs"), sem("f_st"), sem("f_dv")
        x1_loaded = [sem(f"f_xl{g}") for g in range(NG)]
        var_done, rstd_done = ([sem(f"f_{n}{i}") for i in range(4)] for n in ("vd", "rd"))
        normed, turns, rounded, reduced, cosines = sem("f_nm"), sem("f_tu"), sem("f_ro"), sem("f_re"), sem("f_co")
        ffn_in, biased, q_angle, q_cosines, q_ready = sem("f_fi"), sem("f_bi"), sem("f_qa"), sem("f_qc"), sem("f_qr")
        qt_filled, qt_copied, h_filled, h_copied, f_filled, f_added = sem("f_qf"), sem("f_qt"), sem("f_hf"), sem("f_hc"), sem("f_ff"), sem("f_fa")
        x2_ready, x3_ready = sem("f_x2"), sem("f_x3")
        xt_filled, xt_copied, l_filled, exp_in, exp_done, plan_ready = sem("f_xf"), sem("f_xc"), sem("f_lf"), sem("f_ei"), sem("f_ed"), sem("f_mr")
        block = ctx.enter_context(nc.Block())
        G1, B1, FB, G2, B2 = 1, 2, 3, 4, 5
        SCHEDULE = [(g, step - 2 * g) for step in range(11 + 2 * (NG - 1)) for g in reversed(range(NG)) if 0 <= step - 2 * g <= 10]
        BANKS = GT * D // 512
        TB = GT // BANKS
        tiles = lambda g: slice(GT * g, GT * (g + 1))
        flat = lambda z, g: z[:, tiles(g), :].rearrange("p t d -> p (t d)")

        @block.sync
        def _(sp):
            for g in range(NG):
                sp.dma_start(x1[:, tiles(g), :], x1_scr[tiles(g)].rearrange("t p d -> p t d")).then_inc(x1_loaded[g], 16)
            for dst, src in ((row, rows), (w1_sb, w1), (b1_sb, b1), (w2_sb, w2), (wr_sb, wr), (rb_sb, rb), (id_sb, ident)):
                sp.dma_start(dst[:], src).then_inc(loaded, 16)
            for g in range(NG):
                sp.wait_ge(x2_ready, g + 1)
                sp.dma_start(x2_scr[tiles(g)].rearrange("t p d -> p t d"), x1[:, tiles(g), :]).then_inc(stored, 16)
                sp.wait_ge(x3_ready, g + 1)
                r0 = GT * P * g + (NBLK * BR if g >= NG // 2 else 0)
                sp.dma_start(rows_scr[r0:r0 + GT * P, :].rearrange("(t p) d -> p t d", p=P), a[:, tiles(g), :]).then_inc(stored, 16)
            sp.wait_ge(plan_ready, 1)
            sp.dma_start(top_scr, top[:]).then_inc(stored, 16)
            sp.dma_start(wgt_scr, wgt[:]).then_inc(stored, 16)
            sp.wait_ge(stored, 16 * (2 * NG + 2))

        @block.gpsimd
        def _(pool):
            def inverse_std(g, n):
                pool.wait_ge(var_done[n], g + 1)
                nc.gpsimd.tensor_tensor(out=rstd[:, tiles(g)], in0=vare[:, tiles(g)], in1=expo[:, tiles(g)], op=ALU.pow).then_inc(rstd_done[n], 1)

            nc.gpsimd.memset(expo[:], -0.5).then_inc(expo_set, 1)
            pool.wait_ge(expo_set, 1)
            for g, stage in SCHEDULE:
                if stage == 0:
                    inverse_std(g, 0)
                elif stage == 3:
                    inverse_std(g, 1)
                elif stage == 4:
                    pool.wait_ge(ffn_in, g + 1)
                    nc.gpsimd.tensor_tensor(out=t[:, tiles(g), :], in0=a[:, tiles(g), :],
                                            in1=row[:, FB, :].unsqueeze(1).to_broadcast([P, GT, D]), op=ALU.add).then_inc(biased, 1)
                elif stage == 8:
                    inverse_std(g, 2)
                elif stage == 9:
                    inverse_std(g, 3)

        @block.vector
        def _(dve):
            ch = Chain(dve, dv)

            def v(ins):
                ch(ins)
                ch.wait()

            def sums(g, n, src):
                for i in range(GT * g, GT * (g + 1)):
                    ch(nc.vector.bn_stats(out=stats[:, i, :], in_=src[:, i, :]))
                ch.wait()
                for i in range(GT * g, GT * (g + 1)):
                    ch(nc.vector.bn_aggr(out=mv[:, i, :], in_=stats[:, i, :]))
                ch.wait()
                nc.vector.tensor_scalar(vare[:, tiles(g)], mv[:, tiles(g), 1], EPS, None, ALU.add).then_inc(var_done[n], 1)

            def affine_norm(g, n, src, gamma, beta):
                for i in range(GT * g, GT * (g + 1)):
                    ch(nc.vector.scalar_tensor_tensor(out=a[:, i, :], in0=src[:, i, :], scalar=mv[:, i, 0:1], in1=row[:, gamma, :],
                                                      op0=ALU.subtract, op1=ALU.mult))
                ch.wait()
                dve.wait_ge(rstd_done[n], g + 1)
                for i in range(GT * g, GT * (g + 1)):
                    ch(nc.vector.scalar_tensor_tensor(out=a[:, i, :], in0=a[:, i, :], scalar=rstd[:, i:i + 1], in1=row[:, beta, :],
                                                      op0=ALU.mult, op1=ALU.add))
                ch.wait()

            def normalise(g, n, src):
                dve.wait_ge(rstd_done[n], g + 1)
                for i in range(GT * g, GT * (g + 1)):
                    last = nc.vector.tensor_scalar(a[:, i, :], src[:, i, :], mv[:, i, 0:1], rstd[:, i:i + 1], ALU.subtract, ALU.mult)
                return last

            def cumprod(z):
                for j in range(1, HD):
                    v(nc.vector.tensor_tensor(z[:, :, j], z[:, :, j], z[:, :, j - 1], ALU.mult))

            v(nc.vector.memset(half_pi[:], float(np.pi / 2)))
            v(nc.vector.memset(qT[:], 0.0))
            nc.vector.memset(less_round[:], -ROUND).then_inc(consts_set, 1)
            for g, stage in SCHEDULE:
                f = lambda z: flat(z, g)
                if stage == 0:
                    dve.wait_ge(x1_loaded[g], 16)
                    sums(g, 0, x1)
                elif stage == 1:
                    normalise(g, 0, x1).then_inc(normed, 1)
                    dve.wait_ge(normed, g + 1)
                    nc.vector.tensor_scalar(f(t), f(a), 1.0 / (2.0 * np.pi), ROUND, ALU.mult, ALU.add).then_inc(turns, 1)
                elif stage == 2:
                    dve.wait_ge(rounded, g + 1)
                    v(nc.vector.scalar_tensor_tensor(out=f(c), in0=f(t), scalar=-TWO_PI_PARTS[0], in1=f(a), op0=ALU.mult, op1=ALU.add))
                    nc.vector.scalar_tensor_tensor(out=f(c), in0=f(t), scalar=-TWO_PI_PARTS[1], in1=f(c), op0=ALU.mult, op1=ALU.add).then_inc(reduced, 1)
                elif stage == 3:
                    dve.wait_ge(cosines, 2 * g + 2)
                    cumprod(c[:, tiles(g), :].rearrange("p t (h d) -> p (t h) d", d=HD))
                    v(nc.vector.tensor_tensor(f(t), f(a), f(c), ALU.add))
                    sums(g, 1, t)
                elif stage == 4:
                    dve.wait_ge(loaded, 16 * 7)
                    affine_norm(g, 1, t, G1, B1)
                    nc.vector.tensor_copy(qx[:, tiles(g), :], a[:, tiles(g), 0:HD]).then_inc(ffn_in, 1)
                    dve.wait_ge(ffn_in, g + 1)
                    v(nc.vector.tensor_scalar(f(qn), f(qx), 1.0 / (2.0 * np.pi), ROUND, ALU.mult, ALU.add))
                    v(nc.vector.tensor_scalar(f(qn), f(qn), ROUND, None, ALU.subtract))
                    v(nc.vector.scalar_tensor_tensor(out=f(qs), in0=f(qn), scalar=-TWO_PI_PARTS[0], in1=f(qx), op0=ALU.mult, op1=ALU.add))
                    v(nc.vector.scalar_tensor_tensor(out=f(qs), in0=f(qn), scalar=-TWO_PI_PARTS[1], in1=f(qs), op0=ALU.mult, op1=ALU.add))
                    nc.vector.scalar_tensor_tensor(out=f(qs), in0=f(qs), scalar=-1.0, in1=f(qs), op0=ALU.mult, op1=ALU.max).then_inc(q_angle, 1)
                elif stage == 5:
                    dve.wait_ge(q_cosines, g + 1)
                    cumprod(qs[:, tiles(g), :])
                    nc.vector.tensor_copy(qt[:, tiles(g), :], qs[:, tiles(g), :]).then_inc(q_ready, 1)
                elif stage == 8:
                    dve.wait_ge(biased, g + 1)
                    for i in range(BANKS):
                        n = GT * g + TB * i
                        dve.wait_ge(f_filled, BANKS * g + i + 1)
                        nc.vector.tensor_tensor(c[:, n:n + TB, :], ps_f[:, i, :].rearrange("p (t d) -> p t d", d=D), t[:, n:n + TB, :],
                                                ALU.add).then_inc(f_added, 1)
                    dve.wait_ge(f_added, BANKS * (g + 1))
                    sums(g, 2, c)
                elif stage == 9:
                    affine_norm(g, 2, c, G2, B2)
                    nc.vector.tensor_tensor(f(x1), f(x1), f(a), ALU.add).then_inc(x2_ready, 1)
                    dve.wait_ge(x2_ready, g + 1)
                    sums(g, 3, x1)
                elif stage == 10:
                    normalise(g, 3, x1).then_inc(x3_ready, 1)
            dve.wait_ge(l_filled, NG)
            bt = lambda z, n=E: z.unsqueeze(2).to_broadcast([P, NT, n])
            v(nc.vector.tensor_tensor(lg[:], ps_l[:, 0:NT * E].rearrange("p (t e) -> p t e", e=E), rb_sb[:].unsqueeze(1).to_broadcast([P, NT, E]), ALU.add))
            v(nc.vector.tensor_reduce(tiny[:], lg[:], AX.X, ALU.max))
            nc.vector.tensor_tensor(lg[:], lg[:], bt(tiny[:]), ALU.subtract).then_inc(exp_in, 1)
            dve.wait_ge(exp_done, 1)
            v(nc.vector.tensor_reduce(tiny[:], pr[:], AX.X, ALU.add))
            v(nc.vector.reciprocal(tiny[:], tiny[:]))
            v(nc.vector.tensor_tensor(pr[:], pr[:], bt(tiny[:]), ALU.mult))
            for e in range(E):
                if e < E - 1:
                    ch(nc.vector.tensor_tensor(cmp[:, :, e + 1:], pr[:, :, e + 1:], bt(pr[:, :, e], E - 1 - e), ALU.is_gt))
                if e > 0:
                    ch(nc.vector.tensor_tensor(cmp[:, :, 0:e], pr[:, :, 0:e], bt(pr[:, :, e], e), ALU.is_ge))
                v(nc.vector.memset(cmp[:, :, e:e + 1], 0.0))
                v(nc.vector.tensor_reduce(rank[:, :, e], cmp[:], AX.X, ALU.add))
            v(nc.vector.tensor_scalar(top[:, 0], rank[:], 0.5, None, ALU.is_lt))
            v(nc.vector.tensor_scalar(rank[:], rank[:], 1.5, None, ALU.is_lt))
            v(nc.vector.tensor_tensor(top[:, 1], rank[:], top[:, 0], ALU.subtract))
            for k in range(TOPK):
                v(nc.vector.tensor_tensor(cmp[:], pr[:], top[:, k], ALU.mult))
                v(nc.vector.tensor_reduce(wgt[:, k], cmp[:], AX.X, ALU.add))
            v(nc.vector.tensor_tensor(tiny[:], wgt[:, 0], wgt[:, 1], ALU.add))
            v(nc.vector.reciprocal(tiny[:], tiny[:]))
            nc.vector.tensor_tensor(wgt[:], wgt[:], tiny[:].unsqueeze(1).to_broadcast([P, TOPK, NT]), ALU.mult).then_inc(plan_ready, 1)

        @block.scalar
        def _(act):
            act.wait_ge(consts_set, 1)
            for g, stage in SCHEDULE:
                f = lambda z: flat(z, g)
                if stage == 1:
                    act.wait_ge(turns, g + 1)
                    nc.scalar.activation(f(t), f(t), ACT.Identity, bias=less_round[:, 0:1]).then_inc(rounded, 1)
                elif stage == 2:
                    act.wait_ge(reduced, g + 1)
                    nc.scalar.activation(f(c), f(c), ACT.Abs).then_inc(cosines, 1)
                    act.wait_ge(cosines, 2 * g + 1)
                    nc.scalar.activation(f(c), f(c), ACT.Sin, bias=half_pi[:, 0:1], scale=-1.0).then_inc(cosines, 1)
                elif stage == 4:
                    act.wait_ge(q_angle, g + 1)
                    nc.scalar.activation(f(qs), f(qs), ACT.Sin, bias=half_pi[:, 0:1], scale=-1.0).then_inc(q_cosines, 1)
                elif stage == 6:
                    act.wait_ge(qt_filled, g + 1)
                    nc.scalar.copy(qT[0:HD, :], ps_q[:]).then_inc(qt_copied, 1)
                    if g > 0:
                        act.wait_ge(f_filled, BANKS * g)
                    for j in range(FC):
                        i = g * FC + j
                        act.wait_ge(h_filled, i + 1)
                        nc.scalar.activation(hT[:, j, :], ps_h[:, i % 2, :], ACT.Relu, bias=b1_sb[:, j:j + 1]).then_inc(h_copied, 1)
                elif stage == 10:
                    for i in range(BANKS):
                        act.wait_ge(xt_filled, BANKS * g + i + 1)
                        nc.scalar.copy(xT[:, TB * i:TB * (i + 1)].rearrange("p t k d -> p (t k d)"), ps_x[:, i, :]).then_inc(xt_copied, 1)
            act.wait_ge(exp_in, 1)
            nc.scalar.activation(pr[:], lg[:], ACT.Exp).then_inc(exp_done, 1)

        @block.tensor
        def _(pe):
            pe.wait_ge(loaded, 16 * 7)
            for g, stage in SCHEDULE:
                if stage == 6:
                    pe.wait_ge(q_ready, g + 1)
                    for j in range(GT):
                        mm = nc.tensor.transpose(ps_q[:, j * P:(j + 1) * P], qt[:, g * GT + j, :], id_sb[:])
                    mm.then_inc(qt_filled, 1)
                    pe.wait_ge(qt_copied, g + 1)
                    for j in range(FC):
                        i = g * FC + j
                        if i >= 2:
                            pe.wait_ge(h_copied, i - 1)
                        nc.tensor.matmul(ps_h[:, i % 2, :], w1_sb[:, j * P:(j + 1) * P], qT[:], start=True, stop=True).then_inc(h_filled, 1)
                    pe.wait_ge(h_copied, FC * (g + 1))
                    for i in range(BANKS):
                        if g > 0:
                            pe.wait_ge(f_added, BANKS * (g - 1) + i + 1)
                        for j in range(TB):
                            n = TB * i + j
                            for m in range(FC):
                                mm = nc.tensor.matmul(ps_f[:, i, j * D:(j + 1) * D], hT[:, m, n * P:(n + 1) * P], w2_sb[:, m, :],
                                                      start=(m == 0), stop=(m == FC - 1))
                        mm.then_inc(f_filled, 1)
                elif stage == 10:
                    pe.wait_ge(x3_ready, g + 1)
                    for i in range(BANKS):
                        if g > 0:
                            pe.wait_ge(xt_copied, BANKS * (g - 1) + i + 1)
                        for j in range(TB):
                            for k in range(NC):
                                mm = nc.tensor.transpose(ps_x[:, i, (NC * j + k) * P:(NC * j + k + 1) * P],
                                                         a[:, GT * g + TB * i + j, k * P:(k + 1) * P], id_sb[:])
                        mm.then_inc(xt_filled, 1)
                    pe.wait_ge(xt_copied, BANKS * (g + 1))
                    for j in range(GT):
                        i = GT * g + j
                        for k in range(NC):
                            mm = nc.tensor.matmul(ps_l[:, i * E:(i + 1) * E], xT[:, j, k, :], wr_sb[:, k, :], start=(k == 0), stop=(k == NC - 1))
                    mm.then_inc(l_filled, 1)


def experts(nc, x2_scr, rows_scr, top_scr, wgt_scr, ys_scr, wgu, wd, ident, tri, blocks, out):
    with ExitStack() as ctx:
        sb = lambda n, s, d=F32: ctx.enter_context(nc.sbuf_tensor(n, s, d))
        ps = lambda n, s: ctx.enter_context(nc.psum_tensor(n, s, F32))
        sem = lambda n: ctx.enter_context(nc.semaphore(n))
        I32 = mybir.dt.int32
        x3, acc, id_sb = sb("e_x3", [P, NT, D]), sb("e_acc", [P, NT, D]), sb("e_id", [P, P])
        YG = NT // TOPK
        fetched = x3[:].rearrange("p (t k) d -> p t k d", k=TOPK)
        gu_raw, d_raw = sb("e_gur", [P, 2, NC, 2 * EI]), sb("e_dr", [P, 2, EC, D])
        gu_hi, gu_lo = (sb(f"e_gu{n}", [P, 2, NC, 2 * EI], F32R) for n in ("h", "l"))
        d_hi, d_lo = (sb(f"e_d{n}", [P, 2, EC, D], F32R) for n in ("h", "l"))
        silu, h = sb("e_sg", [P, 2, BR]), sb("e_h", [P, 4, BR])
        h_hi, h_lo = (sb(f"e_h{n}", [P, 2, EC, BR], F32R) for n in ("h", "l"))
        xb = sb("e_xb", [P, 2, BJ, D])
        x_hi, x_lo = (sb(f"e_x{n}", [P, 2, NC, BR], F32R) for n in ("h", "l"))
        yb = sb("e_yb", [P, 2, BJ, D])
        tri_sb, one_sb, blk_sb = sb("e_tri", [P, P]), sb("e_one", [P, P]), sb("e_blk", [P, NBLK])
        top, wgt = sb("e_top", [P, TOPK, NT, E]), sb("e_wgt", [P, TOPK, NT])
        taken, count, place, mine = (sb(f"e_{n}", [P, NT, E]) for n in ("tk", "ct", "pl", "mi"))
        total, nblk, first_blk, last_blk = (sb(f"e_{n}", [P, E]) for n in ("tot", "nb", "fb", "lb"))
        past, idf, ids = sb("e_past", [P, NBLK, E]), sb("e_idf", [P, NBLK + 1]), sb("e_ids", [P, NBLK + 1], I32)
        posf, pos, ypos = sb("e_posf", [P, TOPK, NT]), sb("e_pos", [P, TOPK, NT], I32), sb("e_ypos", [P, TOPK, NT], I32)
        tick = sb("e_tick", [P, 1])
        ps_gu, ps_y, ps_x = ps("e_psg", [P, 4, 512]), ps("e_psy", [P, 2, 512]), ps("e_psx", [P, 2, 512])
        plan_loaded, x3_loaded, acc_loaded = sem("e_ld"), sem("e_xl"), sem("e_al")
        gu_loaded, d_loaded, rows_loaded = ([sem(f"e_{n}{s}") for s in range(2)] for n in ("gl", "dl", "rl"))
        dv, taken_ready, ranks_filled, plan_ready, scattered, ticked = (
            sem("e_dv"), sem("e_tr"), sem("e_rf"), sem("e_pr"), sem("e_sc"), sem("e_tk"))
        gu_hi_done, gu_split, d_hi_done, d_split = sem("e_gh"), sem("e_gs"), sem("e_dh"), sem("e_ds")
        x_filled, x_hi_done, x_split = sem("e_xf"), sem("e_xh"), sem("e_xs")
        gu_filled, silu_done, h_done, h_hi_done, h_split = sem("e_gf"), sem("e_sd"), sem("e_hd"), sem("e_hh"), sem("e_hs")
        y_filled, y_copied, y_added = sem("e_yf"), sem("e_yc"), sem("e_ya")
        y_stored = [sem(f"e_ys{s}") for s in range(2)]
        gathered, half_combined, combined, stored = [sem(f"e_ga{s}") for s in range(YG)], sem("e_hc"), sem("e_co"), sem("e_st")
        block = ctx.enter_context(nc.Block())
        REST = EI - (EC - 1) * P
        HALVES = (slice(0, 3 * 2 * P), slice(3 * 2 * P, 2 * EI))
        LAST = HEAD + NBLK - 1
        SETS = NBLK + 2

        def shared(b):
            return isinstance(b, int) and (b < HEAD or b > LAST)

        def set_of(b):
            if isinstance(b, int):
                return 0 if b < HEAD else min(b, LAST + 1) - HEAD + 1
            return b - HEAD + 1

        def slot_of(b, s):
            return s if not shared(b) else 1 if b < HEAD else 0

        @block.sync
        def _(sp):
            def load_rows(b, s):
                sp.dma_start(xb[:, s], rows_scr[bass.ds(b * BR, BR), :].rearrange("(j p) d -> p j d", p=P)).then_inc(rows_loaded[s], 16)

            def load_gu(e, s):
                sp.dma_start(gu_raw[:, s], wgu[bass.ds(e, 1)].rearrange("a p k i -> p (a k) i")).then_inc(gu_loaded[s], 16)

            def load_d(e, s):
                sp.dma_start(d_raw[:, s], wd[bass.ds(e, 1)].rearrange("a p k i -> p (a k) i")).then_inc(d_loaded[s], 16)

            def expert_of(b):
                return sp.value_load(ids[0:1, bass.ds(b - HEAD, 1)], min_val=0, max_val=E)

            for dst, src in ((top, top_scr), (tri_sb, tri), (blk_sb, blocks), (id_sb, ident)):
                sp.dma_start(dst[:], src).then_inc(plan_loaded, 16)
            load_rows(0, 0)
            load_gu(0, 1)
            load_d(0, 1)
            load_rows(1, 1)
            half = HEAD * BJ
            for t0, r0 in ((0, 0), (half, (LAST + 1) * BR)):
                sp.dma_start(x3[:, t0:t0 + half, :], rows_scr[r0:r0 + half * P, :].rearrange("(t p) d -> p t d", p=P)).then_inc(x3_loaded, 16)
            sp.dma_start(acc[:], x2_scr.rearrange("t p d -> p t d")).then_inc(acc_loaded, 16)
            sp.dma_start(wgt[:], wgt_scr).then_inc(acc_loaded, 16)
            sp.wait_ge(plan_ready, 1)
            e = expert_of(HEAD)
            load_gu(e, 0)
            load_d(e, 0)

            def body(it):
                for s in range(2):
                    b = 2 * it + s
                    if not (isinstance(b, int) and (b < HEAD - 1 or b >= LAST)):
                        w = set_of(b + 2)
                        e = expert_of(b + 2)
                        sp.wait_ge(gu_split, 2 * (w - 1))
                        load_gu(e, s)
                        sp.wait_ge(d_split, w - 1)
                        load_d(e, s)
                    if not (isinstance(b, int) and b + 2 >= NALL):
                        if isinstance(b, int) and b + 2 == HEAD:
                            sp.wait_ge(scattered, 16 * TOPK * NT)
                        sp.wait_ge(x_filled, b + 1)
                        load_rows(b + 2, s)
                    if not (isinstance(b, int) and shared(b - 1)):
                        sp.wait_ge(y_copied, b - HEAD)
                        sp.dma_start(ys_scr[bass.ds((b - 1 - HEAD) * BR, BR), :].rearrange("(j p) d -> p j d", p=P),
                                     yb[:, 1 - s]).then_inc(y_stored[1 - s], 16)

            for it in range(3):
                body(it)
            with sp.Fori(3, NALL // 2 - 3) as it:
                body(it)
            for it in range(NALL // 2 - 3, NALL // 2):
                body(it)
            for q in range(NG):
                sp.wait_ge(combined, GT * (q + 1))
                sp.wait_ge(y_added, GT * (q + 1) // BJ)
                sp.dma_start(out[GT * q:GT * (q + 1)].rearrange("t p d -> p t d"), acc[:, GT * q:GT * (q + 1), :]).then_inc(stored, 16)
            sp.wait_ge(stored, 16 * NG)

        @block.gpsimd
        def _(pool):
            def split_d(w, s, nth):
                pool.wait_ge(d_loaded[s], 16 * nth)
                if not (isinstance(w, int) and w < 2):
                    pool.wait_ge(y_filled, w + HEAD - 2)
                nc.gpsimd.tensor_tensor(out=tick[:], in0=tick[:], in1=tick[:], op=ALU.mult).then_inc(ticked, 1)
                nc.gpsimd.tensor_copy(d_hi[:, s], d_raw[:, s]).then_inc(d_hi_done, 1)
                pool.wait_ge(d_hi_done, w + 1)
                nc.gpsimd.tensor_tensor(out=d_lo[:, s], in0=d_raw[:, s], in1=d_hi[:, s].bitcast(F32), op=ALU.subtract).then_inc(d_split, 1)

            nc.gpsimd.memset(tick[:], 0.0).then_inc(ticked, 1)
            pool.wait_ge(ticked, 1)
            split_d(0, 1, 1)
            pool.wait_ge(plan_ready, 1)
            pool.wait_ge(x3_loaded, 32)
            for t in range(NT):
                for k in range(TOPK):
                    nc.gpsimd.indirect_dma_start(rows_scr, bass.IndirectOffsetOnAxis(pos[:, k, t:t + 1], 0), x3[:, t, :], None).then_inc(scattered, 16)
            split_d(1, 0, 1)
            with pool.Fori(1, SETS // 2) as i:
                split_d(2 * i, 1, i + 1)
                split_d(2 * i + 1, 0, i + 1)
            for s in range(2):
                pool.wait_ge(y_stored[s], 16 * (NBLK // 2))
            for t in range(NT):
                if t >= YG:
                    pool.wait_ge(combined, t - YG + 1)
                for k in range(TOPK):
                    nc.gpsimd.indirect_dma_start(fetched[:, t % YG, k, :], None, ys_scr, bass.IndirectOffsetOnAxis(ypos[:, k, t:t + 1], 0)).then_inc(gathered[t % YG], 16)

        @block.vector
        def _(dve):
            ch = Chain(dve, dv)

            def v(ins):
                ch(ins)
                ch.wait()

            def split_rows(b, s):
                dve.wait_ge(x_hi_done, b + 1)
                nc.vector.tensor_tensor(x_lo[:, s].rearrange("p k r -> p (k r)"), ps_x[:, s, :],
                                        x_hi[:, s].rearrange("p k r -> p (k r)").bitcast(F32), ALU.subtract).then_inc(x_split, 1)

            def split_gu(w, s, z):
                dve.wait_ge(gu_hi_done, 2 * w + z + 1)
                cols = HALVES[z]
                nc.vector.tensor_tensor(gu_lo[:, s, :, cols], gu_raw[:, s, :, cols], gu_hi[:, s, :, cols].bitcast(F32),
                                        ALU.subtract).then_inc(gu_split, 1)

            def gate(b, s, c):
                i = EC * b + c
                dve.wait_ge(silu_done, i + 1)
                if not (isinstance(i, int) and i < 4):
                    dve.wait_ge(h_split, i - 3)
                at = (EC * s + c) % 4
                bank = ps_gu[:, at, :]
                if c < EC - 1:
                    nc.vector.tensor_tensor(h[:, at, :], bank[:, BR:2 * BR], silu[:, c % 2, :], ALU.mult).then_inc(h_done, 1)
                else:
                    nc.vector.tensor_tensor(h[0:REST, at, :], bank[REST:2 * REST, 0:BR], silu[0:REST, c % 2, :], ALU.mult).then_inc(h_done, 1)

            def split_h(b, s, c):
                i = EC * b + c
                dve.wait_ge(h_hi_done, i + 1)
                r = slice(0, P if c < EC - 1 else REST)
                nc.vector.tensor_tensor(h_lo[r, s, c, :], h[r, (EC * s + c) % 4, :], h_hi[r, s, c, :].bitcast(F32), ALU.subtract).then_inc(h_split, 1)

            def combine(t):
                dve.wait_ge(gathered[t % YG], 16 * TOPK * (t // YG + 1))
                for k in range(TOPK):
                    ins = nc.vector.scalar_tensor_tensor(out=acc[:, t, :], in0=fetched[:, t % YG, k, :], scalar=wgt[:, k, t:t + 1],
                                                         in1=acc[:, t, :], op0=ALU.mult, op1=ALU.add)
                    if k == 0:
                        ins.then_inc(half_combined, 1)
                        dve.wait_ge(half_combined, t + 1)
                ins.then_inc(combined, 1)

            v(nc.vector.memset(one_sb[:], 1.0))
            dve.wait_ge(plan_loaded, 16 * 4)
            nc.vector.tensor_tensor(taken[:], top[:, 0], top[:, 1], ALU.add).then_inc(taken_ready, 1)
            dve.wait_ge(ranks_filled, 1)
            r = NT * E
            v(nc.vector.tensor_copy(count[:].rearrange("p t e -> p (t e)"), ps_y[:, 1, 0:r]))
            v(nc.vector.tensor_reduce(total[:], count[:].rearrange("p t e -> p e t"), AX.X, ALU.add))
            v(nc.vector.tensor_scalar(nblk[:], total[:], 1.0 / BR, (BR - 1.0) / BR - 0.5 + 0.5 / BR, ALU.mult, ALU.add))
            v(nc.vector.tensor_scalar(nblk[:], nblk[:], ROUND, None, ALU.add))
            v(nc.vector.tensor_scalar(nblk[:], nblk[:], ROUND, None, ALU.subtract))
            v(nc.vector.memset(first_blk[:, 0:1], 0.0))
            for e in range(1, E):
                v(nc.vector.tensor_tensor(first_blk[:, e:e + 1], first_blk[:, e - 1:e], nblk[:, e - 1:e], ALU.add))
            v(nc.vector.tensor_tensor(last_blk[:], first_blk[:], nblk[:], ALU.add))
            v(nc.vector.tensor_tensor(past[:], last_blk[:].unsqueeze(1).to_broadcast([P, NBLK, E]),
                                      blk_sb[:].unsqueeze(2).to_broadcast([P, NBLK, E]), ALU.is_le))
            v(nc.vector.tensor_reduce(idf[:, 0:NBLK], past[:], AX.X, ALU.add))
            v(nc.vector.tensor_scalar(idf[:, 0:NBLK], idf[:, 0:NBLK], E - 1.0, 1.0, ALU.min, ALU.add))
            v(nc.vector.memset(idf[:, NBLK:NBLK + 1], 0.0))
            v(nc.vector.tensor_copy(ids[:], idf[:]))
            ch(nc.vector.tensor_copy(place[:, 1:, :], count[:, 0:NT - 1, :]))
            v(nc.vector.tensor_scalar(place[:, 0, :], first_blk[:], float(BR), None, ALU.mult))
            here, there, d = place, mine, 1
            while d < NT:
                ch(nc.vector.tensor_copy(there[:, 0:d, :], here[:, 0:d, :]))
                v(nc.vector.tensor_tensor(there[:, d:, :], here[:, d:, :], here[:, 0:NT - d, :], ALU.add))
                here, there, d = there, here, 2 * d
            assert here is place
            v(nc.vector.tensor_tensor(place[:].rearrange("p t e -> p (t e)"), place[:].rearrange("p t e -> p (t e)"), ps_y[:, 0, 0:r], ALU.add))
            for k in range(TOPK):
                v(nc.vector.tensor_tensor(mine[:], place[:], top[:, k], ALU.mult))
                v(nc.vector.tensor_reduce(posf[:, k], mine[:], AX.X, ALU.add))
            v(nc.vector.tensor_copy(ypos[:], posf[:]))
            v(nc.vector.tensor_scalar(posf[:], posf[:], float(HEAD * BR), None, ALU.add))
            nc.vector.tensor_copy(pos[:], posf[:]).then_inc(plan_ready, 1)

            split_rows(0, 0)
            for z in range(2):
                split_gu(0, 1, z)
            gate(0, 0, 0)

            def body(it):
                for s in range(2):
                    b = 2 * it + s
                    more = not (isinstance(b, int) and b == NALL - 1)
                    new_set = not isinstance(b, int) or (b + 2 < NALL and set_of(b + 2) != set_of(b + 1))
                    gate(b, s, 1)
                    split_h(b, s, 0)
                    gate(b, s, 2)
                    split_h(b, s, 1)
                    if more:
                        split_rows(b + 1, 1 - s)
                    gate(b, s, 3)
                    split_h(b, s, 2)
                    gate(b, s, 4)
                    split_h(b, s, 3)
                    gate(b, s, 5)
                    split_h(b, s, 4)
                    split_h(b, s, 5)
                    if more:
                        gate(b + 1, 1 - s, 0)
                    if new_set:
                        for z in range(2):
                            split_gu(set_of(b + 2), s, z)
                    if shared(b):
                        n = b if b < HEAD else b - NBLK
                        if b == 0:
                            dve.wait_ge(acc_loaded, 32)
                        if b in COMBINED_IN:
                            dve.wait_ge(y_added, n)
                            for t in COMBINED_IN[b]:
                                combine(t)
                            dve.wait_ge(combined, COMBINED_IN[b][-1] + 1)
                        dve.wait_ge(y_filled, b + 1)
                        nc.vector.tensor_tensor(acc[:, BJ * n:BJ * (n + 1), :].rearrange("p j d -> p (j d)"), ps_y[:, s, :],
                                                acc[:, BJ * n:BJ * (n + 1), :].rearrange("p j d -> p (j d)"), ALU.add).then_inc(y_added, 1)

            body(0)
            body(1)
            with dve.Fori(2, NALL // 2 - 3) as it:
                body(it)
            body(NALL // 2 - 3)
            body(NALL // 2 - 2)
            body(NALL // 2 - 1)

        @block.scalar
        def _(act):
            def split_rows(b, s):
                act.wait_ge(x_filled, b + 1)
                nc.scalar.copy(x_hi[:, s].rearrange("p k r -> p (k r)"), ps_x[:, s, :]).then_inc(x_hi_done, 1)

            def split_gu(w, s, z, nth):
                if z == 0:
                    act.wait_ge(gu_loaded[s], 16 * nth)
                cols = HALVES[z]
                nc.scalar.copy(gu_hi[:, s, :, cols], gu_raw[:, s, :, cols]).then_inc(gu_hi_done, 1)

            def gate(b, s, c):
                i = EC * b + c
                act.wait_ge(gu_filled, i + 1)
                if not (isinstance(i, int) and i < 2):
                    act.wait_ge(h_done, i - 1)
                r = slice(0, P if c < EC - 1 else REST)
                nc.scalar.activation(silu[r, c % 2, :], ps_gu[r, (EC * s + c) % 4, 0:BR], ACT.Silu).then_inc(silu_done, 1)

            def split_h(b, s, c):
                i = EC * b + c
                act.wait_ge(h_done, i + 1)
                if c == 0 and not (isinstance(b, int) and b < 2):
                    act.wait_ge(y_filled, b - 1)
                r = slice(0, P if c < EC - 1 else REST)
                nc.scalar.copy(h_hi[r, s, c, :], h[r, (EC * s + c) % 4, :]).then_inc(h_hi_done, 1)

            split_rows(0, 0)
            for z in range(2):
                split_gu(0, 1, z, 1)
            gate(0, 0, 0)

            def body(it):
                for s in range(2):
                    b = 2 * it + s
                    more = not (isinstance(b, int) and b == NALL - 1)
                    new_set = not isinstance(b, int) or (b + 2 < NALL and set_of(b + 2) != set_of(b + 1))
                    gate(b, s, 1)
                    split_h(b, s, 0)
                    gate(b, s, 2)
                    split_h(b, s, 1)
                    if more:
                        split_rows(b + 1, 1 - s)
                    gate(b, s, 3)
                    split_h(b, s, 2)
                    gate(b, s, 4)
                    split_h(b, s, 3)
                    gate(b, s, 5)
                    split_h(b, s, 4)
                    split_h(b, s, 5)
                    if more:
                        gate(b + 1, 1 - s, 0)
                    if new_set:
                        for z in range(2):
                            split_gu(set_of(b + 2), s, z, it + s)
                    if not shared(b):
                        act.wait_ge(y_filled, b + 1)
                        if not (isinstance(b, int) and b < HEAD + 2):
                            act.wait_ge(y_stored[s], 16 * (it - HEAD // 2))
                        nc.scalar.copy(yb[:, s].rearrange("p j d -> p (j d)"), ps_y[:, s, :]).then_inc(y_copied, 1)

            body(0)
            body(1)
            body(2)
            with act.Fori(3, NALL // 2 - 3) as it:
                body(it)
            body(NALL // 2 - 3)
            body(NALL // 2 - 2)
            body(NALL // 2 - 1)

        @block.tensor
        def _(pe):
            def three(out, a, b, start, stop):
                nc.tensor.matmul(out, a[0], b[0], start=start, stop=False)
                nc.tensor.matmul(out, a[0], b[1], start=False, stop=False)
                return nc.tensor.matmul(out, a[1], b[0], start=False, stop=stop)

            def turn_rows(b, s, nth):
                pe.wait_ge(rows_loaded[s], 16 * nth)
                if not (isinstance(b, int) and b < 2):
                    pe.wait_ge(x_split, b - 1)
                for k in range(NC):
                    for j in range(BJ):
                        mm = nc.tensor.transpose(ps_x[:, s, k * BR + j * P:k * BR + (j + 1) * P], xb[:, s, j, k * P:(k + 1) * P], id_sb[:])
                mm.then_inc(x_filled, 1)

            def gate_up(b, s, c):
                i = EC * b + c
                if not (isinstance(i, int) and i < 4):
                    pe.wait_ge(h_done, i - 3)
                bank, w = ps_gu[:, (EC * s + c) % 4, :], slot_of(b, s)
                for half in range(2 if c < EC - 1 else 1):
                    cols = slice((2 * c + half) * P, (2 * c + half + 1) * P)
                    for k in range(NC):
                        mm = three(bank[:, half * BR:(half + 1) * BR], [z[:, w, k, cols] for z in (gu_hi, gu_lo)],
                                   [z[:, s, k, :] for z in (x_hi, x_lo)], k == 0, k == NC - 1)
                mm.then_inc(gu_filled, 1)

            def start_block(b, s):
                pe.wait_ge(gu_split, 2 * set_of(b) + 2)
                pe.wait_ge(x_split, b + 1)
                gate_up(b, s, 0)

            def down(b, s):
                pe.wait_ge(d_split, set_of(b) + 1)
                if isinstance(b, int) and b < 2:
                    pe.wait_ge(plan_ready, 1)
                elif shared(b - 2):
                    pe.wait_ge(y_added, b - 1 if b - 2 < HEAD else b - 1 - NBLK)
                else:
                    pe.wait_ge(y_copied, b - 1 - HEAD)
                w = slot_of(b, s)
                pe.wait_ge(h_split, EC * (b + 1) - 1)
                for j in range(BJ):
                    for c in range(EC):
                        if j == 0 and c == EC - 1:
                            pe.wait_ge(h_split, EC * (b + 1))
                        r = slice(0, P if c < EC - 1 else REST)
                        mm = three(ps_y[:, s, j * D:(j + 1) * D], [z[r, s, c, j * P:(j + 1) * P] for z in (h_hi, h_lo)],
                                   [z[r, w, c, :] for z in (d_hi, d_lo)], c == 0, c == EC - 1)
                mm.then_inc(y_filled, 1)

            def body(it):
                for s in range(2):
                    b = 2 * it + s
                    more = not (isinstance(b, int) and b == NALL - 1)
                    gate_up(b, s, 1)
                    gate_up(b, s, 2)
                    if more:
                        turn_rows(b + 1, 1 - s, it + 1 + s)
                    for c in range(3, EC):
                        gate_up(b, s, c)
                    if more:
                        start_block(b + 1, 1 - s)
                    down(b, s)

            pe.wait_ge(plan_loaded, 16 * 4)
            pe.wait_ge(taken_ready, 1)
            flat = taken[:].rearrange("p t e -> p (t e)")
            nc.tensor.matmul(ps_y[:, 0, 0:NT * E], tri_sb[:], flat, start=True, stop=True)
            nc.tensor.matmul(ps_y[:, 1, 0:NT * E], one_sb[:], flat, start=True, stop=True).then_inc(ranks_filled, 1)
            turn_rows(0, 0, 1)
            start_block(0, 0)
            for it in range(3):
                body(it)
            with pe.Fori(3, NALL // 2 - 2) as it:
                body(it)
            body(NALL // 2 - 2)
            body(NALL // 2 - 1)


def build(nc, ins, out):
    def scratch(name, shape):
        return nc.dram_tensor(name, shape, F32, kind="Internal").ap()

    q_scr = scratch("q_scr", [2, D, TOK])
    x1_scr, x2_scr = (scratch(n, [NT, P, D]) for n in ("x1_scr", "x2_scr"))
    top_scr, wgt_scr = scratch("top_scr", [P, TOPK, NT, E]), scratch("wgt_scr", [P, TOPK, NT])
    rows_scr, ys_scr = scratch("rows_scr", [NALL * BR, D]), scratch("ys_scr", [NBLK * BR, D])
    project_queries(nc, ins["x"], ins["wq"], ins["bq"], ins["ident"], q_scr)
    cross_attention(nc, ins["ctxT"], ins["x"], q_scr, ins["wk"], ins["bk"], ins["wv"], ins["bv"], ins["wp"],
                    ins["rows"], ins["ident"], ins["sel4"], ins["hmask"], x1_scr, rows_scr)
    circuit_ffn(nc, x1_scr, ins["rows"], ins["w1"], ins["b1"], ins["w2"], ins["wr"], ins["rb"], ins["ident"],
                x2_scr, rows_scr, top_scr, wgt_scr)
    experts(nc, x2_scr, rows_scr, top_scr, wgt_scr, ys_scr, ins["wgu"], ins["wd"], ins["ident"],
            ins["tri"], ins["blocks"], out)


def kernel(**inputs):
    import concourse.bacc as bacc
    from concourse.bass_utils import run_bass_kernel_spmd as run

    a = {k: np.asarray(v) for k, v in inputs.items()}
    chunked = lambda m: np.ascontiguousarray(m.reshape(m.shape[0] // P, P, -1).transpose(1, 0, 2))
    wide = lambda r: np.broadcast_to(r, (P,) + r.shape)
    ctx = a["ctx_1024"]
    ctx = np.concatenate([ctx, np.repeat(ctx[:, -1:], SKP - SK, axis=1)], axis=1)
    heads = lambda v: v.reshape(PAIRS, 2, HD, *v.shape[1:]).swapaxes(0, 1).reshape(2, P, *v.shape[1:])
    pad = EC * P - EI

    def gate_up(g, u):
        cut = EI - EI % P
        g, u = (np.concatenate([s[None], r]).transpose(0, 2, 1) for s, r in (g, u))
        whole = np.stack([z[:, :, :cut].reshape(NEXP, D, -1, P) for z in (g, u)], axis=3).reshape(NEXP, D, -1)
        w = np.concatenate([whole, g[:, :, cut:], u[:, :, cut:]], axis=2)
        return w.reshape(NEXP, NC, P, 2 * EI).transpose(0, 2, 1, 3)

    wd = np.concatenate([a["L0_ffn_sd"][None], a["L0_ffn_rd"]]).transpose(0, 2, 1)
    wd = np.pad(wd, ((0, 0), (0, pad), (0, 0))).reshape(NEXP, EC, P, D).transpose(0, 2, 1, 3)
    data = {
        "x": a["x"].reshape(NT, P, D),
        "ctxT": ctx.transpose(0, 2, 1).reshape(B, NC, P, SKP).transpose(0, 2, 1, 3),
        "wq": chunked(a["L0_xattn_Wq"].T), "bq": a["L0_xattn_bq"].reshape(NC, P).T,
        "wk": chunked(a["L0_xattn_Wk"].T), "bk": a["L0_xattn_bk"].reshape(NC, P).T,
        "wv": chunked(a["L0_xattn_Wv"].T), "bv": heads(a["L0_xattn_bv"]).T,
        "wp": heads(np.ascontiguousarray(a["L0_xattn_Wp"].T)).transpose(1, 0, 2),
        "rows": wide(np.stack([a["L0_xattn_bp"], a["L0_attn_gamma1"], a["L0_attn_beta1"], a["L0_attn_b2"],
                               a["L0_attn_gamma2"], a["L0_attn_beta2"]])),
        "w1": np.pad(a["L0_attn_w1"].T, ((0, P - HD), (0, 0))), "b1": a["L0_attn_b1"].reshape(FC, P).T, "w2": chunked(a["L0_attn_w2"].T),
        "wr": chunked(a["L0_ffn_wr"].T), "rb": wide(a["L0_ffn_rb"]),
        "wgu": gate_up((a["L0_ffn_sg"], a["L0_ffn_rg"]), (a["L0_ffn_su"], a["L0_ffn_ru"])), "wd": wd,
        "tri": np.triu(np.ones((P, P), np.float32), 1),
        "blocks": wide(np.arange(NBLK, dtype=np.float32)),
        "ident": np.eye(P, dtype=np.float32),
        "sel4": np.tile(np.eye(32, dtype=np.float32), (4, 1)),
        "hmask": np.tile(np.repeat(np.eye(2, dtype=np.float32), HD, axis=0), (3, 1)),
    }
    nc = bacc.Bacc("TRN2", target_bir_lowering=False, num_devices=1)
    ins = {}
    for name in data:
        data[name] = np.ascontiguousarray(data[name])
        ins[name] = nc.dram_tensor("in_" + name, data[name].shape, mybir.dt.from_np(data[name].dtype), kind="ExternalInput").ap()
    out = nc.dram_tensor("out", (NT, P, D), F32, kind="ExternalOutput").ap()
    build(nc, ins, out)
    r = run(nc, [{"in_" + k: v for k, v in data.items()}], core_ids=[0])
    return r.results[0]["out"].reshape(B, SQ, D)
```
